# Optimizing a Trainium2 kernel written in Bass

```python
import numpy as np
import jax
import jax.numpy as jnp

def _softmax(x, axis=-1):
    return jax.nn.softmax(x, axis=axis)

def _gelu(x):
    return jax.nn.gelu(x, approximate=True)

def _silu(x):
    return jax.nn.silu(x)

def _sigmoid(x):
    return jax.nn.sigmoid(x)

def _layernorm(x, axis=-1, eps=1e-05):
    m = jnp.mean(x, axis=axis, keepdims=True)
    v = jnp.var(x, axis=axis, keepdims=True)
    return (x - m) / jnp.sqrt(v + eps)

def _scatter_add(tgt, idx, src, axis=0):
    return tgt.at[idx].add(src)

def _segment_sum(src, seg, n):
    return jax.ops.segment_sum(src, seg, n)
kernel_name = 'mk_metaformer_d1_conv_nchw256_r2_97c587'

def setup_inputs(seed: int=0):
    np.random.seed(seed)
    _w = jnp.asarray

    def _rec_inputs():
        import jax
        import jax.numpy as jnp
        _gk = jax.random.key(seed)
        x = -0.0005207 + 1.001 * jax.random.normal(jax.random.fold_in(_gk, 1), (8, 128, 32, 32), jnp.float32)
        return x
    x = _rec_inputs()

    def _L0_conv_setup():
        import jax, jax.numpy as jnp
        import numpy as np
        B, C, H, W = (8, 128, 32, 32)
        HEADS, DH = (8, 32)
        INNER = HEADS * DH
        SCALE = DH ** (-0.5)

        def conv2d(x, w, stride=1, pad=0):
            return jax.lax.conv_general_dilated(x, w, (stride, stride), [(pad, pad), (pad, pad)], dimension_numbers=('NCHW', 'OIHW', 'NCHW'))

        def fixed_pos_emb(h, w):
            half = C // 2
            inv_freq = 1.0 / 10000.0 ** (jnp.arange(0, half, 2, dtype=jnp.float32) / half)
            hs = jnp.linspace(-1.0, 1.0, h)
            ws = jnp.linspace(-1.0, 1.0, w)
            sinu_h = hs[:, None] * inv_freq[None, :]
            sinu_w = ws[:, None] * inv_freq[None, :]
            part_w = jnp.broadcast_to(sinu_w.T[:, None, :], (C // 4, h, w))
            part_h = jnp.broadcast_to(sinu_h.T[:, :, None], (C // 4, h, w))
            sinu = jnp.concatenate([part_w, part_h], axis=0)
            return jnp.concatenate([jnp.sin(sinu), jnp.cos(sinu)], axis=0)[None]

        def rotate_every_two(t):
            t2 = t.reshape(*t.shape[:-1], -1, 2)
            x1, x2 = (t2[..., 0], t2[..., 1])
            return jnp.stack([-x2, x1], axis=-1).reshape(t.shape)

        def rotary_sin_cos(n):
            seq = jnp.linspace(-1.0, 1.0, n)[:, None]
            scales = jnp.logspace(0.0, np.log(5.0) / np.log(2.0), DH // 4, base=2.0).astype(jnp.float32)
            freqs = seq * scales[None, :] * jnp.pi
            xs = jnp.broadcast_to(freqs[:, None, :], (n, n, DH // 4))
            ys = jnp.broadcast_to(freqs[None, :, :], (n, n, DH // 4))
            sin = jnp.concatenate([jnp.sin(xs), jnp.sin(ys)], axis=-1).reshape(n * n, DH // 2)
            cos = jnp.concatenate([jnp.cos(xs), jnp.cos(ys)], axis=-1).reshape(n * n, DH // 2)
            sin = jnp.repeat(sin, 2, axis=-1)[None, None]
            cos = jnp.repeat(cos, 2, axis=-1)[None, None]
            return (sin, cos)

        def split_heads(t):
            return t.reshape(B, HEADS, DH, H * W).transpose(0, 1, 3, 2)
        key = jax.random.key(seed)
        ks = jax.random.split(key, 7)
        x = jax.random.normal(ks[0], (B, C, H, W), dtype=jnp.float32)
        wq = jax.random.normal(ks[1], (INNER, C, 1, 1), dtype=jnp.float32) * 0.05
        wk = jax.random.normal(ks[2], (INNER, C, 3, 3), dtype=jnp.float32) * 0.02
        wv = jax.random.normal(ks[3], (INNER, C, 3, 3), dtype=jnp.float32) * 0.02
        mix = jax.random.normal(ks[4], (HEADS, HEADS), dtype=jnp.float32)
        wo = jax.random.normal(ks[5], (2 * C, INNER, 1, 1), dtype=jnp.float32) * 0.05
        bo = jnp.zeros((2 * C,), dtype=jnp.float32)
        return {'x': x, 'wq': wq, 'wk': wk, 'wv': wv, 'mix': mix, 'wo': wo, 'bo': bo}
    _L0_conv_all = _L0_conv_setup()
    _L0_conv_in = {k: v for k, v in _L0_conv_all.items() if k in ('wq', 'wk', 'wv', 'mix', 'wo', 'bo')}
    del _L0_conv_all

    def _L0_ffn_setup():
        import jax, jax.numpy as jnp
        import numpy as np
        TOP_K = 2
        LN_EPS = 1e-05
        key = jax.random.key(seed)
        ks = jax.random.split(key, 8)
        B, S, D, E, H = (16, 512, 128, 8, 512)
        x = jax.random.normal(ks[0], (B, S, D), dtype=jnp.float32)
        Wr = jax.random.normal(ks[1], (D, E), dtype=jnp.float32) * 0.1
        br = jnp.zeros((E,), dtype=jnp.float32)
        ln_g = jnp.ones((E, D), dtype=jnp.float32)
        ln_b = jnp.zeros((E, D), dtype=jnp.float32)
        W1 = jax.random.normal(ks[2], (E, D, H), dtype=jnp.float32) * (1.0 / np.sqrt(D))
        b1 = jnp.zeros((E, H), dtype=jnp.float32)
        W2 = jax.random.normal(ks[3], (E, H, D), dtype=jnp.float32) * (1.0 / np.sqrt(H))
        b2 = jnp.zeros((E, D), dtype=jnp.float32)
        return {'x': x, 'Wr': Wr, 'br': br, 'ln_g': ln_g, 'ln_b': ln_b, 'W1': W1, 'b1': b1, 'W2': W2, 'b2': b2}
    _L0_ffn_all = _L0_ffn_setup()
    _L0_ffn_in = {k: v for k, v in _L0_ffn_all.items() if k in ('Wr', 'br', 'ln_g', 'ln_b', 'W1', 'b1', 'W2', 'b2')}
    del _L0_ffn_all
    return {'x': x, 'L0_conv_wq': _L0_conv_in['wq'], 'L0_conv_wk': _L0_conv_in['wk'], 'L0_conv_wv': _L0_conv_in['wv'], 'L0_conv_mix': _L0_conv_in['mix'], 'L0_conv_wo': _L0_conv_in['wo'], 'L0_conv_bo': _L0_conv_in['bo'], 'L0_ffn_Wr': _L0_ffn_in['Wr'], 'L0_ffn_br': _L0_ffn_in['br'], 'L0_ffn_ln_g': _L0_ffn_in['ln_g'], 'L0_ffn_ln_b': _L0_ffn_in['ln_b'], 'L0_ffn_W1': _L0_ffn_in['W1'], 'L0_ffn_b1': _L0_ffn_in['b1'], 'L0_ffn_W2': _L0_ffn_in['W2'], 'L0_ffn_b2': _L0_ffn_in['b2']}

def reference(x, L0_conv_wq, L0_conv_wk, L0_conv_wv, L0_conv_mix, L0_conv_wo, L0_conv_bo, L0_ffn_Wr, L0_ffn_br, L0_ffn_ln_g, L0_ffn_ln_b, L0_ffn_W1, L0_ffn_b1, L0_ffn_W2, L0_ffn_b2):
    import jax
    import jax.numpy as jnp

    def _L0_conv_ref(x, wq, wk, wv, mix, wo, bo):
        import jax, jax.numpy as jnp
        import numpy as np
        B, C, H, W = (8, 128, 32, 32)
        HEADS, DH = (8, 32)
        INNER = HEADS * DH
        SCALE = DH ** (-0.5)

        def conv2d(x, w, stride=1, pad=0):
            return jax.lax.conv_general_dilated(x, w, (stride, stride), [(pad, pad), (pad, pad)], dimension_numbers=('NCHW', 'OIHW', 'NCHW'))

        def fixed_pos_emb(h, w):
            half = C // 2
            inv_freq = 1.0 / 10000.0 ** (jnp.arange(0, half, 2, dtype=jnp.float32) / half)
            hs = jnp.linspace(-1.0, 1.0, h)
            ws = jnp.linspace(-1.0, 1.0, w)
            sinu_h = hs[:, None] * inv_freq[None, :]
            sinu_w = ws[:, None] * inv_freq[None, :]
            part_w = jnp.broadcast_to(sinu_w.T[:, None, :], (C // 4, h, w))
            part_h = jnp.broadcast_to(sinu_h.T[:, :, None], (C // 4, h, w))
            sinu = jnp.concatenate([part_w, part_h], axis=0)
            return jnp.concatenate([jnp.sin(sinu), jnp.cos(sinu)], axis=0)[None]

        def rotate_every_two(t):
            t2 = t.reshape(*t.shape[:-1], -1, 2)
            x1, x2 = (t2[..., 0], t2[..., 1])
            return jnp.stack([-x2, x1], axis=-1).reshape(t.shape)

        def rotary_sin_cos(n):
            seq = jnp.linspace(-1.0, 1.0, n)[:, None]
            scales = jnp.logspace(0.0, np.log(5.0) / np.log(2.0), DH // 4, base=2.0).astype(jnp.float32)
            freqs = seq * scales[None, :] * jnp.pi
            xs = jnp.broadcast_to(freqs[:, None, :], (n, n, DH // 4))
            ys = jnp.broadcast_to(freqs[None, :, :], (n, n, DH // 4))
            sin = jnp.concatenate([jnp.sin(xs), jnp.sin(ys)], axis=-1).reshape(n * n, DH // 2)
            cos = jnp.concatenate([jnp.cos(xs), jnp.cos(ys)], axis=-1).reshape(n * n, DH // 2)
            sin = jnp.repeat(sin, 2, axis=-1)[None, None]
            cos = jnp.repeat(cos, 2, axis=-1)[None, None]
            return (sin, cos)

        def split_heads(t):
            return t.reshape(B, HEADS, DH, H * W).transpose(0, 1, 3, 2)
        sinu = fixed_pos_emb(H, W)
        inp = x + 2.0 * sinu
        q = conv2d(inp, wq)
        k = conv2d(inp, wk, 1, 1)
        v = conv2d(inp, wv, 1, 1)
        q, k, v = (split_heads(q), split_heads(k), split_heads(v))
        sin, cos = rotary_sin_cos(H)
        q = q * cos + rotate_every_two(q) * sin
        k = k * cos + rotate_every_two(k) * sin
        dots = jnp.einsum('bhid,bhjd->bhij', q, k) * SCALE
        attn = jax.nn.softmax(dots, axis=-1)
        attn = jnp.einsum('bhij,hg->bgij', attn, mix)
        out = jnp.einsum('bhij,bhjd->bhid', attn, v)
        out = out.transpose(0, 1, 3, 2).reshape(B, INNER, H, W)
        o = conv2d(out, wo) + bo[None, :, None, None]
        a, g = jnp.split(o, 2, axis=1)
        return a * jax.nn.sigmoid(g)

    def _L0_ffn_ref(x, Wr, br, ln_g, ln_b, W1, b1, W2, b2):
        import jax, jax.numpy as jnp
        import numpy as np
        TOP_K = 2
        LN_EPS = 1e-05
        B, S, D = x.shape
        N = B * S
        xt = x.reshape(N, D)
        logits = xt @ Wr + br
        probs = jax.nn.softmax(logits, axis=-1)
        top_p, top_idx = jax.lax.top_k(probs, TOP_K)
        weights = top_p / top_p.sum(axis=-1, keepdims=True)
        mu = xt.mean(axis=-1, keepdims=True)
        var = ((xt - mu) ** 2).mean(axis=-1, keepdims=True)
        xn = (xt - mu) * jax.lax.rsqrt(var + LN_EPS)
        xe = xn[None, :, :] * ln_g[:, None, :] + ln_b[:, None, :]
        h = jax.nn.gelu(jnp.einsum('end,edh->enh', xe, W1) + b1[:, None, :], approximate=False)
        y = jnp.einsum('enh,ehd->end', h, W2) + b2[:, None, :]
        y_tok = jnp.transpose(y, (1, 0, 2))
        sel = jnp.take_along_axis(y_tok, top_idx[:, :, None], axis=1)
        out = (weights[:, :, None] * sel).sum(axis=1)
        return out.reshape(B, S, D)

    def _gn(v, G=32, eps=1e-05):
        B_, C_, H_, W_ = v.shape
        g = v.reshape(B_, G, C_ // G, H_, W_)
        m = jnp.mean(g, axis=(2, 3, 4), keepdims=True)
        s = jnp.var(g, axis=(2, 3, 4), keepdims=True)
        return ((g - m) / jnp.sqrt(s + eps)).reshape(v.shape)

    def _ln_c(v, eps=1e-06):
        m = jnp.mean(v, axis=1, keepdims=True)
        s = jnp.var(v, axis=1, keepdims=True)
        return (v - m) / jnp.sqrt(s + eps)

    def _ln_t(v, eps=1e-05):
        m = jnp.mean(v, axis=-1, keepdims=True)
        s = jnp.var(v, axis=-1, keepdims=True)
        return (v - m) / jnp.sqrt(s + eps)

    def _to_tokens(v):
        B_, C_, H_, W_ = v.shape
        return v.reshape(B_, C_, H_ * W_).transpose(0, 2, 1)

    def _from_tokens(t, like):
        B_, C_, H_, W_ = like.shape
        return t.transpose(0, 2, 1).reshape(B_, C_, H_, W_)
    x = x + _L0_conv_ref(_ln_c(x), L0_conv_wq, L0_conv_wk, L0_conv_wv, L0_conv_mix, L0_conv_wo, L0_conv_bo)
    t = _to_tokens(x)
    t = t + _L0_ffn_ref(_ln_t(t), L0_ffn_Wr, L0_ffn_br, L0_ffn_ln_g, L0_ffn_ln_b, L0_ffn_W1, L0_ffn_b1, L0_ffn_W2, L0_ffn_b2)
    x = _from_tokens(t, x)
    return x

_drawn_inputs = setup_inputs


def setup_inputs(seed=0):
    import zlib

    import numpy as np

    out = dict(_drawn_inputs(seed))
    spreads = {'L0_conv_bo': (0.0, 0.1),
     'L0_ffn_br': (0.0, 0.1),
     'L0_ffn_ln_g': (1.0, 0.2),
     'L0_ffn_ln_b': (0.0, 0.282),
     'L0_ffn_b1': (0.0, 0.275),
     'L0_ffn_b2': (0.0, 0.1)}
    factors = {}
    for name, (base, spread) in spreads.items():
        noise = np.random.default_rng([zlib.crc32(name.encode()), seed]).standard_normal(out[name].shape)
        drawn = base * np.exp(spread * noise) if base else spread * noise
        out[name] = jnp.asarray(drawn.astype(out[name].dtype))
    for name, factor in factors.items():
        out[name] = (out[name] * factor).astype(out[name].dtype)
    return out
```

```python
import numpy as np
import concourse.bass as bass
from concourse import mybir
from contextlib import ExitStack

B, C, IMG = 8, 128, 32
TOK = IMG * IMG
HEADS, DH = 8, 32
INNER = HEADS * DH
TAPS = 9
PAD = IMG + 2
EXP, HID = 8, 512
SCALE = DH ** -0.5
P = 128
NB = 512
QC = 4
QT = TOK // QC
KC = TOK // P
UNITS = HEADS * QC
MROW = 3 * DH
VW = INNER + 2
HK = HID // P
TILES = B * TOK // NB
LO = 32


def wait(eng, sem, count):
    if isinstance(count, int) and count <= 0:
        return
    eng.wait_ge(sem, count)


def build(nc, x, wq, wk, wv, mix, wo, bo, wr, br, ln_g, ln_b, w1, b1, w2, b2,
          pos2, rot_cos, rot_sin, rank, out):
    f32, f32r = mybir.dt.float32, mybir.dt.float32r
    ALU, ACT, AX = mybir.AluOpType, mybir.ActivationFunctionType, mybir.AxisListType.X

    x_d = x.rearrange("b c h w -> b c (h w)")
    out_d = out.rearrange("b c h w -> b c (h w)")
    mid_d = nc.dram_tensor("mid", (B, C, TOK), f32, kind="Internal").ap()

    def f(ap):
        return ap.bitcast(f32)

    def bc(ap, shape):
        return ap.to_broadcast(shape)

    ctx = ExitStack()
    with ctx:
        attn = ExitStack()

        def sem(name):
            return ctx.enter_context(nc.semaphore(name))

        def keep(name, shape, dt):
            return ctx.enter_context(nc.sbuf_tensor(name, shape, dt))

        def a_sb(name, shape, dt):
            return attn.enter_context(nc.sbuf_tensor(name, shape, dt))

        PV = [ctx.enter_context(nc.psum_tensor(f"PV{i}", [P, NB], f32)) for i in range(2)]
        ST = [ctx.enter_context(nc.psum_tensor(f"ST{i}", [P, 2 * NB], f32)) for i in range(2)]
        MX = ctx.enter_context(nc.psum_tensor("MX", [P, 2 * NB], f32))

        def conv_bank(g):
            return ST[g % 4 // 2][:, g % 2 * NB:(g % 2 + 1) * NB]

        ident = keep("ident", [P, P], f32)
        mean_w = keep("mean_w", [P, P], f32)
        half_neg = keep("half_neg", [P, 1], f32)
        ones_row = keep("ones_row", [1, P], f32)

        Eh = a_sb("Eh", [P, 2, KC, QT], f32r)
        El = a_sb("El", [P, 2, KC, QT], f32r)
        E32 = a_sb("E32", [P, 2, 4 * QT], f32)
        kst = [a_sb(f"kst{i}", [MROW + 1, TOK], f32r) for i in range(2)]
        qst = [a_sb(f"qst{i}", [MROW + 1, TOK], f32r) for i in range(2)]
        src = a_sb("src", [P, 4, 2, TOK], f32)
        xh = a_sb("xh", [P, PAD * PAD], f32r)
        xl = a_sb("xl", [P, PAD * PAD], f32r)
        wqh = a_sb("wqh", [P, INNER], f32r)
        wql = a_sb("wql", [P, INNER], f32r)
        wch = a_sb("wch", [P, 2, TAPS, INNER], f32r)
        wcl = a_sb("wcl", [P, 2, TAPS, INNER], f32r)
        woh = a_sb("woh", [P, 2, 2 * C], f32r)
        wol = a_sb("wol", [P, 2, 2 * C], f32r)
        vh = a_sb("vh", [P, KC, VW], f32r)
        vl = a_sb("vl", [P, KC, INNER], f32r)
        acc = a_sb("acc", [P, KC, INNER], f32)
        cos_sb = a_sb("cos_sb", [P, TOK], f32)
        sin_sb = a_sb("sin_sb", [P, TOK], f32)
        pos_sb = a_sb("pos_sb", [P, TOK], f32)
        xt = a_sb("xt", [P, TOK], f32)
        xg = a_sb("xg", [P, TOK], f32)
        mcol = a_sb("mcol", [P, 2, 2, P], f32r)
        negid = a_sb("negid", [P, P], f32r)
        tmp = a_sb("tmp", [P, 2, INNER], f32)
        rl = a_sb("rl", [P, 2], f32)
        eg = a_sb("eg", [P, NB], f32)
        mix_row = a_sb("mix_row", [1, HEADS * HEADS], f32)
        mix_sb = a_sb("mix_sb", [P, HEADS * HEADS], f32)
        bo_sb = a_sb("bo_sb", [P, 2], f32)
        nbo = a_sb("nbo", [P, 1], f32)
        raw = src[:, :, :, :].rearrange("p a b c -> p (a b c)")
        RAWC = C * TAPS
        raw_c = [[raw[:, (2 * w + oc) * RAWC:(2 * w + oc + 1) * RAWC] for oc in range(2)] for w in range(2)]
        raw_q = [raw[:, 4 * RAWC + oc * C:4 * RAWC + (oc + 1) * C] for oc in range(2)]
        raw_o = [raw[:, 4 * RAWC + 2 * C + oc * INNER:4 * RAWC + 2 * C + (oc + 1) * INNER] for oc in range(2)]
        ln_x = src[:, 0, 0, :]
        ln_s = src[:, 1, 0, :]
        rot_a = [E32[:, i, 0:NB] for i in range(2)]
        rot_s = [E32[:, i, NB:2 * NB] for i in range(2)]
        vt = [a_sb(f"vt{i}", [P, NB], f32) for i in range(2)]
        oh = Eh[:, 1, 0:4, :].rearrange("p a b -> p (a b)").rearrange("p (c t) -> p c t", c=2)
        ol = El[:, 1, 0:4, :].rearrange("p a b -> p (a b)").rearrange("p (c t) -> p c t", c=2)

        attn_end = attn.pop_all()
        attn_end.close()

        w1h = keep("w1h", [P, EXP, HID], f32r)
        w1l = keep("w1l", [P, EXP, HID], f32r)
        w2h = keep("w2h", [P, EXP, HK, C], f32r)
        w2l = keep("w2l", [P, EXP, HK, C], f32r)
        w1raw = keep("w1raw", [P, EXP, HID], f32)
        h32 = keep("h32", [P, 2, HK, NB], f32)
        hh = keep("hh", [P, 2, HK, NB], f32r)
        hl = keep("hl", [P, 2, HK, NB], f32r)
        w2raw = h32[:, :, :, :].rearrange("p a b c -> p (a b c)").rearrange("p (e k d) -> p e k d", e=EXP, k=HK)
        xm = [keep(f"xm{i}", [P, NB], f32) for i in range(2)]
        fc = keep("fc", [P, NB], f32)
        fs = keep("fs", [P, NB], f32)
        fa = keep("fa", [P, NB], f32)
        xnh = [keep(f"xnh{i}", [P, NB], f32r) for i in range(2)]
        xnl = [keep(f"xnl{i}", [P, NB], f32r) for i in range(2)]
        wb = [keep(f"wb{i}", [P, NB], f32) for i in range(2)]
        ty = [keep(f"ty{i}", [P, NB], f32) for i in range(2)]
        ya = [keep(f"ya{i}", [P, NB], f32) for i in range(2)]
        sel32 = keep("sel32", [LO + EXP, EXP, P], f32)
        sel = keep("sel", [LO + EXP, EXP, P], f32r)
        wst = [keep(f"wst{i}", [LO + EXP, NB], f32r) for i in range(2)]
        wt32 = keep("wt32", [EXP, NB], f32)
        b2_sb = keep("b2_sb", [EXP, C], f32)
        vec_row = keep("vec_row", [EXP, 2, C], f32)
        b1_row = keep("b1_row", [EXP * HK, P], f32)
        vec_col = keep("vec_col", [P, 2, EXP], f32)
        b1_col = keep("b1_col", [P, EXP * HK], f32)
        wr_sb = keep("wr_sb", [C, EXP], f32)
        br_row = keep("br_row", [1, EXP], f32)
        br_sb = keep("br_sb", [P, EXP], f32)
        rank_row = keep("rank_row", [1, EXP], f32)
        rank_sb = keep("rank_sb", [P, EXP], f32)
        e_const = keep("e_const", [P, 1], f32)
        R4 = NB // P
        lg = keep("lg", [P, R4, EXP], f32)
        r_c = keep("r_c", [P, R4, EXP], f32)
        r_o1 = keep("r_o1", [P, R4, EXP], f32)
        r_o2 = keep("r_o2", [P, R4, EXP], f32)
        r_l2 = keep("r_l2", [P, R4, EXP], f32)
        r_d = keep("r_d", [P, R4, EXP], f32)
        r_e = keep("r_e", [P, R4, EXP], f32)
        r_w = keep("r_w", [P, R4, EXP], f32)
        r_m = keep("r_m", [P, 6, R4], f32)

        H = [ST[k // 2][:, k % 2 * NB:(k % 2 + 1) * NB] for k in range(HK)]
        Y, WB = PV[0][:, :], PV[1][:, :]
        PR, LG = MX[:, 0:NB], MX[:, NB:NB + R4 * EXP]

        s_const = sem("s_const")
        s_ones = sem("s_ones")
        s_negid = sem("s_negid")
        s_wload = sem("s_wload")
        s_tload = sem("s_tload")
        s_wT = sem("s_wT")
        s_wThi = sem("s_wThi")
        s_wTlo = sem("s_wTlo")
        s_mixp = sem("s_mixp")
        s_mix = sem("s_mix")
        s_xt = sem("s_xt")
        s_mean = sem("s_mean")
        s_cent = sem("s_cent")
        s_sq = sem("s_sq")
        s_var = sem("s_var")
        s_ve = sem("s_ve")
        s_rstd = sem("s_rstd")
        s_xn = sem("s_xn")
        s_xhi = sem("s_xhi")
        s_xin = sem("s_xin")
        s_cv = sem("s_cv")
        s_rot = sem("s_rot")
        s_rf = sem("s_rf")
        s_rr = sem("s_rr")
        s_rhi = sem("s_rhi")
        s_rlo = sem("s_rlo")
        s_stk = [sem(f"s_stk{i}") for i in range(2)]
        s_vt = sem("s_vt")
        s_vT = sem("s_vT")
        s_vhi = sem("s_vhi")
        s_vlo = sem("s_vlo")
        s_mx = sem("s_mx")
        s_red = sem("s_red")
        s_mt = sem("s_mt")
        s_mrow = sem("s_mrow")
        s_st = sem("s_st")
        s_ex = sem("s_ex")
        s_lo = sem("s_lo")
        s_pv = sem("s_pv")
        s_rl = sem("s_rl")
        s_nrm = sem("s_nrm")
        s_acc = sem("s_acc")
        s_tr = sem("s_tr")
        s_ohi = sem("s_ohi")
        s_olo = sem("s_olo")
        s_wo = sem("s_wo")
        s_eg = sem("s_eg")
        s_gch = sem("s_gch")
        s_gate = sem("s_gate")
        s_xg = sem("s_xg")
        s_mid = sem("s_mid")

        t_load = sem("t_load")
        t_vec = sem("t_vec")
        t_cst = sem("t_cst")
        t_sel = sem("t_sel")
        t_col = sem("t_col")
        t_colv = sem("t_colv")
        t_lnb = sem("t_lnb")
        t_scale = sem("t_scale")
        t_whi = sem("t_whi")
        t_wlo = sem("t_wlo")
        t_xm = [sem(f"t_xm{i}") for i in range(2)]
        t_m1, t_c1, t_q1, t_v1, t_e1, t_r1, t_a = (sem(n) for n in (
            "t_m1", "t_c1", "t_q1", "t_v1", "t_e1", "t_r1", "t_a"))
        t_m2, t_c2, t_q2, t_v2, t_e2, t_r2, t_xn = (sem(n) for n in (
            "t_m2", "t_c2", "t_q2", "t_v2", "t_e2", "t_r2", "t_xn"))
        t_xnh, t_xnl = sem("t_xnh"), sem("t_xnl")
        t_rc = sem("t_rc")
        t_d = sem("t_d")
        t_ex = sem("t_ex")
        t_w = sem("t_w")
        t_wT = sem("t_wT")
        t_w32, t_whl = sem("t_w32"), sem("t_whl")
        t_b2 = sem("t_b2")
        t_yi = sem("t_yi")
        t_h = sem("t_h")
        t_gl = sem("t_gl")
        t_hh = sem("t_hh")
        t_hh1 = sem("t_hh1")
        t_hl = sem("t_hl")
        t_bc = sem("t_bc")
        t_wb = sem("t_wb")
        t_y = sem("t_y")
        t_yd = sem("t_yd")
        t_ya = sem("t_ya")
        t_out = [sem(f"t_out{i}") for i in range(2)]
        NLINK_R = 12

        def par_of(k):
            k %= 2 * QC
            return k // QC, k % QC, k % 2

        block = ctx.enter_context(nc.Block())

        @block.sync
        def _(sp):
            for w, d in enumerate((wk, wv)):
                for oc in range(2):
                    sp.dma_start(raw_c[w][oc], d.rearrange("o c y x -> o (c y x)")[oc * P:(oc + 1) * P, :]).then_inc(s_wload, 16)
            sp.dma_start(xt[:, :], x_d[0, :, :]).then_inc(s_xt, 16)
            for oc in range(2):
                sp.dma_start(raw_q[oc], wq.rearrange("o c y x -> o (c y x)")[oc * P:(oc + 1) * P, :]).then_inc(s_wload, 16)
                sp.dma_start(raw_o[oc], wo.rearrange("o c y x -> o (c y x)")[oc * P:(oc + 1) * P, :]).then_inc(s_wload, 16)
            sp.dma_start(pos_sb[:, :], pos2).then_inc(s_tload, 16)
            sp.dma_start(cos_sb[:, :], rot_cos).then_inc(s_tload, 16)
            sp.dma_start(sin_sb[:, :], rot_sin).then_inc(s_tload, 16)
            sp.dma_start(mix_row[:, :], mix.rearrange("h g -> (h g)").rearrange("(a n) -> a n", a=1)).then_inc(s_tload, 16)
            sp.dma_start(bo_sb[:, :], bo.rearrange("(a p) -> p a", p=P), allow_slow_non_contiguous=True).then_inc(s_tload, 16)

            def stacks(b, h):
                par, c, r = h % 2, h // 4, h % 4 * DH
                if h == 0:
                    wait(sp, s_rlo, b * 8 + 6)
                wait(sp, s_st, b * 64 + 8 * h - 8)
                for row, part in enumerate((2, 3, 2)):
                    sp.dma_start(f(kst[par][row * DH:(row + 1) * DH, :]), src[r:r + DH, part, c, :]).then_inc(s_stk[par], 16)
                for row, part in enumerate((0, 0, 1)):
                    sp.dma_start(f(qst[par][row * DH:(row + 1) * DH, :]), src[r:r + DH, part, c, :]).then_inc(s_stk[par], 16)

            def store_mid(b, done):
                for hf in range(2):
                    wait(sp, s_gate, done + hf)
                    sp.dma_start(mid_d[b, :, hf * NB:(hf + 1) * NB], xg[:, hf * NB:(hf + 1) * NB]).then_inc(s_mid, 16)

            def batch(b):
                nxt = 1 if isinstance(b, int) else (b + 1) % B
                ready = 1 if isinstance(b, int) else sp.snap(b + 1)
                x_next = x_d[nxt, :, :] if isinstance(b, int) else x_d[sp.snap(nxt), :, :]
                wait(sp, s_xin, ready)
                sp.dma_start(xt[:, :], x_next).then_inc(s_xt, 16)
                if not isinstance(b, int):
                    store_mid(b - 1, sp.snap(b * 2 - 1))
                    wait(sp, s_mid, sp.snap(b * 32))
                sp.dma_start(xg[:, :], x_d[b, :, :]).then_inc(s_xg, 16)
                for h in range(HEADS):
                    stacks(b, h)

            batch(0)
            with sp.Fori(1, B) as b:
                batch(b)
            store_mid(B - 1, 2 * B - 1)

            wait(sp, s_gate, 2 * B)
            sp.dma_start(vec_row[:, 0, :], ln_g).then_inc(t_vec, 16)
            sp.dma_start(vec_row[:, 1, :], ln_b).then_inc(t_vec, 16)
            sp.dma_start(b1_row[:, :], b1.rearrange("e (k p) -> (e k) p", p=P)).then_inc(t_vec, 16)
            sp.dma_start(b2_sb[:, :], b2).then_inc(t_vec, 16)
            sp.dma_start(wr_sb[:, :], wr).then_inc(t_vec, 16)
            sp.dma_start(br_row[:, :], br.rearrange("(a n) -> a n", a=1)).then_inc(t_vec, 16)
            sp.dma_start(rank_row[:, :], rank).then_inc(t_vec, 16)
            sp.dma_start(w1raw[:, :, :], w1.rearrange("e d h -> d e h")).then_inc(t_load, 16)
            sp.dma_start(w2raw, w2.rearrange("e (k p) d -> p e k d", p=P)).then_inc(t_load, 16)
            wait(sp, s_mid, 32 * B)

            def load_tile(it, par):
                sp.dma_start(xm[par][:, :], mid_d[it, :, par * NB:(par + 1) * NB]).then_inc(t_xm[par], 16)

            def store_tile(it, par, added):
                wait(sp, t_ya, added)
                sp.dma_start(out_d[it, :, par * NB:(par + 1) * NB], ya[par][:, :]).then_inc(t_out[par], 16)

            load_tile(0, 0)
            load_tile(0, 1)
            with sp.Fori(0, B - 1) as it:
                added = [sp.snap(it * 16 + 2 + EXP * (par + 1)) for par in range(2)]
                begun = [sp.snap(it * 2 + par + 1) for par in range(2)]
                for par in range(2):
                    store_tile(it, par, added[par])
                    wait(sp, t_yi, begun[par])
                    load_tile(it + 1, par)
            for par in range(2):
                store_tile(B - 1, par, (B - 1) * 16 + 2 + EXP * (par + 1))
            for par in range(2):
                sp.wait_ge(t_out[par], 16 + 16 * B)

        @block.gpsimd
        def _(pool):
            nc.gpsimd.memset(ident[:, :], 0.0).then_inc(s_const, 1)
            pool.wait_ge(s_const, 1)
            nc.gpsimd.affine_select(out=ident[:, :], in_=ident[:, :], compare_op=ALU.not_equal, fill=1.0,
                                    base=0, pattern=[[-1, P]], channel_multiplier=1).then_inc(s_const, 1)
            nc.gpsimd.memset(mean_w[:, :], 1.0 / C).then_inc(s_const, 1)
            nc.gpsimd.memset(half_neg[:, :], -0.5).then_inc(s_const, 1)
            nc.gpsimd.memset(ones_row[:, :], 1.0).then_inc(s_const, 1)
            nc.gpsimd.memset(f(xh[:, :]), 0.0).then_inc(s_const, 1)
            nc.gpsimd.memset(f(xl[:, :]), 0.0).then_inc(s_const, 1)
            nc.gpsimd.memset(f(mcol[:, :, :, :]), 0.0).then_inc(s_const, 1)
            nc.gpsimd.memset(f(vh[:, :, INNER:VW]), 1.0).then_inc(s_const, 1)
            nc.gpsimd.memset(tmp[:, :, :], 0.0).then_inc(s_acc, 2)

            def rstd(n):
                wait(pool, s_ve, n + 1)
                nc.gpsimd.tensor_tensor(ln_s, ln_s, half_neg[:, 0:1].to_broadcast([P, TOK]), ALU.pow).then_inc(s_rstd, 1)

            def add(n, k, p):
                ic = k % QC * 2 + p
                wait(pool, s_nrm, 2 * n + p + 3)
                wait(pool, s_acc, 2 * n + p + 2)
                nc.gpsimd.tensor_tensor(acc[:, ic, :], acc[:, ic, :], tmp[:, p, :], ALU.add).then_inc(s_acc, 1)

            def pair(n0, last=False, b=None):
                for k in range(2 * QC):
                    for p in range(2):
                        add(n0 + k, k, p)
                    if last and k == 6:
                        rstd(b + 1)

            def batch(b):
                with pool.Fori(0, HEADS // 2 - 1) as hp:
                    pair(b * UNITS + hp * 8)
                pair(b * UNITS + UNITS - 8, True, b)

            rstd(0)
            batch(0)
            with pool.Fori(1, B) as b:
                batch(b)

            wait(pool, s_gate, 2 * B)
            nc.gpsimd.memset(sel32[:, :, :], 0.0).then_inc(t_cst, 1)
            pool.wait_ge(t_cst, 1)
            for i in range(2):
                nc.gpsimd.affine_select(out=sel32[:, :, :], in_=sel32[:, :, :], compare_op=ALU.not_equal, fill=1.0,
                                        base=-LO * i, pattern=[[-1, EXP], [0, P]], channel_multiplier=1).then_inc(t_cst, 1)
                pool.wait_ge(t_cst, 2 + i)
            nc.gpsimd.memset(e_const[:, :], float(np.e)).then_inc(t_cst, 1)
            for i in range(2):
                nc.gpsimd.memset(f(wst[i][:, :]), 0.0).then_inc(t_cst, 1)
            for i in range(2):
                nc.gpsimd.memset(ya[i][:, :], 0.0).then_inc(t_out[i], 16)
            nc.gpsimd.memset(ty[0][:, :], 0.0).then_inc(t_ya, 2)

            def square1(t):
                wait(pool, t_c1, t + 1)
                nc.gpsimd.tensor_tensor(fs[:, :], fc[:, :], fc[:, :], ALU.mult).then_inc(t_q1, 1)

            def rsqrt1(t):
                wait(pool, t_e1, t + 1)
                nc.gpsimd.tensor_tensor(fs[:, :], fs[:, :], half_neg[:, 0:1].to_broadcast([P, NB]), ALU.pow).then_inc(t_r1, 1)

            def square2(t):
                wait(pool, t_c2, t + 1)
                nc.gpsimd.tensor_tensor(fs[:, :], fc[:, :], fc[:, :], ALU.mult).then_inc(t_q2, 1)

            def rsqrt2(t):
                wait(pool, t_e2, t + 1)
                nc.gpsimd.tensor_tensor(fs[:, :], fs[:, :], half_neg[:, 0:1].to_broadcast([P, NB]), ALU.pow).then_inc(t_r2, 1)

            def exp_logits(t):
                wait(pool, t_d, t + 1)
                flat = r_d[:, :, :].rearrange("p a e -> p (a e)")
                nc.gpsimd.tensor_tensor(r_e[:, :, :].rearrange("p a e -> p (a e)"),
                                        e_const[:, 0:1].to_broadcast([P, R4 * EXP]), flat, ALU.pow).then_inc(t_ex, 1)

            def tile(it, par, more):
                t = it * 2 + par
                for e in range(EXP):
                    s = it * 16 + par * EXP + e
                    if more:
                        if e == 0:
                            square1(t + 1)
                        if e == 1:
                            rsqrt1(t + 1)
                        if e == 2:
                            square2(t + 1)
                            exp_logits(t + 1)
                        if e == 3:
                            rsqrt2(t + 1)
                    wait(pool, t_yd, s + 2)
                    wait(pool, t_ya, s + 2)
                    nc.gpsimd.tensor_tensor(ya[par][:, :], ya[par][:, :], ty[e % 2][:, :], ALU.add).then_inc(t_ya, 1)

            square1(0)
            rsqrt1(0)
            square2(0)
            exp_logits(0)
            rsqrt2(0)
            with pool.Fori(0, B - 1) as it:
                tile(it, 0, True)
                tile(it, 1, True)
            tile(B - 1, 0, True)
            tile(B - 1, 1, False)

        setup = []
        for w in range(2):
            for oc in range(2):
                for t3 in range(3):
                    cols = (slice(None), w, slice(3 * t3, 3 * t3 + 3), slice(oc * P, (oc + 1) * P))
                    srcs = [raw_c[w][oc].rearrange("o (c t) -> o t c", t=TAPS)[:, 3 * t3 + i, :] for i in range(3)]
                    setup.append((wch[cols], wcl[cols], srcs))
        setup.append((wqh[:, :].rearrange("p (a o) -> p a o", a=2), wql[:, :].rearrange("p (a o) -> p a o", a=2), raw_q))
        for kk in range(2):
            cols = (slice(None), kk, slice(None))
            setup.append((woh[cols].rearrange("p (a o) -> p a o", a=2), wol[cols].rearrange("p (a o) -> p a o", a=2),
                          [raw_o[oc][:, kk * P:(kk + 1) * P] for oc in range(2)]))
        SB = 4

        @block.tensor
        def _(pe):
            def mm(o, w, m, start, stop):
                return nc.tensor.matmul(o, w, m, start=start, stop=stop)

            def split3(o, wh, wl, mh, ml, start, stop):
                mm(o, wh, ml, start, False)
                mm(o, wl, mh, False, False)
                return mm(o, wh, mh, False, stop)

            pe.wait_ge(s_const, 9)
            pe.wait_ge(s_ones, 2)
            pe.wait_ge(s_wload, 16 * 8)
            for g, (_, _, srcs) in enumerate(setup):
                if g >= SB:
                    pe.wait_ge(s_wTlo, g - SB + 1)
                for i, s in enumerate(srcs):
                    last = nc.tensor.transpose(conv_bank(g)[:, i * P:(i + 1) * P], s, ident[:, :])
                last.then_inc(s_wT, 1)
            pe.wait_ge(s_tload, 16 * 5)
            mm(PV[0][:, 0:HEADS * HEADS], ones_row[:, :], mix_row[:, :], True, True).then_inc(s_mixp, 1)

            def mean(n):
                wait(pe, s_xt, (n + 1) * 16)
                for i in range(2):
                    last = mm(MX[:, i * NB:(i + 1) * NB], mean_w[:, :], xt[:, i * NB:(i + 1) * NB], True, True)
                last.then_inc(s_mean, 1)

            def variance(n):
                wait(pe, s_sq, n + 1)
                for i in range(2):
                    last = mm(MX[:, i * NB:(i + 1) * NB], mean_w[:, :], ln_s[:, i * NB:(i + 1) * NB], True, True)
                last.then_inc(s_var, 1)

            img = [t[:, :].rearrange("p (y x) -> p y x", x=PAD) for t in (xh, xl)]

            def conv(b, g):
                kind, c, hf = g // 4, g % 4 // 2, g % 2
                if g == 0:
                    wait(pe, s_xin, b + 1)
                if g >= 4:
                    wait(pe, s_rf, b * 8 + g - 3)
                o = conv_bank(g).rearrange("p (y x) -> p y x", x=IMG)
                taps = [4] if kind == 0 else list(range(TAPS))
                for t in taps:
                    dy, dx = t // 3, t % 3
                    m = [i[:, hf * 16 + dy:hf * 16 + dy + 16, dx:dx + IMG] for i in img]
                    if kind == 0:
                        w = [s[:, c * P:(c + 1) * P] for s in (wqh, wql)]
                    else:
                        w = [s[:, kind - 1, t, c * P:(c + 1) * P] for s in (wch, wcl)]
                    last = split3(o, w[0], w[1], m[0], m[1], t == taps[0], t == taps[-1])
                last.then_inc(s_cv, 1)

            def out_transpose(n, hf):
                if hf == 0:
                    wait(pe, s_acc, (n + 1) * 2 * UNITS + 2)
                for c in range(2):
                    if hf == 1:
                        wait(pe, s_olo, n * 4 + c + 1)
                    for j in range(4):
                        last = nc.tensor.transpose(PV[c][:, j * P:(j + 1) * P],
                                                   acc[:, 4 * hf + j, c * P:(c + 1) * P], ident[:, :])
                    last.then_inc(s_tr, 1)

            def out_project(n, hf):
                wait(pe, s_olo, n * 4 + 2 * hf + 2)
                if hf == 1:
                    wait(pe, s_gate, n * 2 + 1)
                for o in range(2):
                    for c in range(2):
                        cols = slice(o * P, (o + 1) * P)
                        last = split3(MX[:, o * NB:(o + 1) * NB], woh[:, c, cols], wol[:, c, cols],
                                      oh[:, c, :], ol[:, c, :], c == 0, c == 1)
                last.then_inc(s_wo, 1)

            def v_transpose(b, g):
                wait(pe, s_vt, b * 4 + g + 1)
                if g >= 2:
                    wait(pe, s_vlo, b * 4 + g - 1)
                for j in range(4):
                    last = nc.tensor.transpose(PV[g % 2][:, j * P:(j + 1) * P], vt[g % 2][:, j * P:(j + 1) * P], ident[:, :])
                last.then_inc(s_vT, 1)

            def max_scores(n, k, p, head=None):
                st, q, _ = par_of(k)
                if p == 0:
                    wait(pe, s_mrow, n)
                    if q == 0:
                        wait(pe, s_stk[st], head)
                else:
                    wait(pe, s_red, 2 * n + 1)
                for i in range(2):
                    last = mm(MX[:, i * NB:(i + 1) * NB], qst[st][0:MROW, q * QT + p * P:q * QT + (p + 1) * P],
                              kst[st][0:MROW, i * NB:(i + 1) * NB], True, True)
                last.then_inc(s_mx, 1)

            def max_row(n, k):
                wait(pe, s_red, 2 * n + 2)
                for p in range(2):
                    last = mm(MX[:, p * P:(p + 1) * P], mcol[:, k % 2, p, :], negid[:, :], True, True)
                last.then_inc(s_mt, 1)

            def scores(n, k, p):
                st, q, _ = par_of(k)
                if p == 0:
                    wait(pe, s_mrow, n + 1)
                wait(pe, s_ex, 2 * n + p - 1)
                for j in range(4):
                    jc = 4 * p + j
                    last = mm(ST[p][:, j * QT:(j + 1) * QT], kst[st][:, jc * P:(jc + 1) * P],
                              qst[st][:, q * QT:(q + 1) * QT], True, True)
                last.then_inc(s_st, 1)

            def values(n, k, p, jcs):
                e = k % 2
                for jc in jcs:
                    if jc == 0:
                        wait(pe, s_nrm, 2 * n + p + 1)
                    if p == 0 and jc % 4 == 0:
                        wait(pe, s_lo, 2 * n + jc // 4 + 1)
                    hi, lo = (t[:, e, jc, p * P:(p + 1) * P] for t in (Eh, El))
                    mm(PV[p][:, 0:VW], lo, vh[:, jc, :], jc == 0, False)
                    mm(PV[p][:, 0:INNER], hi, vl[:, jc, :], False, False)
                    last = mm(PV[p][:, 0:VW], hi, vh[:, jc, :], False, jc == KC - 1)
                if KC - 1 in jcs:
                    last.then_inc(s_pv, 1)

            def pair(n0, stk_next, last=False, b=None):
                for k in range(2 * QC):
                    n = n0 + k
                    head = stk_next[(k + 2) // QC] if (k + 2) % QC == 0 else None
                    for p in range(2):
                        if p == 0 and not (last and k == 7):
                            max_row(n + 1, k + 1)
                        values(n, k, p, range(0, 4))
                        if not (last and k == 7):
                            scores(n + 1, k + 1, p)
                        if not (last and k >= 6):
                            max_scores(n + 2, k + 2, p, head)
                        if last and k == 6 and p == 0:
                            wait(pe, s_mrow, n + 2)
                            mean(b + 1)
                        if last and k == 6 and p == 1:
                            variance(b + 1)
                        values(n, k, p, range(4, KC))

            def batch(b):
                prev = None if isinstance(b, int) else b - 1
                n = b * UNITS
                for g in range(5):
                    conv(b, g)
                if prev is not None:
                    out_transpose(prev, 0)
                conv(b, 5)
                if prev is not None:
                    out_project(prev, 0)
                    out_transpose(prev, 1)
                conv(b, 6)
                if prev is not None:
                    out_project(prev, 1)
                conv(b, 7)
                conv(b, 8)
                max_scores(n, 0, 0, b * 384 + 96)
                conv(b, 9)
                v_transpose(b, 0)
                max_scores(n, 0, 1)
                conv(b, 10)
                v_transpose(b, 1)
                max_row(n, 0)
                conv(b, 11)
                v_transpose(b, 2)
                max_scores(n + 1, 1, 0)
                scores(n, 0, 0)
                v_transpose(b, 3)
                max_scores(n + 1, 1, 1)
                wait(pe, s_vlo, b * 4 + 4)
                scores(n, 0, 1)
                with pe.Fori(0, HEADS // 2 - 1) as hp:
                    pair(n + hp * 8, [None, b * 384 + hp * 96 + 96, b * 384 + hp * 96 + 192])
                pair(n + UNITS - 8, [None, b * 384 + 384, None], True, b)

            pe.wait_ge(s_negid, 1)
            mean(0)
            variance(0)
            batch(0)
            with pe.Fori(1, B) as b:
                batch(b)
            for hf in range(2):
                out_transpose(B - 1, hf)
                out_project(B - 1, hf)

            pe.wait_ge(s_gate, 2 * B)
            pe.wait_ge(t_vec, 16 * 7)
            for i in range(2):
                nc.tensor.transpose(PV[0][:, i * EXP:(i + 1) * EXP], vec_row[:, i, :], ident[0:EXP, 0:EXP])
            nc.tensor.transpose(PV[0][:, 32:64], b1_row[:, :], ident[0:EXP * HK, 0:EXP * HK])
            mm(PV[0][:, 64:64 + EXP], ones_row[:, :], br_row[:, :], True, True)
            mm(PV[0][:, 80:80 + EXP], ones_row[:, :], rank_row[:, :], True, True).then_inc(t_col, 1)
            pe.wait_ge(t_load, 32)
            pe.wait_ge(t_colv, 1)
            for e in range(EXP):
                for k in range(HK):
                    c = e * HK + k
                    last = mm(PV[1][:, c:c + 1], w1raw[:, e, k * P:(k + 1) * P], vec_col[:, 1, e:e + 1], True, True)
            last.then_inc(t_lnb, 1)

            def mean1(it, par):
                wait(pe, t_xm[par], (it + 1) * 16)
                wait(pe, t_yi, it * 2 + par)
                mm(PR, mean_w[:, :], xm[par][:, :], True, True).then_inc(t_m1, 1)

            def var1(t):
                wait(pe, t_q1, t + 1)
                mm(PR, mean_w[:, :], fs[:, :], True, True).then_inc(t_v1, 1)

            def mean2(t):
                wait(pe, t_a, t + 1)
                for j in range(R4):
                    mm(LG[:, j * EXP:(j + 1) * EXP], fa[:, j * P:(j + 1) * P], wr_sb[:, :], True, True)
                mm(PR, mean_w[:, :], fa[:, :], True, True).then_inc(t_m2, 1)

            def var2(t):
                wait(pe, t_q2, t + 1)
                mm(PR, mean_w[:, :], fs[:, :], True, True).then_inc(t_v2, 1)

            def route_transpose(t):
                wait(pe, t_w, t + 1)
                wait(pe, t_e2, t + 1)
                for j in range(R4):
                    last = nc.tensor.transpose(PR[0:EXP, j * P:(j + 1) * P], r_w[:, j, :], ident[:, :])
                last.then_inc(t_wT, 1)

            def bias2(t):
                wait(pe, t_w32, (t + 1) * 2)
                wait(pe, t_whl, t + 1)
                mm(PR, b2_sb[:, :], wt32[:, :], True, True).then_inc(t_b2, 1)

            def hidden(s, e, par):
                for k in range(HK):
                    wait(pe, t_gl, 4 * s - 3 + k)
                    cols = slice(k * P, (k + 1) * P)
                    split3(H[k], w1h[:, e, cols], w1l[:, e, cols], xnh[par][:, :], xnl[par][:, :], True, True).then_inc(t_h, 1)

            def spread(s, e, par):
                wait(pe, t_wb, s)
                mm(WB, sel[:, e, :], wst[par][:, :], True, True).then_inc(t_bc, 1)

            def project(s, e):
                i = e % 2
                wait(pe, t_yd, s + 1)
                for k in range(HK):
                    if k % 2 == 0:
                        wait(pe, t_hl, 2 * s + k // 2 + 1)
                    last = split3(Y, w2h[:, e, k, :], w2l[:, e, k, :], hh[:, i, k, :], hl[:, i, k, :], k == 0, k == HK - 1)
                last.then_inc(t_y, 1)

            def tile(it, par, more):
                t = it * 2 + par
                for e in range(EXP):
                    s = it * 16 + par * EXP + e
                    if e < EXP - 1 or more:
                        nx = par if e < EXP - 1 else 1 - par
                        if e == EXP - 1:
                            wait(pe, t_xnl, t + 2)
                        hidden(s + 1, (e + 1) % EXP, nx)
                        spread(s + 1, (e + 1) % EXP, nx)
                    if more:
                        if e == 0:
                            mean1(it + par, 1 - par)
                        if e == 1:
                            var1(t + 1)
                        if e == 2:
                            mean2(t + 1)
                        if e == 3:
                            var2(t + 1)
                        if e == 4:
                            route_transpose(t + 1)
                        if e == 5:
                            bias2(t + 1)
                    project(s, e)

            pe.wait_ge(t_colv, 2)
            mean1(0, 0)
            var1(0)
            mean2(0)
            var2(0)
            route_transpose(0)
            bias2(0)
            pe.wait_ge(t_sel, 1)
            pe.wait_ge(t_wlo, 2)
            wait(pe, t_xnl, 1)
            hidden(0, 0, 0)
            spread(0, 0, 0)
            with pe.Fori(0, B - 1) as it:
                tile(it, 0, True)
                tile(it, 1, True)
            tile(B - 1, 0, True)
            tile(B - 1, 1, False)

        @block.scalar
        def _(act):
            def copy(o, i, func=ACT.Copy, **kw):
                return nc.scalar.activation(o, i, func, **kw)

            act.wait_ge(s_const, 9)
            copy(negid[:, :], ident[:, :], scale=-1.0).then_inc(s_negid, 1)
            for g, (hi, _, srcs) in enumerate(setup):
                act.wait_ge(s_wT, g + 1)
                copy(hi, conv_bank(g)[:, 0:len(srcs) * P].rearrange("p (a o) -> p a o", o=P)).then_inc(s_wThi, 1)

            def square(n):
                wait(act, s_cent, n + 1)
                copy(ln_s, ln_x, ACT.Square).then_inc(s_sq, 1)

            def input_hi(n):
                wait(act, s_xn, 2 * n + 2)
                inner = xh[:, :].rearrange("p (y x) -> p y x", x=PAD)[:, 1:IMG + 1, 1:IMG + 1]
                copy(inner, ln_x.rearrange("p (y x) -> p y x", x=IMG)).then_inc(s_xhi, 1)

            def rot_hi(b, g):
                kind, c, hf = g // 4, g % 4 // 2, g % 2
                wait(act, s_rr, b * 8 + g + 1)
                copy(src[:, 2 * kind, c, hf * NB:(hf + 1) * NB].bitcast(f32r), rot_a[g % 2]).then_inc(s_rhi, 1)

            def out_hi(n, hf):
                for c in range(2):
                    wait(act, s_tr, n * 4 + 2 * hf + c + 1)
                    if hf == 1:
                        wait(act, s_wo, n * 2 + 1)
                    copy(oh[:, c, :], PV[c][:, :]).then_inc(s_ohi, 1)

            def gate_exp(n, hf):
                wait(act, s_wo, n * 2 + hf + 1)
                if hf == 1:
                    wait(act, s_gate, n * 2 + 1)
                copy(eg[:, :], MX[:, NB:2 * NB], ACT.Exp, bias=nbo[:, 0:1], scale=-1.0).then_inc(s_eg, 1)

            def v_copy(b, g):
                wait(act, s_cv, b * 12 + 8 + g + 1)
                if g >= 2:
                    wait(act, s_vT, b * 4 + g - 1)
                copy(vt[g % 2][:, :], conv_bank(g)).then_inc(s_vt, 1)

            def v_hi(b, g):
                c, hf = g // 2, g % 2
                wait(act, s_vT, b * 4 + g + 1)
                copy(vh[:, 4 * hf:4 * hf + 4, c * P:(c + 1) * P],
                     PV[g % 2][:, :].rearrange("p (j o) -> p j o", o=P)).then_inc(s_vhi, 1)

            def row_copy(n, k):
                st, q, _ = par_of(k)
                wait(act, s_mt, n + 1)
                copy(qst[st][MROW:MROW + 1, q * QT:(q + 1) * QT], MX[MROW:MROW + 1, 0:QT]).then_inc(s_mrow, 1)

            def exps(n, k, p):
                wait(act, s_st, 2 * n + p + 1)
                copy(Eh[:, k % 2, 4 * p:4 * p + 4, :].rearrange("p a b -> p (a b)"), ST[p][:, :], ACT.Exp, scale=SCALE)
                wait(act, s_lo, 2 * n + p - 1)
                copy(E32[:, p, :], ST[p][:, :], ACT.Exp, scale=SCALE).then_inc(s_ex, 1)

            def pair(n0, last=False, b=None):
                for k in range(2 * QC):
                    if not (last and k == 7):
                        row_copy(n0 + k + 1, k + 1)
                        for p in range(2):
                            exps(n0 + k + 1, k + 1, p)
                            if last and k == 6 and p == 0:
                                square(b + 1)
                    else:
                        input_hi(b + 1)

            def batch(b):
                prev = None if isinstance(b, int) else b - 1
                for g in range(5):
                    rot_hi(b, g)
                if prev is not None:
                    out_hi(prev, 0)
                rot_hi(b, 5)
                if prev is not None:
                    gate_exp(prev, 0)
                    out_hi(prev, 1)
                rot_hi(b, 6)
                if prev is not None:
                    gate_exp(prev, 1)
                rot_hi(b, 7)
                v_copy(b, 0)
                v_copy(b, 1)
                v_hi(b, 0)
                v_copy(b, 2)
                v_hi(b, 1)
                row_copy(b * UNITS, 0)
                v_copy(b, 3)
                v_hi(b, 2)
                exps(b * UNITS, 0, 0)
                v_hi(b, 3)
                exps(b * UNITS, 0, 1)
                with act.Fori(0, HEADS // 2 - 1) as hp:
                    pair(b * UNITS + hp * 8)
                pair(b * UNITS + UNITS - 8, True, b)

            act.wait_ge(s_mix, 2)
            square(0)
            input_hi(0)
            batch(0)
            with act.Fori(1, B) as b:
                batch(b)
            for hf in range(2):
                out_hi(B - 1, hf)
                gate_exp(B - 1, hf)

            act.wait_ge(s_gate, 2 * B)
            act.wait_ge(t_cst, 3)
            copy(sel[:, :, :], sel32[:, :, :]).then_inc(t_sel, 1)
            act.wait_ge(t_load, 32)
            copy(w2h[:, :, :, :], w2raw).then_inc(t_whi, 1)
            act.wait_ge(t_scale, 1)
            copy(w1h[:, :, :], w1raw[:, :, :]).then_inc(t_whi, 1)

            def input_hi2(t, par):
                wait(act, t_xn, t + 1)
                copy(xnh[par][:, :], fc[:, :]).then_inc(t_xnh, 1)

            def route_copy(t, par):
                wait(act, t_wT, t + 1)
                copy(wst[par][0:EXP, :], PR[0:EXP, :]).then_inc(t_w32, 1)
                copy(wt32[:, :], PR[0:EXP, :]).then_inc(t_w32, 1)

            def gelus(s, e):
                i = e % 2
                for k in range(HK):
                    wait(act, t_h, 4 * s + k + 1)
                    copy(h32[:, i, k, :], H[k], ACT.Gelu, bias=b1_col[:, e * HK + k:e * HK + k + 1]).then_inc(t_gl, 1)
                    if k == 2:
                        wait(act, t_gl, 4 * s + 2)
                        copy(hh[:, i, 0:2, :].rearrange("p a b -> p (a b)"),
                             h32[:, i, 0:2, :].rearrange("p a b -> p (a b)")).then_inc(t_hh, 1)

            def spread_copy(s, e):
                wait(act, t_bc, s + 1)
                wait(act, t_yd, s)
                copy(wb[e % 2][:, :], WB).then_inc(t_wb, 1)

            def tile(it, par, more):
                t = it * 2 + par
                for e in range(EXP):
                    s = it * 16 + par * EXP + e
                    if e < EXP - 1 or more:
                        gelus(s + 1, (e + 1) % EXP)
                        spread_copy(s + 1, (e + 1) % EXP)
                    if more and e == 4:
                        input_hi2(t + 1, 1 - par)
                        route_copy(t + 1, 1 - par)

            input_hi2(0, 0)
            act.wait_ge(t_cst, 6)
            route_copy(0, 0)
            act.wait_ge(t_wlo, 2)
            gelus(0, 0)
            spread_copy(0, 0)
            with act.Fori(0, B - 1) as it:
                tile(it, 0, True)
                tile(it, 1, True)
            tile(B - 1, 0, True)
            tile(B - 1, 1, False)

        @block.vector
        def _(dve):
            tt, ts, stt = nc.vector.tensor_tensor, nc.vector.tensor_scalar, nc.vector.scalar_tensor_tensor

            for i in range(2):
                nc.vector.memset(f(kst[i][MROW:MROW + 1, :]), 1.0).then_inc(s_ones, 1)
            for g, (hi, lo, srcs) in enumerate(setup):
                dve.wait_ge(s_wThi, g + 1)
                tt(lo, conv_bank(g)[:, 0:len(srcs) * P].rearrange("p (a o) -> p a o", o=P), f(hi), ALU.subtract).then_inc(s_wTlo, 1)
            dve.wait_ge(s_mixp, 1)
            nc.vector.tensor_copy(mix_sb[:, :], PV[0][:, 0:HEADS * HEADS]).then_inc(s_mix, 1)
            ts(nbo[:, :], bo_sb[:, 1:2], -1.0, None, ALU.mult).then_inc(s_mix, 1)
            nc.vector.memset(acc[:, :, :], 0.0).then_inc(s_nrm, 2)

            def centre(n):
                wait(dve, s_mean, n + 1)
                tt(ln_x, xt[:, :], MX[:, :], ALU.subtract).then_inc(s_cent, 1)

            def var_eps(n):
                wait(dve, s_var, n + 1)
                ts(ln_s, MX[:, :], 1e-6, None, ALU.add).then_inc(s_ve, 1)

            def input_lo(n):
                wait(dve, s_rstd, n + 1)
                tt(ln_x, ln_x, ln_s, ALU.mult).then_inc(s_xn, 1)
                wait(dve, s_xn, 2 * n + 1)
                tt(ln_x, ln_x, pos_sb[:, :], ALU.add).then_inc(s_xn, 1)
                wait(dve, s_xhi, n + 1)
                hi, lo = (t[:, :].rearrange("p (y x) -> p y x", x=PAD)[:, 1:IMG + 1, 1:IMG + 1] for t in (xh, xl))
                tt(lo, ln_x.rearrange("p (y x) -> p y x", x=IMG), f(hi), ALU.subtract).then_inc(s_xin, 1)

            swap = [i ^ 1 for i in range(32)]

            def rotate(b, g):
                kind, c, hf = g // 4, g % 4 // 2, g % 2
                cols = slice(hf * NB, (hf + 1) * NB)
                base = b * 24 + g * 3
                a, s, bank = rot_a[g % 2], rot_s[g % 2], conv_bank(g)
                wait(dve, s_cv, b * 12 + g + 1)
                tt(a, bank, cos_sb[:, cols], ALU.mult).then_inc(s_rot, 1)
                nc.vector.stream_shuffle(s, bank, swap).then_inc(s_rf, 1)
                wait(dve, s_rf, b * 8 + g + 1)
                tt(s, s, sin_sb[:, cols], ALU.mult).then_inc(s_rot, 1)
                wait(dve, s_rot, base + 2)
                tt(a, a, s, ALU.add).then_inc(s_rr, 1)
                wait(dve, s_rhi, b * 8 + g + 1)
                tt(src[:, 2 * kind + 1, c, cols].bitcast(f32r), a, src[:, 2 * kind, c, cols], ALU.subtract).then_inc(s_rlo, 1)
                nc.vector.memset(rl[0:1, 0:1], 0.0).then_inc(s_rot, 1)

            def out_lo(n, hf):
                for c in range(2):
                    wait(dve, s_ohi, n * 4 + 2 * hf + c + 1)
                    tt(ol[:, c, :], PV[c][:, :], f(oh[:, c, :]), ALU.subtract).then_inc(s_olo, 1)

            def gate(n, hf):
                cols = slice(hf * NB, (hf + 1) * NB)
                base = n * 6 + hf * 3
                wait(dve, s_eg, n * 2 + hf + 1)
                ts(eg[:, :], eg[:, :], 1.0, None, ALU.add).then_inc(s_gch, 1)
                wait(dve, s_gch, base + 1)
                nc.vector.reciprocal(eg[:, :], eg[:, :]).then_inc(s_gch, 1)
                wait(dve, s_gch, base + 2)
                stt(eg[:, :], MX[:, 0:NB], bo_sb[:, 0:1], eg[:, :], ALU.add, ALU.mult).then_inc(s_gch, 1)
                wait(dve, s_gch, base + 3)
                wait(dve, s_xg, n * 16 + 16)
                tt(xg[:, cols], xg[:, cols], eg[:, :], ALU.add).then_inc(s_gate, 1)

            def v_lo(b, g):
                c, hf = g // 2, g % 2
                at = (slice(None), slice(4 * hf, 4 * hf + 4), slice(c * P, (c + 1) * P))
                wait(dve, s_vhi, b * 4 + g + 1)
                tt(vl[at], PV[g % 2][:, :].rearrange("p (j o) -> p j o", o=P), f(vh[at]), ALU.subtract).then_inc(s_vlo, 1)

            def take_max(n, k, p):
                wait(dve, s_mx, 2 * n + p + 1)
                nc.vector.tensor_reduce(mcol[:, k % 2, p, MROW:MROW + 1], MX[:, :], AX, ALU.max).then_inc(s_red, 1)

            def exp_lo(n, k, p):
                wait(dve, s_ex, 2 * n + p + 1)
                at = (slice(None), k % 2, slice(4 * p, 4 * p + 4), slice(None))
                tt(El[at].rearrange("p a b -> p (a b)"), E32[:, p, :], f(Eh[at]).rearrange("p a b -> p (a b)"),
                   ALU.subtract).then_inc(s_lo, 1)

            def normalise(n, k, p, head):
                wait(dve, s_pv, 2 * n + p + 1)
                nc.vector.reciprocal(rl[:, p:p + 1], PV[p][:, INNER:INNER + 1]).then_inc(s_rl, 1)
                m = mix_sb[:, bass.ds(head * HEADS, HEADS)].rearrange("p (g a) -> p g a", a=1).to_broadcast([P, HEADS, DH])
                wait(dve, s_rl, 2 * n + p + 1)
                wait(dve, s_acc, 2 * n + p + 1)
                stt(tmp[:, p, :].rearrange("p (g d) -> p g d", d=DH), PV[p][:, 0:INNER].rearrange("p (g d) -> p g d", d=DH),
                    rl[:, p:p + 1], m, ALU.mult, ALU.mult).then_inc(s_nrm, 1)

            def pair(n0, h0, last=False, b=None):
                for k in range(2 * QC):
                    n, head = n0 + k, h0 + k // QC
                    for p in range(2):
                        if not (last and k >= 6):
                            take_max(n + 2, k + 2, p)
                        if last and k == 6 and p == 0:
                            centre(b + 1)
                        if last and k == 7 and p == 0:
                            var_eps(b + 1)
                        normalise(n, k, p, head)
                        if not (last and k == 7):
                            exp_lo(n + 1, k + 1, p)
                if last:
                    input_lo(b + 1)

            def batch(b):
                prev = None if isinstance(b, int) else b - 1
                n = b * UNITS
                for g in range(5):
                    rotate(b, g)
                if prev is not None:
                    out_lo(prev, 0)
                rotate(b, 5)
                if prev is not None:
                    gate(prev, 0)
                    out_lo(prev, 1)
                rotate(b, 6)
                if prev is not None:
                    gate(prev, 1)
                    wait(dve, s_tr, prev * 4 + 4)
                    nc.vector.memset(acc[:, :, :], 0.0)
                rotate(b, 7)
                take_max(n, 0, 0)
                v_lo(b, 0)
                take_max(n, 0, 1)
                v_lo(b, 1)
                v_lo(b, 2)
                take_max(n + 1, 1, 0)
                exp_lo(n, 0, 0)
                v_lo(b, 3)
                take_max(n + 1, 1, 1)
                exp_lo(n, 0, 1)
                with dve.Fori(0, HEADS // 2 - 1) as hp:
                    pair(n + hp * 8, hp * 2)
                pair(n + UNITS - 8, HEADS - 2, True, b)

            dve.wait_ge(s_tload, 16 * 5)
            centre(0)
            var_eps(0)
            input_lo(0)
            batch(0)
            with dve.Fori(1, B) as b:
                batch(b)
            for hf in range(2):
                out_lo(B - 1, hf)
                gate(B - 1, hf)

            dve.wait_ge(s_gate, 2 * B)
            dve.wait_ge(t_col, 1)
            nc.vector.tensor_copy(vec_col[:, :, :].rearrange("p a e -> p (a e)"), PV[0][:, 0:2 * EXP])
            nc.vector.tensor_copy(br_sb[:, :], PV[0][:, 64:64 + EXP])
            nc.vector.tensor_copy(rank_sb[:, :], PV[0][:, 80:80 + EXP])
            nc.vector.tensor_copy(b1_col[:, :], PV[0][:, 32:64]).then_inc(t_colv, 1)
            dve.wait_ge(t_lnb, 1)
            dve.wait_ge(t_colv, 1)
            tt(b1_col[:, :], PV[1][:, 0:EXP * HK], b1_col[:, :], ALU.add).then_inc(t_colv, 1)
            for e in range(EXP):
                last = ts(w1raw[:, e, :], w1raw[:, e, :], vec_col[:, 0, e:e + 1], None, ALU.mult)
            last.then_inc(t_scale, 1)
            dve.wait_ge(t_whi, 1)
            tt(w2l[:, :, :, :], w2raw, f(w2h[:, :, :, :]), ALU.subtract).then_inc(t_wlo, 1)
            dve.wait_ge(t_whi, 2)
            tt(w1l[:, :, :], w1raw[:, :, :], f(w1h[:, :, :]), ALU.subtract).then_inc(t_wlo, 1)

            def centre1(t, par):
                wait(dve, t_m1, t + 1)
                tt(fc[:, :], xm[par][:, :], PR, ALU.subtract).then_inc(t_c1, 1)

            def eps1(t):
                wait(dve, t_v1, t + 1)
                ts(fs[:, :], PR, 1e-5, None, ALU.add).then_inc(t_e1, 1)

            def norm1(t):
                wait(dve, t_r1, t + 1)
                tt(fa[:, :], fc[:, :], fs[:, :], ALU.mult).then_inc(t_a, 1)

            def centre2(t):
                wait(dve, t_m2, t + 1)
                wait(dve, t_a, t + 1)
                tt(fc[:, :], fa[:, :], PR, ALU.subtract).then_inc(t_c2, 1)

            def eps2(t):
                wait(dve, t_v2, t + 1)
                ts(fs[:, :], PR, 1e-5, None, ALU.add).then_inc(t_e2, 1)

            def norm2(t):
                wait(dve, t_r2, t + 1)
                tt(fc[:, :], fc[:, :], fs[:, :], ALU.mult).then_inc(t_xn, 1)

            def split2(t, par):
                wait(dve, t_xnh, t + 1)
                tt(xnl[par][:, :], fc[:, :], f(xnh[par][:, :]), ALU.subtract).then_inc(t_xnl, 1)

            def over(v):
                return v.rearrange("p (a o) -> p a o", o=1).to_broadcast([P, R4, EXP])

            rank_b = rank_sb[:, :].rearrange("p (o e) -> p o e", o=1).to_broadcast([P, R4, EXP])
            br_b = br_sb[:, :].rearrange("p (o e) -> p o e", o=1).to_broadcast([P, R4, EXP])
            all3 = (slice(None),) * 3

            class Links:
                def __init__(self, t):
                    self.t, self.n = t, 0

                def __call__(self, instruction):
                    self.n += 1
                    instruction.then_inc(t_rc, 1)
                    dve.wait_ge(t_rc, self.t * NLINK_R + self.n)

            def top2(t):
                link = Links(t)
                link(tt(lg[all3], LG.rearrange("p (a e) -> p a e", e=EXP), br_b, ALU.add))
                link(nc.vector.tensor_reduce(r_m[:, 0, :], lg[all3], AX, ALU.max))
                tt(r_d[all3], lg[all3], over(r_m[:, 0, :]), ALU.subtract).then_inc(t_d, 1)
                link(tt(r_c[all3], lg[all3], over(r_m[:, 0, :]), ALU.is_equal))
                link(tt(r_c[all3], r_c[all3], rank_b, ALU.mult))
                link(nc.vector.tensor_reduce(r_m[:, 1, :], r_c[all3], AX, ALU.max))
                link(tt(r_o1[all3], r_c[all3], over(r_m[:, 1, :]), ALU.is_equal))
                link(stt(r_l2[all3], r_o1[all3], -3.0e38, lg[all3], ALU.mult, ALU.add))
                link(nc.vector.tensor_reduce(r_m[:, 2, :], r_l2[all3], AX, ALU.max))
                link(tt(r_c[all3], r_l2[all3], over(r_m[:, 2, :]), ALU.is_equal))
                link(tt(r_c[all3], r_c[all3], rank_b, ALU.mult))
                link(nc.vector.tensor_reduce(r_m[:, 3, :], r_c[all3], AX, ALU.max))
                link(tt(r_o2[all3], r_c[all3], over(r_m[:, 3, :]), ALU.is_equal))
                assert link.n == NLINK_R

            t_wc = sem("t_wc")

            def weigh(t):
                tt(r_o1[all3], r_o1[all3], r_o2[all3], ALU.add).then_inc(t_wc, 1)
                wait(dve, t_ex, t + 1)
                dve.wait_ge(t_wc, t * 4 + 1)
                tt(r_e[all3], r_e[all3], r_o1[all3], ALU.mult).then_inc(t_wc, 1)
                dve.wait_ge(t_wc, t * 4 + 2)
                nc.vector.tensor_reduce(r_m[:, 4, :], r_e[all3], AX, ALU.add).then_inc(t_wc, 1)
                dve.wait_ge(t_wc, t * 4 + 3)
                nc.vector.reciprocal(r_m[:, 5, :], r_m[:, 4, :]).then_inc(t_wc, 1)
                dve.wait_ge(t_wc, t * 4 + 4)
                tt(r_w[all3], r_e[all3], over(r_m[:, 5, :]), ALU.mult).then_inc(t_w, 1)

            def route_lo(t, par):
                wait(dve, t_w32, (t + 1) * 2)
                tt(wst[par][LO:LO + EXP, :], PR[0:EXP, :], f(wst[par][0:EXP, :]), ALU.subtract).then_inc(t_whl, 1)

            def start_sum(it, par):
                wait(dve, t_b2, it * 2 + par + 1)
                wait(dve, t_out[par], it * 16 + 16)
                tt(ya[par][:, :], xm[par][:, :], PR, ALU.add).then_inc(t_yi, 1)

            def gelu_lo(s, e):
                i = e % 2
                pairs = [(t[:, i, 2 * j:2 * j + 2, :].rearrange("p a b -> p (a b)")) for j in range(2) for t in (hl, h32, hh)]
                wait(dve, t_hh, s + 1)
                tt(pairs[0], pairs[1], f(pairs[2]), ALU.subtract).then_inc(t_hl, 1)
                wait(dve, t_gl, 4 * s + 4)
                nc.vector.tensor_copy(pairs[5], pairs[4]).then_inc(t_hh1, 1)
                wait(dve, t_hh1, s + 1)
                tt(pairs[3], pairs[4], f(pairs[5]), ALU.subtract).then_inc(t_hl, 1)

            def weight_out(s, e):
                wait(dve, t_y, s + 1)
                wait(dve, t_wb, s + 1)
                wait(dve, t_ya, s + 1)
                tt(ty[e % 2][:, :], Y, wb[e % 2][:, :], ALU.mult).then_inc(t_yd, 1)

            def tile(it, par, more):
                t = it * 2 + par
                for e in range(EXP):
                    s = it * 16 + par * EXP + e
                    if more:
                        if e == 2:
                            norm1(t + 1)
                        if e == 4:
                            norm2(t + 1)
                            weigh(t + 1)
                    if e < EXP - 1 or more:
                        gelu_lo(s + 1, (e + 1) % EXP)
                    if more:
                        if e == 0:
                            centre1(t + 1, 1 - par)
                        if e == 1:
                            eps1(t + 1)
                        if e == 2:
                            centre2(t + 1)
                            top2(t + 1)
                        if e == 3:
                            eps2(t + 1)
                        if e == 4:
                            split2(t + 1, 1 - par)
                            route_lo(t + 1, 1 - par)
                        if e == 5:
                            start_sum(it + par, 1 - par)
                    weight_out(s, e)

            dve.wait_ge(t_cst, 6)
            centre1(0, 0)
            eps1(0)
            norm1(0)
            centre2(0)
            top2(0)
            eps2(0)
            norm2(0)
            weigh(0)
            split2(0, 0)
            route_lo(0, 0)
            start_sum(0, 0)
            nc.vector.memset(rl2 := ty[1][:, 0:1], 0.0).then_inc(t_yd, 1)
            gelu_lo(0, 0)
            with dve.Fori(0, B - 1) as it:
                tile(it, 0, True)
                tile(it, 1, True)
            tile(B - 1, 0, True)
            tile(B - 1, 1, False)


_INS = ["x", "L0_conv_wq", "L0_conv_wk", "L0_conv_wv", "L0_conv_mix", "L0_conv_wo", "L0_conv_bo",
        "L0_ffn_Wr", "L0_ffn_br", "L0_ffn_ln_g", "L0_ffn_ln_b", "L0_ffn_W1", "L0_ffn_b1", "L0_ffn_W2", "L0_ffn_b2"]


def position_tables():
    one = np.float32
    half = C // 2
    inv = (1.0 / np.power(one(10000.0), np.arange(0, half, 2, dtype=one) / one(half))).astype(one)
    seq = np.linspace(-1.0, 1.0, IMG, dtype=one)
    sinu = seq[None, :] * inv[:, None]
    part_w = np.broadcast_to(sinu[:, None, :], (C // 4, IMG, IMG))
    part_h = np.broadcast_to(sinu[:, :, None], (C // 4, IMG, IMG))
    s = np.concatenate([part_w, part_h], axis=0)
    pos2 = one(2.0) * np.concatenate([np.sin(s), np.cos(s)], axis=0).reshape(C, TOK)
    scales = np.logspace(0.0, np.log(5.0) / np.log(2.0), DH // 4, base=2.0).astype(one)
    fr = (seq[:, None] * scales[None, :] * one(np.pi)).astype(one)
    xs = np.broadcast_to(fr[:, None, :], (IMG, IMG, DH // 4))
    ys = np.broadcast_to(fr[None, :, :], (IMG, IMG, DH // 4))
    ang = np.concatenate([xs, ys], axis=-1).reshape(TOK, DH // 2)
    cos = np.repeat(np.cos(ang), 2, axis=-1).T
    sin = np.repeat(np.sin(ang), 2, axis=-1).T
    sign = np.where(np.arange(DH) % 2 == 0, -1.0, 1.0).astype(one)[:, None]
    rank = (EXP - np.arange(EXP)).astype(one)[None, :]
    return [np.ascontiguousarray(t, dtype=one) for t in (
        pos2, np.tile(cos, (P // DH, 1)), np.tile(sin * sign, (P // DH, 1)), rank)]


def kernel(**inputs):
    import concourse.bacc as _bacc
    from concourse import mybir as _mybir
    from concourse.bass_utils import run_bass_kernel_spmd as _run

    nc = _bacc.Bacc("TRN2", target_bir_lowering=False, num_devices=1)
    arrays, args = {}, []

    def give(name, a):
        arrays[name] = a
        args.append(nc.dram_tensor(name, a.shape, _mybir.dt.from_np(a.dtype), kind="ExternalInput").ap())

    for name in _INS:
        give(f"in_{name}_dram", np.ascontiguousarray(inputs[name]))
    for name, t in zip(("pos2", "rot_cos", "rot_sin", "rank"), position_tables()):
        give(f"table_{name}_dram", t)
    args.append(nc.dram_tensor("out_0_dram", (B, C, IMG, IMG), _mybir.dt.float32, kind="ExternalOutput").ap())
    build(nc, *args)
    r = _run(nc, [arrays], core_ids=[0])
    return r.results[0]["out_0_dram"]
```

```python
import numpy as np
import concourse.bass as bass
from concourse import mybir
from contextlib import ExitStack

B, C, IMG = 8, 128, 32
TOK = IMG * IMG
HEADS, DH = 8, 32
INNER = HEADS * DH
TAPS = 9
PAD = IMG + 2
EXP, HID = 8, 512
SCALE = DH ** -0.5
P = 128
NB = 512
QC = 4
QT = TOK // QC
KC = TOK // P
UNITS = HEADS * QC
MROW = 3 * DH
VW = INNER + 2
HK = HID // P
TILES = B * TOK // NB
LO = 32


def wait(eng, sem, count):
    if isinstance(count, int) and count <= 0:
        return
    eng.wait_ge(sem, count)


def build(nc, x, wq, wk, wv, mix, wo, bo, wr, br, ln_g, ln_b, w1, b1, w2, b2,
          pos2, rot_cos, rot_sin, rank, out):
    f32, f32r = mybir.dt.float32, mybir.dt.float32r
    ALU, ACT, AX = mybir.AluOpType, mybir.ActivationFunctionType, mybir.AxisListType.X

    x_d = x.rearrange("b c h w -> b c (h w)")
    out_d = out.rearrange("b c h w -> b c (h w)")
    mid_d = nc.dram_tensor("mid", (B, C, TOK), f32, kind="Internal").ap()

    def f(ap):
        return ap.bitcast(f32)

    def bc(ap, shape):
        return ap.to_broadcast(shape)

    ctx = ExitStack()
    with ctx:
        attn = ExitStack()

        def sem(name):
            return ctx.enter_context(nc.semaphore(name))

        def keep(name, shape, dt):
            return ctx.enter_context(nc.sbuf_tensor(name, shape, dt))

        def a_sb(name, shape, dt):
            return attn.enter_context(nc.sbuf_tensor(name, shape, dt))

        PV = [ctx.enter_context(nc.psum_tensor(f"PV{i}", [P, NB], f32)) for i in range(2)]
        ST = [ctx.enter_context(nc.psum_tensor(f"ST{i}", [P, 2 * NB], f32)) for i in range(2)]
        MX = ctx.enter_context(nc.psum_tensor("MX", [P, 2 * NB], f32))

        def conv_bank(g):
            return ST[g % 4 // 2][:, g % 2 * NB:(g % 2 + 1) * NB]

        ident = keep("ident", [P, P], f32)
        mean_w = keep("mean_w", [P, P], f32)
        mean_c = keep("mean_c", [P, 2], f32)
        ones_row = keep("ones_row", [1, P], f32)

        Eh = a_sb("Eh", [P, 2, KC, QT], f32r)
        El = a_sb("El", [P, 2, KC, QT], f32r)
        E32 = a_sb("E32", [P, 2, 4 * QT], f32)
        kst = [a_sb(f"kst{i}", [MROW + 1, TOK], f32r) for i in range(2)]
        qst = [a_sb(f"qst{i}", [MROW + 1, TOK], f32r) for i in range(2)]
        src = a_sb("src", [P, 4, 2, TOK], f32)
        xh = a_sb("xh", [P, PAD * PAD], f32r)
        xl = a_sb("xl", [P, PAD * PAD], f32r)
        wqh = a_sb("wqh", [P, INNER], f32r)
        wql = a_sb("wql", [P, INNER], f32r)
        wch = a_sb("wch", [P, 2, TAPS, INNER], f32r)
        wcl = a_sb("wcl", [P, 2, TAPS, INNER], f32r)
        woh = a_sb("woh", [P, 2, 2 * C], f32r)
        wol = a_sb("wol", [P, 2, 2 * C], f32r)
        vh = a_sb("vh", [P, KC, VW], f32r)
        vl = a_sb("vl", [P, KC, INNER], f32r)
        acc = a_sb("acc", [P, KC, INNER], f32)
        cos_sb = a_sb("cos_sb", [P, TOK], f32)
        sin_sb = a_sb("sin_sb", [P, TOK], f32)
        pos_sb = a_sb("pos_sb", [P, TOK], f32)
        xt = a_sb("xt", [P, TOK], f32)
        xg = a_sb("xg", [P, TOK], f32)
        mcol = a_sb("mcol", [P, 2, 2, P], f32r)
        negid = a_sb("negid", [P, P], f32r)
        tmp = a_sb("tmp", [P, 2, INNER], f32)
        rs = a_sb("rs", [P, 3, KC], f32)
        rl = a_sb("rl", [P, 2], f32)
        eg = a_sb("eg", [P, NB], f32)
        mix_row = a_sb("mix_row", [1, HEADS * HEADS], f32)
        mix_sb = a_sb("mix_sb", [P, HEADS * HEADS], f32)
        bo_sb = a_sb("bo_sb", [P, 2], f32)
        nbo = a_sb("nbo", [P, 1], f32)
        raw = src[:, :, :, :].rearrange("p a b c -> p (a b c)")
        RAWC = C * TAPS
        raw_c = [[raw[:, (2 * w + oc) * RAWC:(2 * w + oc + 1) * RAWC] for oc in range(2)] for w in range(2)]
        raw_q = [raw[:, 4 * RAWC + oc * C:4 * RAWC + (oc + 1) * C] for oc in range(2)]
        raw_o = [raw[:, 4 * RAWC + 2 * C + oc * INNER:4 * RAWC + 2 * C + (oc + 1) * INNER] for oc in range(2)]
        ln_x = src[:, 0, 0, :]
        ln_s = src[:, 1, 0, :]
        rot_a = [E32[:, i, 0:NB] for i in range(2)]
        rot_s = [E32[:, i, NB:2 * NB] for i in range(2)]
        vt = [a_sb(f"vt{i}", [P, NB], f32) for i in range(2)]
        oh = Eh[:, 1, 0:4, :].rearrange("p a b -> p (a b)").rearrange("p (c t) -> p c t", c=2)
        ol = El[:, 1, 0:4, :].rearrange("p a b -> p (a b)").rearrange("p (c t) -> p c t", c=2)

        attn_end = attn.pop_all()
        attn_end.close()

        w1h = keep("w1h", [P, EXP, HID], f32r)
        w1l = keep("w1l", [P, EXP, HID], f32r)
        w2h = keep("w2h", [P, EXP, HK, C], f32r)
        w2l = keep("w2l", [P, EXP, HK, C], f32r)
        w1raw = keep("w1raw", [P, EXP, HID], f32)
        h32 = keep("h32", [P, 2, HK, NB], f32)
        hh = keep("hh", [P, 2, HK, NB], f32r)
        hl = keep("hl", [P, 2, HK, NB], f32r)
        w2raw = h32[:, :, :, :].rearrange("p a b c -> p (a b c)").rearrange("p (e k d) -> p e k d", e=EXP, k=HK)
        xm = [keep(f"xm{i}", [P, NB], f32) for i in range(2)]
        fc = keep("fc", [P, NB], f32)
        fs = keep("fs", [P, NB], f32)
        frs = keep("frs", [P, 3, NB // P], f32)
        fa = keep("fa", [P, NB], f32)
        xnh = [keep(f"xnh{i}", [P, NB], f32r) for i in range(2)]
        xnl = [keep(f"xnl{i}", [P, NB], f32r) for i in range(2)]
        wb = [keep(f"wb{i}", [P, NB], f32) for i in range(2)]
        ty = [keep(f"ty{i}", [P, NB], f32) for i in range(2)]
        ya = [keep(f"ya{i}", [P, NB], f32) for i in range(2)]
        sel32 = keep("sel32", [LO + EXP, EXP, P], f32)
        sel = keep("sel", [LO + EXP, EXP, P], f32r)
        wst = [keep(f"wst{i}", [LO + EXP, NB], f32r) for i in range(2)]
        wt32 = keep("wt32", [EXP, NB], f32)
        b2_sb = keep("b2_sb", [EXP, C], f32)
        vec_row = keep("vec_row", [EXP, 2, C], f32)
        b1_row = keep("b1_row", [EXP * HK, P], f32)
        vec_col = keep("vec_col", [P, 2, EXP], f32)
        b1_col = keep("b1_col", [P, EXP * HK], f32)
        wr_sb = keep("wr_sb", [C, EXP], f32)
        br_row = keep("br_row", [1, EXP], f32)
        br_sb = keep("br_sb", [P, EXP], f32)
        rank_row = keep("rank_row", [1, EXP], f32)
        rank_sb = keep("rank_sb", [P, EXP], f32)
        e_const = keep("e_const", [P, 1], f32)
        R4 = NB // P
        lg = keep("lg", [P, R4, EXP], f32)
        r_c = keep("r_c", [P, R4, EXP], f32)
        r_o1 = keep("r_o1", [P, R4, EXP], f32)
        r_o2 = keep("r_o2", [P, R4, EXP], f32)
        r_l2 = keep("r_l2", [P, R4, EXP], f32)
        r_d = keep("r_d", [P, R4, EXP], f32)
        r_e = keep("r_e", [P, R4, EXP], f32)
        r_w = keep("r_w", [P, R4, EXP], f32)
        r_m = keep("r_m", [P, 6, R4], f32)

        H = [ST[k // 2][:, k % 2 * NB:(k % 2 + 1) * NB] for k in range(HK)]
        Y, WB = PV[0][:, :], PV[1][:, :]
        PR, LG, B2 = MX[:, 0:NB], MX[:, NB:NB + R4 * EXP], MX[:, NB:2 * NB]

        s_const = sem("s_const")
        s_ones = sem("s_ones")
        s_negid = sem("s_negid")
        s_wload = sem("s_wload")
        s_tload = sem("s_tload")
        s_wT = sem("s_wT")
        s_wThi = sem("s_wThi")
        s_wTlo = sem("s_wTlo")
        s_mixp = sem("s_mixp")
        s_mix = sem("s_mix")
        s_xt = sem("s_xt")
        s_mean = sem("s_mean")
        s_cent = sem("s_cent")
        s_sq = sem("s_sq")
        s_var = sem("s_var")
        s_rsq = sem("s_rsq")
        s_rstd = sem("s_rstd")
        s_rbc = sem("s_rbc")
        s_xn = sem("s_xn")
        s_xhi = sem("s_xhi")
        s_xin = sem("s_xin")
        s_cv = sem("s_cv")
        s_rot = sem("s_rot")
        s_rf = sem("s_rf")
        s_rr = sem("s_rr")
        s_rhi = sem("s_rhi")
        s_rlo = sem("s_rlo")
        s_stk = [sem(f"s_stk{i}") for i in range(2)]
        s_vt = sem("s_vt")
        s_vT = sem("s_vT")
        s_vhi = sem("s_vhi")
        s_vlo = sem("s_vlo")
        s_mx = sem("s_mx")
        s_red = sem("s_red")
        s_mt = sem("s_mt")
        s_mrow = sem("s_mrow")
        s_st = sem("s_st")
        s_ex = sem("s_ex")
        s_lo = sem("s_lo")
        s_pv = sem("s_pv")
        s_rl = sem("s_rl")
        s_nrm = sem("s_nrm")
        s_acc = sem("s_acc")
        s_tr = sem("s_tr")
        s_ohi = sem("s_ohi")
        s_olo = sem("s_olo")
        s_wo = sem("s_wo")
        s_eg = sem("s_eg")
        s_gch = sem("s_gch")
        s_gate = sem("s_gate")
        s_xg = sem("s_xg")
        s_mid = sem("s_mid")

        t_load = sem("t_load")
        t_vec = sem("t_vec")
        t_cst = sem("t_cst")
        t_sel = sem("t_sel")
        t_col = sem("t_col")
        t_colv = sem("t_colv")
        t_lnb = sem("t_lnb")
        t_scale = sem("t_scale")
        t_whi = sem("t_whi")
        t_wlo = sem("t_wlo")
        t_xm = [sem(f"t_xm{i}") for i in range(2)]
        t_m1, t_c1, t_q1, t_v1, t_r1, t_b1, t_a = (sem(n) for n in (
            "t_m1", "t_c1", "t_q1", "t_v1", "t_r1", "t_b1", "t_a"))
        t_m2, t_c2, t_q2, t_v2, t_r2, t_b2n, t_xn = (sem(n) for n in (
            "t_m2", "t_c2", "t_q2", "t_v2", "t_r2", "t_b2n", "t_xn"))
        t_rsq = sem("t_rsq")
        t_xnh, t_xnl = sem("t_xnh"), sem("t_xnl")
        t_rc = sem("t_rc")
        t_d = sem("t_d")
        t_ex = sem("t_ex")
        t_w = sem("t_w")
        t_wT = sem("t_wT")
        t_w32, t_whl = sem("t_w32"), sem("t_whl")
        t_b2 = sem("t_b2")
        t_yi = sem("t_yi")
        t_h = sem("t_h")
        t_gl = sem("t_gl")
        t_hh = sem("t_hh")
        t_hh1 = sem("t_hh1")
        t_hl = sem("t_hl")
        t_bc = sem("t_bc")
        t_wb = sem("t_wb")
        t_y = sem("t_y")
        t_yd = sem("t_yd")
        t_ya = sem("t_ya")
        t_out = [sem(f"t_out{i}") for i in range(2)]
        NLINK_R = 12

        def par_of(k):
            k %= 2 * QC
            return k // QC, k % QC, k % 2

        block = ctx.enter_context(nc.Block())

        @block.sync
        def _(sp):
            for w, d in enumerate((wk, wv)):
                for oc in range(2):
                    sp.dma_start(raw_c[w][oc], d.rearrange("o c y x -> o (c y x)")[oc * P:(oc + 1) * P, :]).then_inc(s_wload, 16)
            sp.dma_start(xt[:, :], x_d[0, :, :]).then_inc(s_xt, 16)
            for oc in range(2):
                sp.dma_start(raw_q[oc], wq.rearrange("o c y x -> o (c y x)")[oc * P:(oc + 1) * P, :]).then_inc(s_wload, 16)
                sp.dma_start(raw_o[oc], wo.rearrange("o c y x -> o (c y x)")[oc * P:(oc + 1) * P, :]).then_inc(s_wload, 16)
            sp.dma_start(pos_sb[:, :], pos2).then_inc(s_tload, 16)
            sp.dma_start(cos_sb[:, :], rot_cos).then_inc(s_tload, 16)
            sp.dma_start(sin_sb[:, :], rot_sin).then_inc(s_tload, 16)
            sp.dma_start(mix_row[:, :], mix.rearrange("h g -> (h g)").rearrange("(a n) -> a n", a=1)).then_inc(s_tload, 16)
            sp.dma_start(bo_sb[:, :], bo.rearrange("(a p) -> p a", p=P), allow_slow_non_contiguous=True).then_inc(s_tload, 16)

            def stacks(b, h):
                par, c, r = h % 2, h // 4, h % 4 * DH
                if h == 0:
                    wait(sp, s_rlo, b * 8 + 6)
                wait(sp, s_st, b * 64 + 8 * h - 8)
                for row, part in enumerate((2, 3, 2)):
                    sp.dma_start(f(kst[par][row * DH:(row + 1) * DH, :]), src[r:r + DH, part, c, :]).then_inc(s_stk[par], 16)
                for row, part in enumerate((0, 0, 1)):
                    sp.dma_start(f(qst[par][row * DH:(row + 1) * DH, :]), src[r:r + DH, part, c, :]).then_inc(s_stk[par], 16)

            def store_mid(b, done):
                for hf in range(2):
                    wait(sp, s_gate, done + hf)
                    sp.dma_start(mid_d[b, :, hf * NB:(hf + 1) * NB], xg[:, hf * NB:(hf + 1) * NB]).then_inc(s_mid, 16)

            def batch(b):
                nxt = 1 if isinstance(b, int) else (b + 1) % B
                ready = 1 if isinstance(b, int) else sp.snap(b + 1)
                x_next = x_d[nxt, :, :] if isinstance(b, int) else x_d[sp.snap(nxt), :, :]
                wait(sp, s_xin, ready)
                sp.dma_start(xt[:, :], x_next).then_inc(s_xt, 16)
                if not isinstance(b, int):
                    store_mid(b - 1, sp.snap(b * 2 - 1))
                    wait(sp, s_mid, sp.snap(b * 32))
                sp.dma_start(xg[:, :], x_d[b, :, :]).then_inc(s_xg, 16)
                for h in range(HEADS):
                    stacks(b, h)

            batch(0)
            with sp.Fori(1, B) as b:
                batch(b)
            store_mid(B - 1, 2 * B - 1)

            wait(sp, s_gate, 2 * B)
            sp.dma_start(vec_row[:, 0, :], ln_g).then_inc(t_vec, 16)
            sp.dma_start(vec_row[:, 1, :], ln_b).then_inc(t_vec, 16)
            sp.dma_start(b1_row[:, :], b1.rearrange("e (k p) -> (e k) p", p=P)).then_inc(t_vec, 16)
            sp.dma_start(b2_sb[:, :], b2).then_inc(t_vec, 16)
            sp.dma_start(wr_sb[:, :], wr).then_inc(t_vec, 16)
            sp.dma_start(br_row[:, :], br.rearrange("(a n) -> a n", a=1)).then_inc(t_vec, 16)
            sp.dma_start(rank_row[:, :], rank).then_inc(t_vec, 16)
            sp.dma_start(w1raw[:, :, :], w1.rearrange("e d h -> d e h")).then_inc(t_load, 16)
            sp.dma_start(w2raw, w2.rearrange("e (k p) d -> p e k d", p=P)).then_inc(t_load, 16)
            wait(sp, s_mid, 32 * B)

            def load_tile(it, par):
                sp.dma_start(xm[par][:, :], mid_d[it, :, par * NB:(par + 1) * NB]).then_inc(t_xm[par], 16)

            def store_tile(it, par, added):
                wait(sp, t_ya, added)
                sp.dma_start(out_d[it, :, par * NB:(par + 1) * NB], ya[par][:, :]).then_inc(t_out[par], 16)

            load_tile(0, 0)
            load_tile(0, 1)
            with sp.Fori(0, B - 1) as it:
                added = [sp.snap(it * 16 + 2 + EXP * (par + 1)) for par in range(2)]
                begun = [sp.snap(it * 2 + par + 1) for par in range(2)]
                for par in range(2):
                    store_tile(it, par, added[par])
                    wait(sp, t_yi, begun[par])
                    load_tile(it + 1, par)
            for par in range(2):
                store_tile(B - 1, par, (B - 1) * 16 + 2 + EXP * (par + 1))
            for par in range(2):
                sp.wait_ge(t_out[par], 16 + 16 * B)

        @block.gpsimd
        def _(pool):
            nc.gpsimd.memset(ident[:, :], 0.0).then_inc(s_const, 1)
            pool.wait_ge(s_const, 1)
            nc.gpsimd.affine_select(out=ident[:, :], in_=ident[:, :], compare_op=ALU.not_equal, fill=1.0,
                                    base=0, pattern=[[-1, P]], channel_multiplier=1).then_inc(s_const, 1)
            nc.gpsimd.memset(mean_w[:, :], 1.0 / C).then_inc(s_const, 1)
            nc.gpsimd.memset(mean_c[:, :], 1.0 / C).then_inc(s_const, 1)
            nc.gpsimd.memset(ones_row[:, :], 1.0).then_inc(s_const, 1)
            nc.gpsimd.memset(f(xh[:, :]), 0.0).then_inc(s_const, 1)
            nc.gpsimd.memset(f(xl[:, :]), 0.0).then_inc(s_const, 1)
            nc.gpsimd.memset(f(mcol[:, :, :, :]), 0.0).then_inc(s_const, 1)
            nc.gpsimd.memset(f(vh[:, :, INNER:VW]), 1.0).then_inc(s_const, 1)
            nc.gpsimd.memset(tmp[:, :, :], 0.0).then_inc(s_acc, 2)

            def add(n, k, p):
                ic = k % QC * 2 + p
                wait(pool, s_nrm, 2 * n + p + 3)
                wait(pool, s_acc, 2 * n + p + 2)
                nc.gpsimd.tensor_tensor(acc[:, ic, :], acc[:, ic, :], tmp[:, p, :], ALU.add).then_inc(s_acc, 1)

            def rotate(b, g):
                a, s = rot_a[g % 2], rot_s[g % 2]
                wait(pool, s_rf, b * 8 + g + 1)
                nc.gpsimd.tensor_tensor(s, s, sin_sb[:, g % 2 * NB:(g % 2 + 1) * NB], ALU.mult).then_inc(s_rot, 1)
                wait(pool, s_rot, b * 8 + g + 1)
                nc.gpsimd.tensor_tensor(a, a, s, ALU.add).then_inc(s_rr, 1)

            with pool.Fori(0, B) as b:
                for g in range(8):
                    rotate(b, g)
                with pool.Fori(0, HEADS // 2) as hp:
                    for k in range(2 * QC):
                        for p in range(2):
                            add(b * UNITS + hp * 8 + k, k, p)

            wait(pool, s_gate, 2 * B)
            nc.gpsimd.memset(sel32[:, :, :], 0.0).then_inc(t_cst, 1)
            pool.wait_ge(t_cst, 1)
            for i in range(2):
                nc.gpsimd.affine_select(out=sel32[:, :, :], in_=sel32[:, :, :], compare_op=ALU.not_equal, fill=1.0,
                                        base=-LO * i, pattern=[[-1, EXP], [0, P]], channel_multiplier=1).then_inc(t_cst, 1)
                pool.wait_ge(t_cst, 2 + i)
            nc.gpsimd.memset(e_const[:, :], float(np.e)).then_inc(t_cst, 1)
            for i in range(2):
                nc.gpsimd.memset(f(wst[i][:, :]), 0.0).then_inc(t_cst, 1)
            for i in range(2):
                nc.gpsimd.memset(ya[i][:, :], 0.0).then_inc(t_out[i], 16)
            nc.gpsimd.memset(ty[0][:, :], 0.0).then_inc(t_ya, 2)

            def square1(t):
                wait(pool, t_c1, t + 1)
                nc.gpsimd.tensor_tensor(fs[:, :], fc[:, :], fc[:, :], ALU.mult).then_inc(t_q1, 1)

            def square2(t):
                wait(pool, t_c2, t + 1)
                nc.gpsimd.tensor_tensor(fs[:, :], fc[:, :], fc[:, :], ALU.mult).then_inc(t_q2, 1)

            def exp_logits(t):
                wait(pool, t_d, t + 1)
                flat = r_d[:, :, :].rearrange("p a e -> p (a e)")
                nc.gpsimd.tensor_tensor(r_e[:, :, :].rearrange("p a e -> p (a e)"),
                                        e_const[:, 0:1].to_broadcast([P, R4 * EXP]), flat, ALU.pow).then_inc(t_ex, 1)

            def tile(it, par, more):
                t = it * 2 + par
                for e in range(EXP):
                    s = it * 16 + par * EXP + e
                    if more:
                        if e == 0:
                            square1(t + 1)
                        if e == 3:
                            square2(t + 1)
                            exp_logits(t + 1)
                    wait(pool, t_yd, s + 2)
                    wait(pool, t_ya, s + 2)
                    nc.gpsimd.tensor_tensor(ya[par][:, :], ya[par][:, :], ty[e % 2][:, :], ALU.add).then_inc(t_ya, 1)

            square1(0)
            square2(0)
            exp_logits(0)
            with pool.Fori(0, B - 1) as it:
                tile(it, 0, True)
                tile(it, 1, True)
            tile(B - 1, 0, True)
            tile(B - 1, 1, False)

        setup = []
        for w in range(2):
            for oc in range(2):
                for t3 in range(3):
                    cols = (slice(None), w, slice(3 * t3, 3 * t3 + 3), slice(oc * P, (oc + 1) * P))
                    srcs = [raw_c[w][oc].rearrange("o (c t) -> o t c", t=TAPS)[:, 3 * t3 + i, :] for i in range(3)]
                    setup.append((wch[cols], wcl[cols], srcs))
        setup.append((wqh[:, :].rearrange("p (a o) -> p a o", a=2), wql[:, :].rearrange("p (a o) -> p a o", a=2), raw_q))
        for kk in range(2):
            cols = (slice(None), kk, slice(None))
            setup.append((woh[cols].rearrange("p (a o) -> p a o", a=2), wol[cols].rearrange("p (a o) -> p a o", a=2),
                          [raw_o[oc][:, kk * P:(kk + 1) * P] for oc in range(2)]))
        SB = 4

        @block.tensor
        def _(pe):
            def mm(o, w, m, start, stop):
                return nc.tensor.matmul(o, w, m, start=start, stop=stop)

            def split3(o, wh, wl, mh, ml, start, stop):
                mm(o, wh, ml, start, False)
                mm(o, wl, mh, False, False)
                return mm(o, wh, mh, False, stop)

            pe.wait_ge(s_const, 9)
            pe.wait_ge(s_ones, 2)
            pe.wait_ge(s_wload, 16 * 8)
            for g, (_, _, srcs) in enumerate(setup):
                if g >= SB:
                    pe.wait_ge(s_wTlo, g - SB + 1)
                for i, s in enumerate(srcs):
                    last = nc.tensor.transpose(conv_bank(g)[:, i * P:(i + 1) * P], s, ident[:, :])
                last.then_inc(s_wT, 1)
            pe.wait_ge(s_tload, 16 * 5)
            mm(PV[0][:, 0:HEADS * HEADS], ones_row[:, :], mix_row[:, :], True, True).then_inc(s_mixp, 1)

            def prepare(n, k):
                if not isinstance(n, int) or n > 0:
                    if k < 6:
                        wait(pe, s_red, n * 2 * UNITS + 2 * k - 11)
                    else:
                        wait(pe, s_mrow, n * UNITS)
                if k == 2:
                    wait(pe, s_xt, (n + 1) * 16)
                if k == 3:
                    wait(pe, s_cent, n * 2 + 1)
                if k in (2, 3):
                    mm(MX[:, 0:NB], mean_w[:, :], xt[:, (k - 2) * NB:(k - 1) * NB], True, True).then_inc(s_mean, 1)
                if k == 4:
                    wait(pe, s_sq, n + 1)
                    for j in range(KC):
                        last = mm(MX[:, 2 * j:2 * j + 2], ln_s[:, j * P:(j + 1) * P], mean_c[:, :], True, True)
                    last.then_inc(s_var, 1)
                if k in (5, 6):
                    i = k - 5
                    if i == 0:
                        wait(pe, s_rstd, n + 1)
                    else:
                        wait(pe, s_xn, n * 3 + 1)
                    for j in range(KC // 2):
                        last = mm(MX[:, j * P:(j + 1) * P], rs[:, 1, 4 * i + j:4 * i + j + 1].to_broadcast([P, P]),
                                  ident[:, :], True, True)
                    last.then_inc(s_rbc, 1)

            def prepared(n, k):
                if k in (2, 3):
                    wait(pe, s_cent, n * 2 + k - 1)
                if k == 4:
                    wait(pe, s_rsq, n * 10 + 1)
                if k == 5:
                    wait(pe, s_xn, n * 3 + 1)

            img = [t[:, :].rearrange("p (y x) -> p y x", x=PAD) for t in (xh, xl)]

            def conv(b, g, taps=None):
                kind, c, hf = g // 4, g % 4 // 2, g % 2
                if g == 0:
                    wait(pe, s_xin, b + 1)
                if g >= 4 and (taps is None or taps[0] == 0):
                    wait(pe, s_rf, b * 8 + g - 3)
                o = conv_bank(g).rearrange("p (y x) -> p y x", x=IMG)
                every = [4] if kind == 0 else list(range(TAPS))
                for t in taps or every:
                    dy, dx = t // 3, t % 3
                    m = [i[:, hf * 16 + dy:hf * 16 + dy + 16, dx:dx + IMG] for i in img]
                    if kind == 0:
                        w = [s[:, c * P:(c + 1) * P] for s in (wqh, wql)]
                    else:
                        w = [s[:, kind - 1, t, c * P:(c + 1) * P] for s in (wch, wcl)]
                    last = split3(o, w[0], w[1], m[0], m[1], t == every[0], t == every[-1])
                if t == every[-1]:
                    last.then_inc(s_cv, 1)

            def out_transpose(n, hf):
                if hf == 0:
                    wait(pe, s_acc, (n + 1) * 2 * UNITS + 2)
                for c in range(2):
                    if hf == 1:
                        wait(pe, s_olo, n * 4 + c + 1)
                    for j in range(4):
                        last = nc.tensor.transpose(PV[c][:, j * P:(j + 1) * P],
                                                   acc[:, 4 * hf + j, c * P:(c + 1) * P], ident[:, :])
                    last.then_inc(s_tr, 1)

            def out_project(n, hf):
                wait(pe, s_olo, n * 4 + 2 * hf + 2)
                if hf == 1:
                    wait(pe, s_gate, n * 2 + 1)
                for o in range(2):
                    for c in range(2):
                        cols = slice(o * P, (o + 1) * P)
                        last = split3(MX[:, o * NB:(o + 1) * NB], woh[:, c, cols], wol[:, c, cols],
                                      oh[:, c, :], ol[:, c, :], c == 0, c == 1)
                last.then_inc(s_wo, 1)

            def v_transpose(b, g):
                wait(pe, s_vt, b * 4 + g + 1)
                if g >= 2:
                    wait(pe, s_vlo, b * 4 + g - 1)
                for j in range(4):
                    last = nc.tensor.transpose(PV[g % 2][:, j * P:(j + 1) * P], vt[g % 2][:, j * P:(j + 1) * P], ident[:, :])
                last.then_inc(s_vT, 1)

            def max_scores(n, k, p, head=None):
                st, q, _ = par_of(k)
                if p == 0:
                    wait(pe, s_mrow, n)
                    if q == 0:
                        wait(pe, s_stk[st], head)
                else:
                    wait(pe, s_red, 2 * n + 1)
                for i in range(2):
                    last = mm(MX[:, i * NB:(i + 1) * NB], qst[st][0:MROW, q * QT + p * P:q * QT + (p + 1) * P],
                              kst[st][0:MROW, i * NB:(i + 1) * NB], True, True)
                last.then_inc(s_mx, 1)

            def max_row(n, k):
                wait(pe, s_red, 2 * n + 2)
                for p in range(2):
                    last = mm(MX[:, p * P:(p + 1) * P], mcol[:, k % 2, p, :], negid[:, :], True, True)
                last.then_inc(s_mt, 1)

            def scores(n, k, p):
                st, q, _ = par_of(k)
                if p == 0:
                    wait(pe, s_mrow, n + 1)
                wait(pe, s_ex, 2 * n + p - 1)
                for j in range(4):
                    jc = 4 * p + j
                    last = mm(ST[p][:, j * QT:(j + 1) * QT], kst[st][:, jc * P:(jc + 1) * P],
                              qst[st][:, q * QT:(q + 1) * QT], True, True)
                last.then_inc(s_st, 1)

            def values(n, k, p, jcs):
                e = k % 2
                for jc in jcs:
                    if jc == 0:
                        wait(pe, s_nrm, 2 * n + p + 1)
                    if p == 0 and jc % 4 == 0:
                        wait(pe, s_lo, 2 * n + jc // 4 + 1)
                    hi, lo = (t[:, e, jc, p * P:(p + 1) * P] for t in (Eh, El))
                    mm(PV[p][:, 0:VW], lo, vh[:, jc, :], jc == 0, False)
                    mm(PV[p][:, 0:INNER], hi, vl[:, jc, :], False, False)
                    last = mm(PV[p][:, 0:VW], hi, vh[:, jc, :], False, jc == KC - 1)
                if KC - 1 in jcs:
                    last.then_inc(s_pv, 1)

            def pair(n0, stk_next, last=False, b=None):
                for k in range(2 * QC):
                    n = n0 + k
                    head = stk_next[(k + 2) // QC] if (k + 2) % QC == 0 else None
                    for p in range(2):
                        values(n, k, p, range(0, 2))
                        if p == 0 and not (last and k == 7):
                            max_row(n + 1, k + 1)
                        if last and p == 1:
                            if 2 <= k <= 6:
                                prepare(b + 1, k)
                        values(n, k, p, range(2, 4))
                        if not (last and k == 7):
                            scores(n + 1, k + 1, p)
                        if not (last and k >= 6):
                            if last and p == 1:
                                prepared(b + 1, k)
                            max_scores(n + 2, k + 2, p, head)
                        values(n, k, p, range(4, KC))

            def batch(b):
                prev = None if isinstance(b, int) else b - 1
                n = b * UNITS
                for g in range(5):
                    conv(b, g)
                if prev is not None:
                    out_transpose(prev, 0)
                conv(b, 5)
                if prev is not None:
                    out_project(prev, 0)
                    out_transpose(prev, 1)
                conv(b, 6)
                if prev is not None:
                    out_project(prev, 1)
                conv(b, 7)
                conv(b, 8)
                max_scores(n, 0, 0, b * 384 + 96)
                conv(b, 9)
                v_transpose(b, 0)
                max_scores(n, 0, 1)
                conv(b, 10)
                v_transpose(b, 1)
                max_row(n, 0)
                conv(b, 11, range(0, 5))
                max_scores(n + 1, 1, 0)
                scores(n, 0, 0)
                conv(b, 11, range(5, TAPS))
                v_transpose(b, 2)
                max_scores(n + 1, 1, 1)
                v_transpose(b, 3)
                wait(pe, s_vlo, b * 4 + 4)
                scores(n, 0, 1)
                with pe.Fori(0, HEADS // 2 - 1) as hp:
                    pair(n + hp * 8, [None, b * 384 + hp * 96 + 96, b * 384 + hp * 96 + 192])
                pair(n + UNITS - 8, [None, b * 384 + 384, None], True, b)

            pe.wait_ge(s_negid, 1)
            for k in range(2, 7):
                prepare(0, k)
            batch(0)
            with pe.Fori(1, B) as b:
                batch(b)
            for hf in range(2):
                out_transpose(B - 1, hf)
                out_project(B - 1, hf)

            pe.wait_ge(s_gate, 2 * B)
            pe.wait_ge(t_vec, 16 * 7)
            for i in range(2):
                nc.tensor.transpose(PV[0][:, i * EXP:(i + 1) * EXP], vec_row[:, i, :], ident[0:EXP, 0:EXP])
            nc.tensor.transpose(PV[0][:, 32:64], b1_row[:, :], ident[0:EXP * HK, 0:EXP * HK])
            mm(PV[0][:, 64:64 + EXP], ones_row[:, :], br_row[:, :], True, True)
            mm(PV[0][:, 80:80 + EXP], ones_row[:, :], rank_row[:, :], True, True).then_inc(t_col, 1)
            pe.wait_ge(t_load, 32)
            pe.wait_ge(t_colv, 1)
            for e in range(EXP):
                for k in range(HK):
                    c = e * HK + k
                    last = mm(PV[1][:, c:c + 1], w1raw[:, e, k * P:(k + 1) * P], vec_col[:, 1, e:e + 1], True, True)
            last.then_inc(t_lnb, 1)

            def mean1(it, par):
                wait(pe, t_xm[par], (it + 1) * 16)
                wait(pe, t_whl, it * 2 + par)
                mm(PR, mean_w[:, :], xm[par][:, :], True, True).then_inc(t_m1, 1)

            def token_mean(signal):
                for j in range(R4):
                    last = mm(PR[:, 2 * j:2 * j + 2], fs[:, j * P:(j + 1) * P], mean_c[:, :], True, True)
                last.then_inc(signal, 1)

            def token_spread(signal):
                for j in range(R4):
                    last = mm(PR[:, j * P:(j + 1) * P], frs[:, 1, j:j + 1].to_broadcast([P, P]), ident[:, :], True, True)
                last.then_inc(signal, 1)

            def var1(t):
                wait(pe, t_q1, t + 1)
                token_mean(t_v1)

            def spread1(t):
                wait(pe, t_r1, t + 1)
                token_spread(t_b1)

            def mean2(t):
                wait(pe, t_a, t + 1)
                wait(pe, t_yi, t)
                for j in range(R4):
                    mm(LG[:, j * EXP:(j + 1) * EXP], fa[:, j * P:(j + 1) * P], wr_sb[:, :], True, True)
                mm(PR, mean_w[:, :], fa[:, :], True, True).then_inc(t_m2, 1)

            def var2(t):
                wait(pe, t_q2, t + 1)
                token_mean(t_v2)

            def spread2(t):
                wait(pe, t_r2, t + 1)
                token_spread(t_b2n)

            def route_transpose(t):
                wait(pe, t_w, t + 1)
                wait(pe, t_xn, t + 1)
                for j in range(R4):
                    last = nc.tensor.transpose(PR[0:EXP, j * P:(j + 1) * P], r_w[:, j, :], ident[:, :])
                last.then_inc(t_wT, 1)

            def bias2(t):
                wait(pe, t_w32, (t + 1) * 2)
                mm(B2, b2_sb[:, :], wt32[:, :], True, True).then_inc(t_b2, 1)

            def hidden(s, e, par):
                for k in range(HK):
                    wait(pe, t_gl, 4 * s - 3 + k)
                    cols = slice(k * P, (k + 1) * P)
                    split3(H[k], w1h[:, e, cols], w1l[:, e, cols], xnh[par][:, :], xnl[par][:, :], True, True).then_inc(t_h, 1)

            def spread(t, s, e, par):
                wait(pe, t_wb, s)
                if e == 0:
                    wait(pe, t_whl, t + 1)
                mm(WB, sel[:, e, :], wst[par][:, :], True, True).then_inc(t_bc, 1)

            def project(s, e):
                i = e % 2
                wait(pe, t_yd, s + 1)
                for k in range(HK):
                    if k % 2 == 0:
                        wait(pe, t_hl, 2 * s + k // 2 + 1)
                    last = split3(Y, w2h[:, e, k, :], w2l[:, e, k, :], hh[:, i, k, :], hl[:, i, k, :], k == 0, k == HK - 1)
                last.then_inc(t_y, 1)

            def tile(it, par, more):
                t = it * 2 + par
                for e in range(EXP):
                    s = it * 16 + par * EXP + e
                    if e < EXP - 1 or more:
                        nx = par if e < EXP - 1 else 1 - par
                        if e == EXP - 1:
                            wait(pe, t_xnl, t + 2)
                        hidden(s + 1, (e + 1) % EXP, nx)
                        spread(t + (e + 1) // EXP, s + 1, (e + 1) % EXP, nx)
                    if more:
                        if e == 0:
                            mean1(it + par, 1 - par)
                        if e == 1:
                            var1(t + 1)
                        if e == 2:
                            spread1(t + 1)
                        if e == 3:
                            mean2(t + 1)
                        if e == 4:
                            var2(t + 1)
                        if e == 5:
                            spread2(t + 1)
                        if e == 6:
                            route_transpose(t + 1)
                        if e == 7:
                            bias2(t + 1)
                    project(s, e)

            pe.wait_ge(t_colv, 2)
            mean1(0, 0)
            var1(0)
            spread1(0)
            mean2(0)
            var2(0)
            spread2(0)
            route_transpose(0)
            bias2(0)
            pe.wait_ge(t_sel, 1)
            pe.wait_ge(t_wlo, 2)
            wait(pe, t_xnl, 1)
            hidden(0, 0, 0)
            spread(0, 0, 0, 0)
            with pe.Fori(0, B - 1) as it:
                tile(it, 0, True)
                tile(it, 1, True)
            tile(B - 1, 0, True)
            tile(B - 1, 1, False)

        @block.scalar
        def _(act):
            def copy(o, i, func=ACT.Copy, **kw):
                return nc.scalar.activation(o, i, func, **kw)

            act.wait_ge(s_const, 9)
            copy(negid[:, :], ident[:, :], scale=-1.0).then_inc(s_negid, 1)
            for g, (hi, _, srcs) in enumerate(setup):
                act.wait_ge(s_wT, g + 1)
                copy(hi, conv_bank(g)[:, 0:len(srcs) * P].rearrange("p (a o) -> p a o", o=P)).then_inc(s_wThi, 1)

            def square(n):
                wait(act, s_cent, 2 * n + 2)
                copy(ln_s, ln_x, ACT.Square).then_inc(s_sq, 1)

            def input_hi(n):
                wait(act, s_xn, 3 * n + 3)
                inner = xh[:, :].rearrange("p (y x) -> p y x", x=PAD)[:, 1:IMG + 1, 1:IMG + 1]
                copy(inner, ln_x.rearrange("p (y x) -> p y x", x=IMG)).then_inc(s_xhi, 1)

            def rot_hi(b, g):
                kind, c, hf = g // 4, g % 4 // 2, g % 2
                wait(act, s_rr, b * 8 + g + 1)
                copy(src[:, 2 * kind, c, hf * NB:(hf + 1) * NB].bitcast(f32r), rot_a[g % 2]).then_inc(s_rhi, 1)

            def out_hi(n, hf):
                for c in range(2):
                    wait(act, s_tr, n * 4 + 2 * hf + c + 1)
                    if hf == 1:
                        wait(act, s_wo, n * 2 + 1)
                    copy(oh[:, c, :], PV[c][:, :]).then_inc(s_ohi, 1)

            def gate_exp(n, hf):
                wait(act, s_wo, n * 2 + hf + 1)
                if hf == 1:
                    wait(act, s_gate, n * 2 + 1)
                copy(eg[:, :], MX[:, NB:2 * NB], ACT.Exp, bias=nbo[:, 0:1], scale=-1.0).then_inc(s_eg, 1)

            def v_copy(b, g):
                wait(act, s_cv, b * 12 + 8 + g + 1)
                if g >= 2:
                    wait(act, s_vT, b * 4 + g - 1)
                copy(vt[g % 2][:, :], conv_bank(g)).then_inc(s_vt, 1)

            def v_hi(b, g):
                c, hf = g // 2, g % 2
                wait(act, s_vT, b * 4 + g + 1)
                copy(vh[:, 4 * hf:4 * hf + 4, c * P:(c + 1) * P],
                     PV[g % 2][:, :].rearrange("p (j o) -> p j o", o=P)).then_inc(s_vhi, 1)

            def row_copy(n, k):
                st, q, _ = par_of(k)
                wait(act, s_mt, n + 1)
                copy(qst[st][MROW:MROW + 1, q * QT:(q + 1) * QT], MX[MROW:MROW + 1, 0:QT]).then_inc(s_mrow, 1)

            def exps(n, k, p):
                wait(act, s_st, 2 * n + p + 1)
                copy(Eh[:, k % 2, 4 * p:4 * p + 4, :].rearrange("p a b -> p (a b)"), ST[p][:, :], ACT.Exp, scale=SCALE)
                wait(act, s_lo, 2 * n + p - 1)
                copy(E32[:, p, :], ST[p][:, :], ACT.Exp, scale=SCALE).then_inc(s_ex, 1)

            def pair(n0, last=False, b=None):
                for k in range(2 * QC):
                    if not (last and k == 7):
                        row_copy(n0 + k + 1, k + 1)
                        for p in range(2):
                            exps(n0 + k + 1, k + 1, p)
                        if last and k == 3:
                            square(b + 1)
                    else:
                        input_hi(b + 1)

            def batch(b):
                prev = None if isinstance(b, int) else b - 1
                for g in range(5):
                    rot_hi(b, g)
                if prev is not None:
                    out_hi(prev, 0)
                rot_hi(b, 5)
                if prev is not None:
                    gate_exp(prev, 0)
                    out_hi(prev, 1)
                rot_hi(b, 6)
                if prev is not None:
                    gate_exp(prev, 1)
                rot_hi(b, 7)
                v_copy(b, 0)
                v_copy(b, 1)
                v_hi(b, 0)
                v_copy(b, 2)
                v_hi(b, 1)
                row_copy(b * UNITS, 0)
                exps(b * UNITS, 0, 0)
                v_copy(b, 3)
                v_hi(b, 2)
                v_hi(b, 3)
                exps(b * UNITS, 0, 1)
                with act.Fori(0, HEADS // 2 - 1) as hp:
                    pair(b * UNITS + hp * 8)
                pair(b * UNITS + UNITS - 8, True, b)

            act.wait_ge(s_mix, 2)
            square(0)
            input_hi(0)
            batch(0)
            with act.Fori(1, B) as b:
                batch(b)
            for hf in range(2):
                out_hi(B - 1, hf)
                gate_exp(B - 1, hf)

            act.wait_ge(s_gate, 2 * B)
            act.wait_ge(t_cst, 3)
            copy(sel[:, :, :], sel32[:, :, :]).then_inc(t_sel, 1)
            act.wait_ge(t_load, 32)
            copy(w2h[:, :, :, :], w2raw).then_inc(t_whi, 1)
            act.wait_ge(t_scale, 1)
            copy(w1h[:, :, :], w1raw[:, :, :]).then_inc(t_whi, 1)

            def input_hi2(t, par):
                wait(act, t_xn, t + 1)
                copy(xnh[par][:, :], fc[:, :]).then_inc(t_xnh, 1)

            def route_copy(t, par):
                wait(act, t_wT, t + 1)
                copy(wst[par][0:EXP, :], PR[0:EXP, :]).then_inc(t_w32, 1)
                copy(wt32[:, :], PR[0:EXP, :]).then_inc(t_w32, 1)

            def gelus(s, e):
                i = e % 2
                for k in range(HK):
                    wait(act, t_h, 4 * s + k + 1)
                    copy(h32[:, i, k, :], H[k], ACT.Gelu, bias=b1_col[:, e * HK + k:e * HK + k + 1]).then_inc(t_gl, 1)
                    if k == 2:
                        wait(act, t_gl, 4 * s + 2)
                        copy(hh[:, i, 0:2, :].rearrange("p a b -> p (a b)"),
                             h32[:, i, 0:2, :].rearrange("p a b -> p (a b)")).then_inc(t_hh, 1)

            def spread_copy(s, e):
                wait(act, t_bc, s + 1)
                wait(act, t_yd, s)
                copy(wb[e % 2][:, :], WB).then_inc(t_wb, 1)

            def tile(it, par, more):
                t = it * 2 + par
                for e in range(EXP):
                    s = it * 16 + par * EXP + e
                    if e < EXP - 1 or more:
                        gelus(s + 1, (e + 1) % EXP)
                        spread_copy(s + 1, (e + 1) % EXP)
                    if more and e == 5:
                        input_hi2(t + 1, 1 - par)
                    if more and e == 6:
                        route_copy(t + 1, 1 - par)

            input_hi2(0, 0)
            act.wait_ge(t_cst, 6)
            route_copy(0, 0)
            act.wait_ge(t_wlo, 2)
            gelus(0, 0)
            spread_copy(0, 0)
            with act.Fori(0, B - 1) as it:
                tile(it, 0, True)
                tile(it, 1, True)
            tile(B - 1, 0, True)
            tile(B - 1, 1, False)

        @block.vector
        def _(dve):
            tt, ts, stt = nc.vector.tensor_tensor, nc.vector.tensor_scalar, nc.vector.scalar_tensor_tensor

            for i in range(2):
                nc.vector.memset(f(kst[i][MROW:MROW + 1, :]), 1.0).then_inc(s_ones, 1)
            for g, (hi, lo, srcs) in enumerate(setup):
                dve.wait_ge(s_wThi, g + 1)
                tt(lo, conv_bank(g)[:, 0:len(srcs) * P].rearrange("p (a o) -> p a o", o=P), f(hi), ALU.subtract).then_inc(s_wTlo, 1)
            dve.wait_ge(s_mixp, 1)
            nc.vector.tensor_copy(mix_sb[:, :], PV[0][:, 0:HEADS * HEADS]).then_inc(s_mix, 1)
            ts(nbo[:, :], bo_sb[:, 1:2], -1.0, None, ALU.mult).then_inc(s_mix, 1)
            nc.vector.memset(acc[:, :, :], 0.0).then_inc(s_nrm, 2)

            def rsqrt(v, y, t, variance, eps, chain, base, done):
                i32 = mybir.dt.int32
                steps = [lambda: ts(v, variance, eps, None, ALU.add),
                         lambda: ts(y.bitcast(i32), v.bitcast(i32), -0.5, float(0x5f3759df), ALU.mult, ALU.add)]
                for _ in range(3):
                    steps += [lambda: stt(t, y, -0.5, y, ALU.mult, ALU.mult),
                              lambda: tt(t, t, v, ALU.mult),
                              lambda: stt(y, t, 1.5, y, ALU.add, ALU.mult)]
                for i, step in enumerate(steps[:-1]):
                    step().then_inc(chain, 1)
                    dve.wait_ge(chain, base + i + 1)
                steps[-1]().then_inc(done, 1)

            def prepare(n, k):
                half = slice((k - 2) % 3 * NB, ((k - 2) % 3 + 1) * NB)
                if k in (2, 3):
                    wait(dve, s_mean, n * 2 + k - 1)
                    tt(ln_x[:, half], xt[:, half], MX[:, 0:NB], ALU.subtract).then_inc(s_cent, 1)
                if k == 4:
                    wait(dve, s_var, n + 1)
                    rsqrt(rs[:, 0, :], rs[:, 1, :], rs[:, 2, :], MX[:, 0:2 * KC:2], 1e-6, s_rsq, n * 10, s_rstd)
                if k in (5, 6):
                    wait(dve, s_rbc, n * 2 + k - 4)
                    tt(ln_x[:, half], ln_x[:, half], MX[:, 0:NB], ALU.mult).then_inc(s_xn, 1)
                if k == 7:
                    wait(dve, s_xn, n * 3 + 2)
                    tt(ln_x, ln_x, pos_sb[:, :], ALU.add).then_inc(s_xn, 1)

            def input_lo(n):
                wait(dve, s_xhi, n + 1)
                hi, lo = (t[:, :].rearrange("p (y x) -> p y x", x=PAD)[:, 1:IMG + 1, 1:IMG + 1] for t in (xh, xl))
                tt(lo, ln_x.rearrange("p (y x) -> p y x", x=IMG), f(hi), ALU.subtract).then_inc(s_xin, 1)

            swap = [i ^ 1 for i in range(32)]

            def rotate(b, g):
                hf, bank = g % 2, conv_bank(g)
                wait(dve, s_cv, b * 12 + g + 1)
                if g >= 2:
                    wait(dve, s_rlo, b * 8 + g - 1)
                tt(rot_a[g % 2], bank, cos_sb[:, hf * NB:(hf + 1) * NB], ALU.mult)
                nc.vector.stream_shuffle(rot_s[g % 2], bank, swap).then_inc(s_rf, 1)

            def rot_lo(b, g):
                kind, c, hf = g // 4, g % 4 // 2, g % 2
                cols = slice(hf * NB, (hf + 1) * NB)
                wait(dve, s_rhi, b * 8 + g + 1)
                tt(src[:, 2 * kind + 1, c, cols].bitcast(f32r), rot_a[g % 2], src[:, 2 * kind, c, cols],
                   ALU.subtract).then_inc(s_rlo, 1)

            def out_lo(n, hf):
                for c in range(2):
                    wait(dve, s_ohi, n * 4 + 2 * hf + c + 1)
                    tt(ol[:, c, :], PV[c][:, :], f(oh[:, c, :]), ALU.subtract).then_inc(s_olo, 1)

            def gate(n, hf):
                cols = slice(hf * NB, (hf + 1) * NB)
                base = n * 6 + hf * 3
                wait(dve, s_eg, n * 2 + hf + 1)
                ts(eg[:, :], eg[:, :], 1.0, None, ALU.add).then_inc(s_gch, 1)
                wait(dve, s_gch, base + 1)
                nc.vector.reciprocal(eg[:, :], eg[:, :]).then_inc(s_gch, 1)
                wait(dve, s_gch, base + 2)
                stt(eg[:, :], MX[:, 0:NB], bo_sb[:, 0:1], eg[:, :], ALU.add, ALU.mult).then_inc(s_gch, 1)
                wait(dve, s_gch, base + 3)
                wait(dve, s_xg, n * 16 + 16)
                tt(xg[:, cols], xg[:, cols], eg[:, :], ALU.add).then_inc(s_gate, 1)

            def v_lo(b, g):
                c, hf = g // 2, g % 2
                at = (slice(None), slice(4 * hf, 4 * hf + 4), slice(c * P, (c + 1) * P))
                wait(dve, s_vhi, b * 4 + g + 1)
                tt(vl[at], PV[g % 2][:, :].rearrange("p (j o) -> p j o", o=P), f(vh[at]), ALU.subtract).then_inc(s_vlo, 1)

            def take_max(n, k, p):
                wait(dve, s_mx, 2 * n + p + 1)
                nc.vector.tensor_reduce(mcol[:, k % 2, p, MROW:MROW + 1], MX[:, :], AX, ALU.max).then_inc(s_red, 1)

            def exp_lo(n, k, p):
                wait(dve, s_ex, 2 * n + p + 1)
                at = (slice(None), k % 2, slice(4 * p, 4 * p + 4), slice(None))
                tt(El[at].rearrange("p a b -> p (a b)"), E32[:, p, :], f(Eh[at]).rearrange("p a b -> p (a b)"),
                   ALU.subtract).then_inc(s_lo, 1)

            def normalise(n, k, p, head):
                wait(dve, s_pv, 2 * n + p + 1)
                nc.vector.reciprocal(rl[:, p:p + 1], PV[p][:, INNER:INNER + 1]).then_inc(s_rl, 1)
                m = mix_sb[:, bass.ds(head * HEADS, HEADS)].rearrange("p (g a) -> p g a", a=1).to_broadcast([P, HEADS, DH])
                wait(dve, s_rl, 2 * n + p + 1)
                wait(dve, s_acc, 2 * n + p + 1)
                stt(tmp[:, p, :].rearrange("p (g d) -> p g d", d=DH), PV[p][:, 0:INNER].rearrange("p (g d) -> p g d", d=DH),
                    rl[:, p:p + 1], m, ALU.mult, ALU.mult).then_inc(s_nrm, 1)

            def pair(n0, h0, last=False, b=None):
                for k in range(2 * QC):
                    n, head = n0 + k, h0 + k // QC
                    for p in range(2):
                        if not (last and k >= 6):
                            take_max(n + 2, k + 2, p)
                        if last and k == 7:
                            if p == 0:
                                prepare(b + 1, 7)
                            else:
                                input_lo(b + 1)
                        normalise(n, k, p, head)
                        if not (last and k == 7):
                            exp_lo(n + 1, k + 1, p)
                        if last and 2 <= k <= 6 and p == 0:
                            prepare(b + 1, k)

            def batch(b):
                prev = None if isinstance(b, int) else b - 1
                n = b * UNITS
                rotate(b, 0)
                for g in range(1, 5):
                    rotate(b, g)
                    rot_lo(b, g - 1)
                if prev is not None:
                    out_lo(prev, 0)
                rotate(b, 5)
                rot_lo(b, 4)
                rot_lo(b, 5)
                if prev is not None:
                    gate(prev, 0)
                    out_lo(prev, 1)
                rotate(b, 6)
                rot_lo(b, 6)
                if prev is not None:
                    gate(prev, 1)
                    wait(dve, s_tr, prev * 4 + 4)
                    nc.vector.memset(acc[:, :, :], 0.0)
                rotate(b, 7)
                rot_lo(b, 7)
                take_max(n, 0, 0)
                v_lo(b, 0)
                take_max(n, 0, 1)
                v_lo(b, 1)
                take_max(n + 1, 1, 0)
                exp_lo(n, 0, 0)
                v_lo(b, 2)
                take_max(n + 1, 1, 1)
                v_lo(b, 3)
                exp_lo(n, 0, 1)
                with dve.Fori(0, HEADS // 2 - 1) as hp:
                    pair(n + hp * 8, hp * 2)
                pair(n + UNITS - 8, HEADS - 2, True, b)

            dve.wait_ge(s_tload, 16 * 5)
            for k in range(2, 8):
                prepare(0, k)
            input_lo(0)
            batch(0)
            with dve.Fori(1, B) as b:
                batch(b)
            for hf in range(2):
                out_lo(B - 1, hf)
                gate(B - 1, hf)

            dve.wait_ge(s_gate, 2 * B)
            dve.wait_ge(t_col, 1)
            nc.vector.tensor_copy(vec_col[:, :, :].rearrange("p a e -> p (a e)"), PV[0][:, 0:2 * EXP])
            nc.vector.tensor_copy(br_sb[:, :], PV[0][:, 64:64 + EXP])
            nc.vector.tensor_copy(rank_sb[:, :], PV[0][:, 80:80 + EXP])
            nc.vector.tensor_copy(b1_col[:, :], PV[0][:, 32:64]).then_inc(t_colv, 1)
            dve.wait_ge(t_lnb, 1)
            dve.wait_ge(t_colv, 1)
            tt(b1_col[:, :], PV[1][:, 0:EXP * HK], b1_col[:, :], ALU.add).then_inc(t_colv, 1)
            for e in range(EXP):
                last = ts(w1raw[:, e, :], w1raw[:, e, :], vec_col[:, 0, e:e + 1], None, ALU.mult)
            last.then_inc(t_scale, 1)
            dve.wait_ge(t_whi, 1)
            tt(w2l[:, :, :, :], w2raw, f(w2h[:, :, :, :]), ALU.subtract).then_inc(t_wlo, 1)
            dve.wait_ge(t_whi, 2)
            tt(w1l[:, :, :], w1raw[:, :, :], f(w1h[:, :, :]), ALU.subtract).then_inc(t_wlo, 1)

            def centre1(t, par):
                wait(dve, t_m1, t + 1)
                tt(fc[:, :], xm[par][:, :], PR, ALU.subtract).then_inc(t_c1, 1)

            def rstd1(t):
                wait(dve, t_v1, t + 1)
                rsqrt(frs[:, 0, :], frs[:, 1, :], frs[:, 2, :], PR[:, 0:2 * R4:2], 1e-5, t_rsq, t * 20, t_r1)

            def norm1(t):
                wait(dve, t_b1, t + 1)
                tt(fa[:, :], fc[:, :], PR, ALU.mult).then_inc(t_a, 1)

            def centre2(t):
                wait(dve, t_m2, t + 1)
                wait(dve, t_a, t + 1)
                tt(fc[:, :], fa[:, :], PR, ALU.subtract).then_inc(t_c2, 1)

            def rstd2(t):
                wait(dve, t_v2, t + 1)
                rsqrt(frs[:, 0, :], frs[:, 1, :], frs[:, 2, :], PR[:, 0:2 * R4:2], 1e-5, t_rsq, t * 20 + 10, t_r2)

            def norm2(t):
                wait(dve, t_b2n, t + 1)
                tt(fc[:, :], fc[:, :], PR, ALU.mult).then_inc(t_xn, 1)

            def split2(t, par):
                wait(dve, t_xnh, t + 1)
                tt(xnl[par][:, :], fc[:, :], f(xnh[par][:, :]), ALU.subtract).then_inc(t_xnl, 1)

            def over(v):
                return v.rearrange("p (a o) -> p a o", o=1).to_broadcast([P, R4, EXP])

            rank_b = rank_sb[:, :].rearrange("p (o e) -> p o e", o=1).to_broadcast([P, R4, EXP])
            br_b = br_sb[:, :].rearrange("p (o e) -> p o e", o=1).to_broadcast([P, R4, EXP])
            all3 = (slice(None),) * 3

            class Links:
                def __init__(self, t):
                    self.t, self.n = t, 0

                def __call__(self, instruction):
                    self.n += 1
                    instruction.then_inc(t_rc, 1)
                    dve.wait_ge(t_rc, self.t * NLINK_R + self.n)

            def top2(t):
                link = Links(t)
                link(tt(lg[all3], LG.rearrange("p (a e) -> p a e", e=EXP), br_b, ALU.add))
                link(nc.vector.tensor_reduce(r_m[:, 0, :], lg[all3], AX, ALU.max))
                tt(r_d[all3], lg[all3], over(r_m[:, 0, :]), ALU.subtract).then_inc(t_d, 1)
                link(tt(r_c[all3], lg[all3], over(r_m[:, 0, :]), ALU.is_equal))
                link(tt(r_c[all3], r_c[all3], rank_b, ALU.mult))
                link(nc.vector.tensor_reduce(r_m[:, 1, :], r_c[all3], AX, ALU.max))
                link(tt(r_o1[all3], r_c[all3], over(r_m[:, 1, :]), ALU.is_equal))
                link(stt(r_l2[all3], r_o1[all3], -3.0e38, lg[all3], ALU.mult, ALU.add))
                link(nc.vector.tensor_reduce(r_m[:, 2, :], r_l2[all3], AX, ALU.max))
                link(tt(r_c[all3], r_l2[all3], over(r_m[:, 2, :]), ALU.is_equal))
                link(tt(r_c[all3], r_c[all3], rank_b, ALU.mult))
                link(nc.vector.tensor_reduce(r_m[:, 3, :], r_c[all3], AX, ALU.max))
                link(tt(r_o2[all3], r_c[all3], over(r_m[:, 3, :]), ALU.is_equal))
                assert link.n == NLINK_R

            t_wc = sem("t_wc")

            def weigh(t):
                tt(r_o1[all3], r_o1[all3], r_o2[all3], ALU.add).then_inc(t_wc, 1)
                wait(dve, t_ex, t + 1)
                dve.wait_ge(t_wc, t * 4 + 1)
                tt(r_e[all3], r_e[all3], r_o1[all3], ALU.mult).then_inc(t_wc, 1)
                dve.wait_ge(t_wc, t * 4 + 2)
                nc.vector.tensor_reduce(r_m[:, 4, :], r_e[all3], AX, ALU.add).then_inc(t_wc, 1)
                dve.wait_ge(t_wc, t * 4 + 3)
                nc.vector.reciprocal(r_m[:, 5, :], r_m[:, 4, :]).then_inc(t_wc, 1)
                dve.wait_ge(t_wc, t * 4 + 4)
                tt(r_w[all3], r_e[all3], over(r_m[:, 5, :]), ALU.mult).then_inc(t_w, 1)

            def route_lo(t, par):
                wait(dve, t_w32, (t + 1) * 2)
                tt(wst[par][LO:LO + EXP, :], PR[0:EXP, :], f(wst[par][0:EXP, :]), ALU.subtract).then_inc(t_whl, 1)

            def start_sum(it, par):
                wait(dve, t_b2, it * 2 + par + 1)
                wait(dve, t_out[par], it * 16 + 16)
                tt(ya[par][:, :], xm[par][:, :], B2, ALU.add).then_inc(t_yi, 1)

            def gelu_lo(s, e):
                i = e % 2
                pairs = [(t[:, i, 2 * j:2 * j + 2, :].rearrange("p a b -> p (a b)")) for j in range(2) for t in (hl, h32, hh)]
                wait(dve, t_hh, s + 1)
                tt(pairs[0], pairs[1], f(pairs[2]), ALU.subtract).then_inc(t_hl, 1)
                wait(dve, t_gl, 4 * s + 4)
                nc.vector.tensor_copy(pairs[5], pairs[4]).then_inc(t_hh1, 1)
                wait(dve, t_hh1, s + 1)
                tt(pairs[3], pairs[4], f(pairs[5]), ALU.subtract).then_inc(t_hl, 1)

            def weight_out(s, e):
                wait(dve, t_y, s + 1)
                wait(dve, t_wb, s + 1)
                wait(dve, t_ya, s + 1)
                tt(ty[e % 2][:, :], Y, wb[e % 2][:, :], ALU.mult).then_inc(t_yd, 1)

            def tile(it, par, more):
                t = it * 2 + par
                for e in range(EXP):
                    s = it * 16 + par * EXP + e
                    if more and e == 6:
                        split2(t + 1, 1 - par)
                    if e < EXP - 1 or more:
                        gelu_lo(s + 1, (e + 1) % EXP)
                    if more:
                        if e == 0:
                            centre1(t + 1, 1 - par)
                        if e == 1:
                            rstd1(t + 1)
                        if e == 2:
                            norm1(t + 1)
                        if e == 3:
                            centre2(t + 1)
                            top2(t + 1)
                        if e == 4:
                            rstd2(t + 1)
                        if e == 5:
                            norm2(t + 1)
                            weigh(t + 1)
                        if e == 6:
                            route_lo(t + 1, 1 - par)
                        if e == 7:
                            start_sum(it + par, 1 - par)
                    weight_out(s, e)

            dve.wait_ge(t_cst, 6)
            centre1(0, 0)
            rstd1(0)
            norm1(0)
            centre2(0)
            top2(0)
            rstd2(0)
            norm2(0)
            weigh(0)
            split2(0, 0)
            route_lo(0, 0)
            start_sum(0, 0)
            nc.vector.memset(rl2 := ty[1][:, 0:1], 0.0).then_inc(t_yd, 1)
            gelu_lo(0, 0)
            with dve.Fori(0, B - 1) as it:
                tile(it, 0, True)
                tile(it, 1, True)
            tile(B - 1, 0, True)
            tile(B - 1, 1, False)


_INS = ["x", "L0_conv_wq", "L0_conv_wk", "L0_conv_wv", "L0_conv_mix", "L0_conv_wo", "L0_conv_bo",
        "L0_ffn_Wr", "L0_ffn_br", "L0_ffn_ln_g", "L0_ffn_ln_b", "L0_ffn_W1", "L0_ffn_b1", "L0_ffn_W2", "L0_ffn_b2"]


def position_tables():
    one = np.float32
    half = C // 2
    inv = (1.0 / np.power(one(10000.0), np.arange(0, half, 2, dtype=one) / one(half))).astype(one)
    seq = np.linspace(-1.0, 1.0, IMG, dtype=one)
    sinu = seq[None, :] * inv[:, None]
    part_w = np.broadcast_to(sinu[:, None, :], (C // 4, IMG, IMG))
    part_h = np.broadcast_to(sinu[:, :, None], (C // 4, IMG, IMG))
    s = np.concatenate([part_w, part_h], axis=0)
    pos2 = one(2.0) * np.concatenate([np.sin(s), np.cos(s)], axis=0).reshape(C, TOK)
    scales = np.logspace(0.0, np.log(5.0) / np.log(2.0), DH // 4, base=2.0).astype(one)
    fr = (seq[:, None] * scales[None, :] * one(np.pi)).astype(one)
    xs = np.broadcast_to(fr[:, None, :], (IMG, IMG, DH // 4))
    ys = np.broadcast_to(fr[None, :, :], (IMG, IMG, DH // 4))
    ang = np.concatenate([xs, ys], axis=-1).reshape(TOK, DH // 2)
    cos = np.repeat(np.cos(ang), 2, axis=-1).T
    sin = np.repeat(np.sin(ang), 2, axis=-1).T
    sign = np.where(np.arange(DH) % 2 == 0, -1.0, 1.0).astype(one)[:, None]
    rank = (EXP - np.arange(EXP)).astype(one)[None, :]
    return [np.ascontiguousarray(t, dtype=one) for t in (
        pos2, np.tile(cos, (P // DH, 1)), np.tile(sin * sign, (P // DH, 1)), rank)]


def kernel(**inputs):
    import concourse.bacc as _bacc
    from concourse import mybir as _mybir
    from concourse.bass_utils import run_bass_kernel_spmd as _run

    nc = _bacc.Bacc("TRN2", target_bir_lowering=False, num_devices=1)
    arrays, args = {}, []

    def give(name, a):
        arrays[name] = a
        args.append(nc.dram_tensor(name, a.shape, _mybir.dt.from_np(a.dtype), kind="ExternalInput").ap())

    for name in _INS:
        give(f"in_{name}_dram", np.ascontiguousarray(inputs[name]))
    for name, t in zip(("pos2", "rot_cos", "rot_sin", "rank"), position_tables()):
        give(f"table_{name}_dram", t)
    args.append(nc.dram_tensor("out_0_dram", (B, C, IMG, IMG), _mybir.dt.float32, kind="ExternalOutput").ap())
    build(nc, *args)
    r = _run(nc, [arrays], core_ids=[0])
    return r.results[0]["out_0_dram"]
```

```python
import numpy as np
import concourse.bass as bass
from concourse import mybir
from contextlib import ExitStack

B, C, IMG = 8, 128, 32
TOK = IMG * IMG
HEADS, DH = 8, 32
INNER = HEADS * DH
TAPS = 9
PAD = IMG + 2
EXP, HID = 8, 512
SCALE = DH ** -0.5
P = 128
NB = 512
QC = 4
QT = TOK // QC
KC = TOK // P
UNITS = HEADS * QC
MROW = 3 * DH
VW = INNER + 2
HK = HID // P
TILES = B * TOK // NB
LGW = EXP + 2
LO = 32


def wait(eng, sem, count):
    if isinstance(count, int) and count <= 0:
        return
    eng.wait_ge(sem, count)


def build(nc, x, wq, wk, wv, mix, wo, bo, wr, br, ln_g, ln_b, w1, b1, w2, b2,
          pos2, rot_cos, rot_sin, rank, out):
    f32, f32r = mybir.dt.float32, mybir.dt.float32r
    ALU, ACT, AX = mybir.AluOpType, mybir.ActivationFunctionType, mybir.AxisListType.X

    x_d = x.rearrange("b c h w -> b c (h w)")
    out_d = out.rearrange("b c h w -> b c (h w)")
    mid_d = nc.dram_tensor("mid", (B, C, TOK), f32, kind="Internal").ap()

    def f(ap):
        return ap.bitcast(f32)

    def bc(ap, shape):
        return ap.to_broadcast(shape)

    ctx = ExitStack()
    with ctx:
        attn = ExitStack()

        def sem(name):
            return ctx.enter_context(nc.semaphore(name))

        def keep(name, shape, dt):
            return ctx.enter_context(nc.sbuf_tensor(name, shape, dt))

        def a_sb(name, shape, dt):
            return attn.enter_context(nc.sbuf_tensor(name, shape, dt))

        PV = [ctx.enter_context(nc.psum_tensor(f"PV{i}", [P, NB], f32)) for i in range(2)]
        ST = [ctx.enter_context(nc.psum_tensor(f"ST{i}", [P, 2 * NB], f32)) for i in range(2)]
        MX = ctx.enter_context(nc.psum_tensor("MX", [P, 2 * NB], f32))

        def conv_bank(g):
            return ST[g % 4 // 2][:, g % 2 * NB:(g % 2 + 1) * NB]

        ident = keep("ident", [P, P], f32)
        mean_w = keep("mean_w", [P, P], f32)
        mean_c = keep("mean_c", [P, 2], f32)
        ones_row = keep("ones_row", [1, P], f32)
        vec_row = keep("vec_row", [EXP, 3, C], f32)
        b1_row = keep("b1_row", [EXP * HK, P], f32)
        wr_sb = keep("wr_sb", [C, LGW], f32)
        br_row = keep("br_row", [1, EXP], f32)
        rank_row = keep("rank_row", [1, EXP], f32)
        vec_col = keep("vec_col", [P, 3, EXP], f32)
        b1_col = keep("b1_col", [P, EXP * HK], f32)
        br_sb = keep("br_sb", [P, EXP], f32)
        rank_sb = keep("rank_sb", [P, EXP], f32)
        e_const = keep("e_const", [P, 1], f32)

        R4 = NB // P
        lg, r_c, r_o1, r_o2, r_l2, r_d, r_e, r_w = (keep(n, [P, R4, EXP], f32) for n in (
            "lg", "r_c", "r_o1", "r_o2", "r_l2", "r_d", "r_e", "r_w"))
        r_m = keep("r_m", [P, 6, R4], f32)

        wch = a_sb("wch", [P, 2, TAPS, INNER], f32r)
        wcl = a_sb("wcl", [P, 2, TAPS, INNER], f32r)
        kst = [a_sb(f"kst{i}", [MROW + 1, TOK], f32r) for i in range(2)]
        qst = [a_sb(f"qst{i}", [MROW + 1, TOK], f32r) for i in range(2)]
        src = a_sb("src", [P, 4, 2, TOK], f32)
        xh = a_sb("xh", [P, PAD * PAD], f32r)
        xl = a_sb("xl", [P, PAD * PAD], f32r)
        wqh = a_sb("wqh", [P, INNER], f32r)
        wql = a_sb("wql", [P, INNER], f32r)
        cos_sb = a_sb("cos_sb", [P, TOK], f32)
        sin_sb = a_sb("sin_sb", [P, TOK], f32)
        pos_sb = a_sb("pos_sb", [P, TOK], f32)
        xt = a_sb("xt", [P, TOK], f32)
        vh = a_sb("vh", [P, KC, VW], f32r)
        vl = a_sb("vl", [P, KC, INNER], f32r)
        Eh = a_sb("Eh", [P, 2, KC, QT], f32r)
        El = a_sb("El", [P, 2, KC, QT], f32r)
        E32 = a_sb("E32", [P, 2, 4 * QT], f32)
        woh = a_sb("woh", [P, 2, 2 * C], f32r)
        wol = a_sb("wol", [P, 2, 2 * C], f32r)
        acc = a_sb("acc", [P, KC, INNER], f32)
        xg = a_sb("xg", [P, TOK], f32)
        mcol = a_sb("mcol", [P, 2, 2, P], f32r)
        negid = a_sb("negid", [P, P], f32r)
        tmp = a_sb("tmp", [P, 2, INNER], f32)
        rs = a_sb("rs", [P, 3, KC], f32)
        rl = a_sb("rl", [P, 2], f32)
        eg = a_sb("eg", [P, NB], f32)
        mix_row = a_sb("mix_row", [1, HEADS * HEADS], f32)
        mix_sb = a_sb("mix_sb", [P, HEADS * HEADS], f32)
        bo_sb = a_sb("bo_sb", [P, 2], f32)
        nbo = a_sb("nbo", [P, 1], f32)
        raw = src[:, :, :, :].rearrange("p a b c -> p (a b c)")
        RAWC = C * TAPS
        raw_c = [[raw[:, (2 * w + oc) * RAWC:(2 * w + oc + 1) * RAWC] for oc in range(2)] for w in range(2)]
        raw_q = [raw[:, 4 * RAWC + oc * C:4 * RAWC + (oc + 1) * C] for oc in range(2)]
        raw_o = [raw[:, 4 * RAWC + 2 * C + oc * INNER:4 * RAWC + 2 * C + (oc + 1) * INNER] for oc in range(2)]
        def ln_x(n):
            return acc[:, 0:4, :].rearrange("p a b -> p (a b)") if isinstance(n, int) and n == 0 else src[:, 0, 0, :]

        def ln_s(n):
            return acc[:, 4:8, :].rearrange("p a b -> p (a b)") if isinstance(n, int) and n == 0 else src[:, 1, 0, :]

        rot_a = [E32[:, i, 0:NB] for i in range(2)]
        rot_s = [E32[:, i, NB:2 * NB] for i in range(2)]
        vt = [a_sb(f"vt{i}", [P, NB], f32) for i in range(2)]
        oh = Eh[:, 1, 0:4, :].rearrange("p a b -> p (a b)").rearrange("p (c t) -> p c t", c=2)
        ol = El[:, 1, 0:4, :].rearrange("p a b -> p (a b)").rearrange("p (c t) -> p c t", c=2)

        attn_end = attn.pop_all()
        attn_end.close()

        w1raw = keep("w1raw", [P, EXP, HID], f32)
        w2raw = keep("w2raw", [P, EXP, HK, C], f32)
        sel32 = keep("sel32", [LO + EXP, EXP, P], f32)
        w1h = keep("w1h", [P, EXP, HID], f32r)
        w1l = keep("w1l", [P, EXP, HID], f32r)
        w2h = keep("w2h", [P, EXP, HK, C], f32r)
        w2l = keep("w2l", [P, EXP, HK, C], f32r)
        xm = [keep(f"xm{i}", [P, NB], f32) for i in range(2)]
        fc = keep("fc", [P, NB], f32)
        fs = keep("fs", [P, NB], f32)
        frs = keep("frs", [P, 8, NB // P], f32)
        xnh = [keep(f"xnh{i}", [P, NB], f32r) for i in range(2)]
        xnl = [keep(f"xnl{i}", [P, NB], f32r) for i in range(2)]
        wst = [keep(f"wst{i}", [LO + EXP, NB], f32r) for i in range(2)]
        sel = keep("sel", [LO + EXP, EXP, P], f32r)
        wb = [keep(f"wb{i}", [P, NB], f32) for i in range(2)]
        ty = [keep(f"ty{i}", [P, NB], f32) for i in range(2)]
        ya = [keep(f"ya{i}", [P, NB], f32) for i in range(2)]
        h32 = keep("h32", [P, 2, HK, NB], f32)
        hh = keep("hh", [P, 2, HK, NB], f32r)
        hl = keep("hl", [P, 2, HK, NB], f32r)

        H = [ST[k // 2][:, k % 2 * NB:(k % 2 + 1) * NB] for k in range(HK)]
        Y, WB = PV[0][:, :], PV[1][:, :]

        def prep_banks(t):
            m = ST[0] if isinstance(t, int) and t == 0 else MX
            return m[:, 0:NB], m[:, NB:2 * NB]

        s_const = sem("s_const")
        s_ones = sem("s_ones")
        s_negid = sem("s_negid")
        s_wload = sem("s_wload")
        s_tload = sem("s_tload")
        s_wT = sem("s_wT")
        s_wThi = sem("s_wThi")
        s_wTlo = sem("s_wTlo")
        s_mixp = sem("s_mixp")
        s_mix = sem("s_mix")
        s_xt = sem("s_xt")
        s_mean = sem("s_mean")
        s_cent = sem("s_cent")
        s_sq = sem("s_sq")
        s_var = sem("s_var")
        s_rsq = sem("s_rsq")
        s_rstd = sem("s_rstd")
        s_rbc = sem("s_rbc")
        s_xn = sem("s_xn")
        s_xhi = sem("s_xhi")
        s_xin = sem("s_xin")
        s_cv = sem("s_cv")
        s_rot = sem("s_rot")
        s_rf = sem("s_rf")
        s_rr = sem("s_rr")
        s_rhi = sem("s_rhi")
        s_rlo = sem("s_rlo")
        s_stk = [sem(f"s_stk{i}") for i in range(2)]
        s_vt = sem("s_vt")
        s_vT = sem("s_vT")
        s_vhi = sem("s_vhi")
        s_vlo = sem("s_vlo")
        s_mx = sem("s_mx")
        s_red = sem("s_red")
        s_mt = sem("s_mt")
        s_mrow = sem("s_mrow")
        s_st = sem("s_st")
        s_ex = sem("s_ex")
        s_lo = sem("s_lo")
        s_pv = sem("s_pv")
        s_rl = sem("s_rl")
        s_nrm = sem("s_nrm")
        s_acc = sem("s_acc")
        s_tr = sem("s_tr")
        s_ohi = sem("s_ohi")
        s_olo = sem("s_olo")
        s_wo = sem("s_wo")
        s_eg = sem("s_eg")
        s_gch = sem("s_gch")
        s_gate = sem("s_gate")
        s_xg = sem("s_xg")
        s_mid = sem("s_mid")

        t_load = sem("t_load")
        t_vec = sem("t_vec")
        t_econ = sem("t_econ")
        t_sel32 = sem("t_sel32")
        t_cst = sem("t_cst")
        t_sel = sem("t_sel")
        t_col = sem("t_col")
        t_colv = sem("t_colv")
        t_lnb = sem("t_lnb")
        t_whi = sem("t_whi")
        t_wlo = sem("t_wlo")
        t_xm = [sem(f"t_xm{i}") for i in range(2)]
        t_mean = sem("t_mean")
        t_cent = sem("t_cent")
        t_sq = sem("t_sq")
        t_stat = sem("t_stat")
        t_link = sem("t_link")
        t_norm = sem("t_norm")
        t_fact = sem("t_fact")
        t_mul = sem("t_mul")
        t_xn = sem("t_xn")
        t_xnh, t_xnl = sem("t_xnh"), sem("t_xnl")
        t_rc = sem("t_rc")
        t_d = sem("t_d")
        t_ex = sem("t_ex")
        t_w = sem("t_w")
        t_wT = sem("t_wT")
        t_whh, t_whl = sem("t_whh"), sem("t_whl")
        t_h = sem("t_h")
        t_gl = sem("t_gl")
        t_hh = sem("t_hh")
        t_hh1 = sem("t_hh1")
        t_hl = sem("t_hl")
        t_bc = sem("t_bc")
        t_wb = sem("t_wb")
        t_y = sem("t_y")
        t_yd = sem("t_yd")
        t_ya = sem("t_ya")
        t_out = [sem(f"t_out{i}") for i in range(2)]
        NLINK_S = 28
        NLINK_R = 13

        def par_of(k):
            k %= 2 * QC
            return k // QC, k % QC, k % 2

        block = ctx.enter_context(nc.Block())

        @block.sync
        def _(sp):
            sp.dma_start(xt[:, :], x_d[0, :, :]).then_inc(s_xt, 16)
            for w, d in enumerate((wk, wv)):
                for oc in range(2):
                    sp.dma_start(raw_c[w][oc], d.rearrange("o c y x -> o (c y x)")[oc * P:(oc + 1) * P, :]).then_inc(s_wload, 16)
            for oc in range(2):
                sp.dma_start(raw_q[oc], wq.rearrange("o c y x -> o (c y x)")[oc * P:(oc + 1) * P, :]).then_inc(s_wload, 16)
                sp.dma_start(raw_o[oc], wo.rearrange("o c y x -> o (c y x)")[oc * P:(oc + 1) * P, :]).then_inc(s_wload, 16)
            sp.dma_start(pos_sb[:, :], pos2).then_inc(s_tload, 16)
            sp.dma_start(cos_sb[:, :], rot_cos).then_inc(s_tload, 16)
            sp.dma_start(sin_sb[:, :], rot_sin).then_inc(s_tload, 16)
            sp.dma_start(mix_row[:, :], mix.rearrange("h g -> (h g)").rearrange("(a n) -> a n", a=1)).then_inc(s_tload, 16)
            sp.dma_start(bo_sb[:, :], bo.rearrange("(a p) -> p a", p=P), allow_slow_non_contiguous=True).then_inc(s_tload, 16)
            sp.dma_start(vec_row[:, 0, :], ln_g).then_inc(t_vec, 16)
            sp.dma_start(vec_row[:, 1, :], ln_b).then_inc(t_vec, 16)
            sp.dma_start(b1_row[:, :], b1.rearrange("e (k p) -> (e k) p", p=P)).then_inc(t_vec, 16)
            sp.dma_start(vec_row[:, 2, :], b2).then_inc(t_vec, 16)
            sp.dma_start(wr_sb[:, 0:EXP], wr).then_inc(t_vec, 16)
            sp.dma_start(br_row[:, :], br.rearrange("(a n) -> a n", a=1)).then_inc(t_vec, 16)
            sp.dma_start(rank_row[:, :], rank).then_inc(t_vec, 16)

            def stacks(b, h):
                par, c, r = h % 2, h // 4, h % 4 * DH
                if h == 0:
                    wait(sp, s_rlo, b * 8 + 6)
                wait(sp, s_st, b * 64 + 8 * h - 8)
                for row, part in enumerate((2, 3, 2)):
                    sp.dma_start(f(kst[par][row * DH:(row + 1) * DH, :]), src[r:r + DH, part, c, :]).then_inc(s_stk[par], 16)
                for row, part in enumerate((0, 0, 1)):
                    sp.dma_start(f(qst[par][row * DH:(row + 1) * DH, :]), src[r:r + DH, part, c, :]).then_inc(s_stk[par], 16)

            def store_mid(b, done):
                for hf in range(2):
                    wait(sp, s_gate, done + hf)
                    sp.dma_start(mid_d[b, :, hf * NB:(hf + 1) * NB], xg[:, hf * NB:(hf + 1) * NB]).then_inc(s_mid, 16)

            def batch(b):
                nxt = 1 if isinstance(b, int) else (b + 1) % B
                ready = 1 if isinstance(b, int) else sp.snap(b + 1)
                x_next = x_d[nxt, :, :] if isinstance(b, int) else x_d[sp.snap(nxt), :, :]
                wait(sp, s_xin, ready)
                sp.dma_start(xt[:, :], x_next).then_inc(s_xt, 16)
                stacks(b, 0)
                if not isinstance(b, int):
                    store_mid(b - 1, sp.snap(b * 2 - 1))
                    wait(sp, s_mid, sp.snap(b * 32))
                sp.dma_start(xg[:, :], x_d[b, :, :]).then_inc(s_xg, 16)
                for h in range(1, HEADS):
                    stacks(b, h)

            batch(0)
            with sp.Fori(1, B) as b:
                batch(b)

            wait(sp, s_cv, 12 * B)
            sp.dma_start(w1raw[:, :, :], w1.rearrange("e d h -> d e h")).then_inc(t_load, 16)
            sp.dma_start(w2raw[:, :, :, :], w2.rearrange("e (k p) d -> p e k d", p=P)).then_inc(t_load, 16)

            def load_tile(it, par):
                sp.dma_start(xm[par][:, :], mid_d[it, :, par * NB:(par + 1) * NB]).then_inc(t_xm[par], 16)

            def store_tile(it, par, added):
                wait(sp, t_ya, added)
                sp.dma_start(out_d[it, :, par * NB:(par + 1) * NB], ya[par][:, :]).then_inc(t_out[par], 16)

            wait(sp, s_xin, B + 1)
            load_tile(0, 0)
            load_tile(0, 1)
            store_mid(B - 1, 2 * B - 1)
            wait(sp, s_mid, 32 * B)
            with sp.Fori(0, B - 1) as it:
                added = [sp.snap(it * 16 + 2 + EXP * (par + 1)) for par in range(2)]
                begun = [sp.snap(it * 16 + 2 + EXP * par + 1) for par in range(2)]
                for par in range(2):
                    wait(sp, t_ya, begun[par])
                    load_tile(it + 1, par)
                    store_tile(it, par, added[par])
            for par in range(2):
                store_tile(B - 1, par, (B - 1) * 16 + 2 + EXP * (par + 1))
            for par in range(2):
                sp.wait_ge(t_out[par], 16 + 16 * B)

        @block.gpsimd
        def _(pool):
            nc.gpsimd.memset(ident[:, :], 0.0).then_inc(s_const, 1)
            pool.wait_ge(s_const, 1)
            nc.gpsimd.affine_select(out=ident[:, :], in_=ident[:, :], compare_op=ALU.not_equal, fill=1.0,
                                    base=0, pattern=[[-1, P]], channel_multiplier=1).then_inc(s_const, 1)
            nc.gpsimd.memset(mean_w[:, :], 1.0 / C).then_inc(s_const, 1)
            nc.gpsimd.memset(mean_c[:, :], 1.0 / C).then_inc(s_const, 1)
            nc.gpsimd.memset(ones_row[:, :], 1.0).then_inc(s_const, 1)
            nc.gpsimd.memset(f(xh[:, :]), 0.0).then_inc(s_const, 1)
            nc.gpsimd.memset(f(xl[:, :]), 0.0).then_inc(s_const, 1)
            nc.gpsimd.memset(wr_sb[:, EXP:LGW], 1.0 / C).then_inc(s_const, 1)
            nc.gpsimd.memset(f(mcol[:, :, :, :]), 0.0).then_inc(s_const, 1)
            nc.gpsimd.memset(f(vh[:, :, INNER:VW]), 1.0).then_inc(s_const, 1)
            nc.gpsimd.memset(tmp[:, :, :], 0.0).then_inc(s_acc, 2)
            nc.gpsimd.memset(e_const[:, :], float(np.e)).then_inc(t_econ, 1)

            def add(n, k, p):
                ic = k % QC * 2 + p
                wait(pool, s_nrm, 2 * n + p + 3)
                wait(pool, s_acc, 2 * n + p + 2)
                nc.gpsimd.tensor_tensor(acc[:, ic, :], acc[:, ic, :], tmp[:, p, :], ALU.add).then_inc(s_acc, 1)

            def rotate(b, g):
                a, s = rot_a[g % 2], rot_s[g % 2]
                wait(pool, s_rf, b * 8 + g + 1)
                nc.gpsimd.tensor_tensor(s, s, sin_sb[:, g % 2 * NB:(g % 2 + 1) * NB], ALU.mult).then_inc(s_rot, 1)
                wait(pool, s_rot, b * 8 + g + 1)
                nc.gpsimd.tensor_tensor(a, a, s, ALU.add).then_inc(s_rr, 1)

            with pool.Fori(0, B) as b:
                for g in range(8):
                    rotate(b, g)
                with pool.Fori(0, HEADS // 2) as hp:
                    for k in range(2 * QC):
                        for p in range(2):
                            add(b * UNITS + hp * 8 + k, k, p)

            wait(pool, s_cv, 12 * B)
            nc.gpsimd.memset(sel32[:, :, :], 0.0).then_inc(t_sel32, 1)
            pool.wait_ge(t_sel32, 1)
            for i in range(2):
                nc.gpsimd.affine_select(out=sel32[:, :, :], in_=sel32[:, :, :], compare_op=ALU.not_equal, fill=1.0,
                                        base=-LO * i, pattern=[[-1, EXP], [0, P]], channel_multiplier=1).then_inc(t_sel32, 1)
                pool.wait_ge(t_sel32, 2 + i)

            def square(t):
                wait(pool, t_cent, t + 1)
                nc.gpsimd.tensor_tensor(fs[:, :], fc[:, :], fc[:, :], ALU.mult).then_inc(t_sq, 1)

            def exp_logits(t):
                wait(pool, t_d, t + 1)
                flat = r_d[:, :, :].rearrange("p a e -> p (a e)")
                nc.gpsimd.tensor_tensor(r_e[:, :, :].rearrange("p a e -> p (a e)"),
                                        e_const[:, 0:1].to_broadcast([P, R4 * EXP]), flat, ALU.pow).then_inc(t_ex, 1)

            def tile(it, par, more):
                t = it * 2 + par
                for e in range(EXP):
                    s = it * 16 + par * EXP + e
                    if more:
                        if e == 0:
                            square(t + 1)
                        if e == 4:
                            exp_logits(t + 1)
                    wait(pool, t_yd, s + 2)
                    wait(pool, t_ya, s + 2)
                    if e == 0:
                        wait(pool, t_out[par], it * 16 + 16)
                    base = xm[par] if e == 0 else ya[par]
                    nc.gpsimd.tensor_tensor(ya[par][:, :], base[:, :], ty[e % 2][:, :], ALU.add).then_inc(t_ya, 1)

            wait(pool, s_pv, 2 * UNITS * B)
            square(0)
            for i in range(2):
                nc.gpsimd.memset(f(wst[i][:, :]), 0.0).then_inc(t_cst, 1)
            pool.wait_ge(t_econ, 1)
            exp_logits(0)
            wait(pool, s_mid, 32 * B)
            for i in range(2):
                nc.gpsimd.memset(ya[i][:, :], 0.0).then_inc(t_out[i], 16)
            nc.gpsimd.memset(ty[0][:, :], 0.0).then_inc(t_ya, 2)
            with pool.Fori(0, B - 1) as it:
                tile(it, 0, True)
                tile(it, 1, True)
            tile(B - 1, 0, True)
            tile(B - 1, 1, False)

        setup = []
        for w in range(2):
            for oc in range(2):
                for t3 in range(3):
                    cols = (slice(None), w, slice(3 * t3, 3 * t3 + 3), slice(oc * P, (oc + 1) * P))
                    srcs = [raw_c[w][oc].rearrange("o (c t) -> o t c", t=TAPS)[:, 3 * t3 + i, :] for i in range(3)]
                    setup.append((wch[cols], wcl[cols], srcs))
        setup.append((wqh[:, :].rearrange("p (a o) -> p a o", a=2), wql[:, :].rearrange("p (a o) -> p a o", a=2), raw_q))
        for kk in range(2):
            cols = (slice(None), kk, slice(None))
            setup.append((woh[cols].rearrange("p (a o) -> p a o", a=2), wol[cols].rearrange("p (a o) -> p a o", a=2),
                          [raw_o[oc][:, kk * P:(kk + 1) * P] for oc in range(2)]))
        SB = 4

        @block.tensor
        def _(pe):
            def mm(o, w, m, start, stop):
                return nc.tensor.matmul(o, w, m, start=start, stop=stop)

            def split3(o, wh, wl, mh, ml, start, stop):
                mm(o, wh, ml, start, False)
                mm(o, wl, mh, False, False)
                return mm(o, wh, mh, False, stop)

            def weights(gs):
                for g in gs:
                    srcs = setup[g][2]
                    if g >= SB:
                        pe.wait_ge(s_wTlo, g - SB + 1)
                    for i, s in enumerate(srcs):
                        last = nc.tensor.transpose(conv_bank(g)[:, i * P:(i + 1) * P], s, ident[:, :])
                    last.then_inc(s_wT, 1)

            def prepare(n, k):
                if not isinstance(n, int) or n > 0:
                    if k < 6:
                        wait(pe, s_red, n * 2 * UNITS + 2 * k - 11)
                    else:
                        wait(pe, s_mrow, n * UNITS)
                if k == 2:
                    wait(pe, s_xt, (n + 1) * 16)
                if k == 3:
                    wait(pe, s_cent, n * 2 + 1)
                if k in (2, 3):
                    mm(MX[:, 0:NB], mean_w[:, :], xt[:, (k - 2) * NB:(k - 1) * NB], True, True).then_inc(s_mean, 1)
                if k == 4:
                    wait(pe, s_sq, n + 1)
                    for j in range(KC):
                        last = mm(MX[:, 2 * j:2 * j + 2], ln_s(n)[:, j * P:(j + 1) * P], mean_c[:, :], True, True)
                    last.then_inc(s_var, 1)
                if k in (5, 6):
                    i = k - 5
                    if i == 0:
                        wait(pe, s_rstd, n + 1)
                    else:
                        wait(pe, s_xn, n * 3 + 1)
                    for j in range(KC // 2):
                        last = mm(MX[:, j * P:(j + 1) * P], rs[:, 1, 4 * i + j:4 * i + j + 1].to_broadcast([P, P]),
                                  ident[:, :], True, True)
                    last.then_inc(s_rbc, 1)

            def prepared(n, k):
                if k in (2, 3):
                    wait(pe, s_cent, n * 2 + k - 1)
                if k == 4:
                    wait(pe, s_rsq, n * 10 + 1)
                if k == 5:
                    wait(pe, s_xn, n * 3 + 1)

            img = [t[:, :].rearrange("p (y x) -> p y x", x=PAD) for t in (xh, xl)]

            def conv(b, g, taps=None):
                kind, c, hf = g // 4, g % 4 // 2, g % 2
                if g == 0:
                    wait(pe, s_xin, b + 1)
                if g >= 4 and (taps is None or taps[0] == 0):
                    wait(pe, s_rf, b * 8 + g - 3)
                o = conv_bank(g).rearrange("p (y x) -> p y x", x=IMG)
                every = [4] if kind == 0 else list(range(TAPS))
                for t in taps or every:
                    dy, dx = t // 3, t % 3
                    m = [i[:, hf * 16 + dy:hf * 16 + dy + 16, dx:dx + IMG] for i in img]
                    if kind == 0:
                        w = [s[:, c * P:(c + 1) * P] for s in (wqh, wql)]
                    else:
                        w = [s[:, kind - 1, t, c * P:(c + 1) * P] for s in (wch, wcl)]
                    last = split3(o, w[0], w[1], m[0], m[1], t == every[0], t == every[-1])
                if t == every[-1]:
                    last.then_inc(s_cv, 1)

            def out_transpose(n, hf):
                if hf == 0:
                    wait(pe, s_acc, (n + 1) * 2 * UNITS + 2)
                for c in range(2):
                    if hf == 1:
                        wait(pe, s_olo, n * 4 + c + 1)
                    for j in range(4):
                        last = nc.tensor.transpose(PV[c][:, j * P:(j + 1) * P],
                                                   acc[:, 4 * hf + j, c * P:(c + 1) * P], ident[:, :])
                    last.then_inc(s_tr, 1)

            def out_project(n, hf):
                wait(pe, s_olo, n * 4 + 2 * hf + 2)
                if hf == 1:
                    wait(pe, s_gate, n * 2 + 1)
                for o in range(2):
                    for c in range(2):
                        cols = slice(o * P, (o + 1) * P)
                        last = split3(MX[:, o * NB:(o + 1) * NB], woh[:, c, cols], wol[:, c, cols],
                                      oh[:, c, :], ol[:, c, :], c == 0, c == 1)
                last.then_inc(s_wo, 1)

            def v_transpose(b, g):
                wait(pe, s_vt, b * 4 + g + 1)
                if g >= 2:
                    wait(pe, s_vlo, b * 4 + g - 1)
                for j in range(4):
                    last = nc.tensor.transpose(PV[g % 2][:, j * P:(j + 1) * P], vt[g % 2][:, j * P:(j + 1) * P], ident[:, :])
                last.then_inc(s_vT, 1)

            def max_scores(n, k, p, head=None):
                st, q, _ = par_of(k)
                if p == 0:
                    wait(pe, s_mrow, n)
                    if q == 0:
                        wait(pe, s_stk[st], head)
                else:
                    wait(pe, s_red, 2 * n + 1)
                for i in range(2):
                    last = mm(MX[:, i * NB:(i + 1) * NB], qst[st][0:MROW, q * QT + p * P:q * QT + (p + 1) * P],
                              kst[st][0:MROW, i * NB:(i + 1) * NB], True, True)
                last.then_inc(s_mx, 1)

            def max_row(n, k):
                wait(pe, s_red, 2 * n + 2)
                for p in range(2):
                    last = mm(MX[:, p * P:(p + 1) * P], mcol[:, k % 2, p, :], negid[:, :], True, True)
                last.then_inc(s_mt, 1)

            def scores(n, k, p):
                st, q, _ = par_of(k)
                if p == 0:
                    wait(pe, s_mrow, n + 1)
                wait(pe, s_ex, 2 * n + p - 1)
                for j in range(4):
                    jc = 4 * p + j
                    last = mm(ST[p][:, j * QT:(j + 1) * QT], kst[st][:, jc * P:(jc + 1) * P],
                              qst[st][:, q * QT:(q + 1) * QT], True, True)
                last.then_inc(s_st, 1)

            def values(n, k, p, jcs):
                e = k % 2
                for jc in jcs:
                    if jc == 0:
                        wait(pe, s_nrm, 2 * n + p + 1)
                    if p == 0 and jc % 4 == 0:
                        wait(pe, s_lo, 2 * n + jc // 4 + 1)
                    hi, lo = (t[:, e, jc, p * P:(p + 1) * P] for t in (Eh, El))
                    mm(PV[p][:, 0:VW], lo, vh[:, jc, :], jc == 0, False)
                    mm(PV[p][:, 0:INNER], hi, vl[:, jc, :], False, False)
                    last = mm(PV[p][:, 0:VW], hi, vh[:, jc, :], False, jc == KC - 1)
                if KC - 1 in jcs:
                    last.then_inc(s_pv, 1)

            def pair(n0, stk_next, last=False, b=None, split=None):
                if split is not None:
                    wait(pe, s_vlo, split)
                for k in range(2 * QC):
                    n = n0 + k
                    head = stk_next[(k + 2) // QC] if (k + 2) % QC == 0 else None
                    for p in range(2):
                        values(n, k, p, range(0, 2))
                        if p == 0 and not (last and k == 7):
                            max_row(n + 1, k + 1)
                        if last and p == 1:
                            if 2 <= k <= 6:
                                prepare(b + 1, k)
                        values(n, k, p, range(2, 4))
                        if not (last and k == 7):
                            scores(n + 1, k + 1, p)
                        if not (last and k >= 6):
                            if last and p == 1:
                                prepared(b + 1, k)
                            max_scores(n + 2, k + 2, p, head)
                        values(n, k, p, range(4, KC))

            def batch(b):
                prev = None if isinstance(b, int) else b - 1
                n = b * UNITS
                for g in range(4):
                    conv(b, g)
                if prev is not None:
                    out_transpose(prev, 0)
                conv(b, 4)
                if prev is not None:
                    out_project(prev, 0)
                    out_transpose(prev, 1)
                conv(b, 5)
                conv(b, 6)
                if prev is not None:
                    out_project(prev, 1)
                conv(b, 7)
                conv(b, 8)
                if prev is not None:
                    wait(pe, s_gate, b * 2)
                max_scores(n, 0, 0, b * 384 + 96)
                conv(b, 9)
                v_transpose(b, 0)
                max_scores(n, 0, 1)
                conv(b, 10)
                v_transpose(b, 1)
                max_row(n, 0)
                conv(b, 11, range(0, 5))
                max_scores(n + 1, 1, 0)
                scores(n, 0, 0)
                conv(b, 11, range(5, TAPS))
                v_transpose(b, 2)
                max_scores(n + 1, 1, 1)
                v_transpose(b, 3)
                scores(n, 0, 1)
                with pe.Fori(0, HEADS // 2 - 1) as hp:
                    pair(n + hp * 8, [None, b * 384 + hp * 96 + 96, b * 384 + hp * 96 + 192], split=b * 4 + 4)
                pair(n + UNITS - 8, [None, b * 384 + 384, None], True, b)

            pe.wait_ge(s_const, 10)
            pe.wait_ge(s_ones, 2)
            pe.wait_ge(s_negid, 1)
            prepare(0, 2)
            prepare(0, 3)
            prepare(0, 4)
            pe.wait_ge(s_wload, 16 * 8)
            weights(range(0, 3))
            prepare(0, 5)
            prepare(0, 6)
            weights(range(3, len(setup)))
            pe.wait_ge(s_tload, 16 * 5)
            mm(PV[0][:, 0:HEADS * HEADS], ones_row[:, :], mix_row[:, :], True, True).then_inc(s_mixp, 1)
            pe.wait_ge(t_vec, 16 * 7)
            for i in range(3):
                nc.tensor.transpose(PV[1][:, i * EXP:(i + 1) * EXP], vec_row[:, i, :], ident[0:EXP, 0:EXP])
            nc.tensor.transpose(PV[1][:, 32:64], b1_row[:, :], ident[0:EXP * HK, 0:EXP * HK])
            mm(PV[1][:, 64:64 + EXP], ones_row[:, :], br_row[:, :], True, True)
            mm(PV[1][:, 80:80 + EXP], ones_row[:, :], rank_row[:, :], True, True).then_inc(t_col, 1)
            pe.wait_ge(s_wTlo, len(setup))
            batch(0)
            with pe.Fori(1, B) as b:
                batch(b)

            def bias_through(experts):
                for e in experts:
                    for k in range(HK):
                        c = e * HK + k
                        last = mm(ST[1][:, c:c + 1], w1raw[:, e, k * P:(k + 1) * P], vec_col[:, 1, e:e + 1], True, True)
                last.then_inc(t_lnb, 1)

            def mean(it, par):
                wait(pe, t_xm[par], (it + 1) * 16)
                t = 0 if isinstance(it, int) and it + par == 0 else None
                wait(pe, t_whl, it * 2 + par)
                PR = prep_banks(t)[0]
                mm(PR, mean_w[:, :], xm[par][:, :], True, True).then_inc(t_mean, 1)

            def token_sums(t):
                wait(pe, t_sq, t + 1)
                PR, LG = prep_banks(t)
                for j in range(R4):
                    mm(PR[:, 2 * j:2 * j + 2], fs[:, j * P:(j + 1) * P], mean_c[:, :], True, True)
                for j in range(R4):
                    last = mm(LG[:, j * LGW:(j + 1) * LGW], fc[:, j * P:(j + 1) * P], wr_sb[:, :], True, True)
                last.then_inc(t_stat, 1)

            def token_factors(t):
                wait(pe, t_norm, t + 1)
                wait(pe, t_d, t + 1)
                for bank, i in zip(prep_banks(t), (6, 7)):
                    for j in range(R4):
                        last = mm(bank[:, j * P:(j + 1) * P], frs[:, i, j:j + 1].to_broadcast([P, P]), ident[:, :], True, True)
                last.then_inc(t_fact, 1)

            def route_transpose(t):
                wait(pe, t_w, t + 1)
                wait(pe, t_xn, t + 1)
                PR = prep_banks(t)[0]
                for j in range(R4):
                    last = nc.tensor.transpose(PR[0:EXP, j * P:(j + 1) * P], r_w[:, j, :], ident[:, :])
                last.then_inc(t_wT, 1)

            def hidden(s, e, par):
                for k in range(HK):
                    wait(pe, t_gl, 4 * s - 3 + k)
                    cols = slice(k * P, (k + 1) * P)
                    split3(H[k], w1h[:, e, cols], w1l[:, e, cols], xnh[par][:, :], xnl[par][:, :], True, True).then_inc(t_h, 1)

            def spread(t, s, e, par):
                wait(pe, t_wb, s)
                if e == 0:
                    wait(pe, t_whl, t + 1)
                mm(WB, sel[:, e, :], wst[par][:, :], True, True).then_inc(t_bc, 1)

            def project(s, e):
                i = e % 2
                wait(pe, t_yd, s + 1)
                for k in range(HK):
                    if k % 2 == 0:
                        wait(pe, t_hl, 2 * s + k // 2 + 1)
                    last = split3(Y, w2h[:, e, k, :], w2l[:, e, k, :], hh[:, i, k, :], hl[:, i, k, :], k == 0, k == HK - 1)
                last.then_inc(t_y, 1)

            def tile(it, par, more):
                t = it * 2 + par
                for e in range(EXP):
                    s = it * 16 + par * EXP + e
                    if e < EXP - 1 or more:
                        nx = par if e < EXP - 1 else 1 - par
                        if e == EXP - 1:
                            wait(pe, t_xnl, t + 2)
                        if e == 1:
                            wait(pe, t_wlo, 2 * EXP)
                        hidden(s + 1, (e + 1) % EXP, nx)
                        spread(t + (e + 1) // EXP, s + 1, (e + 1) % EXP, nx)
                    if more:
                        if e == 0:
                            mean(it + par, 1 - par)
                        if e == 1:
                            token_sums(t + 1)
                        if e == 5:
                            token_factors(t + 1)
                        if e == 6:
                            route_transpose(t + 1)
                    project(s, e)

            out_transpose(B - 1, 0)
            mean(0, 0)
            pe.wait_ge(t_colv, 1)
            pe.wait_ge(t_load, 32)
            bias_through(range(0, 2))
            out_project(B - 1, 0)
            out_transpose(B - 1, 1)
            token_sums(0)
            bias_through(range(2, 5))
            out_project(B - 1, 1)
            bias_through(range(5, EXP))
            token_factors(0)
            route_transpose(0)
            pe.wait_ge(t_sel, 1)
            pe.wait_ge(t_wlo, 2 * 2)
            pe.wait_ge(t_colv, 2)
            pe.wait_ge(t_xnl, 1)
            pe.wait_ge(t_d, 1)
            pe.wait_ge(t_whl, 1)
            pe.wait_ge(s_gate, 2 * B)
            hidden(0, 0, 0)
            spread(0, 0, 0, 0)
            with pe.Fori(0, B - 1) as it:
                tile(it, 0, True)
                tile(it, 1, True)
            tile(B - 1, 0, True)
            tile(B - 1, 1, False)

        @block.scalar
        def _(act):
            def copy(o, i, func=ACT.Copy, **kw):
                return nc.scalar.activation(o, i, func, **kw)

            act.wait_ge(s_const, 10)
            copy(negid[:, :], ident[:, :], scale=-1.0).then_inc(s_negid, 1)

            def weights(gs):
                for g in gs:
                    hi, _, srcs = setup[g]
                    act.wait_ge(s_wT, g + 1)
                    copy(hi, conv_bank(g)[:, 0:len(srcs) * P].rearrange("p (a o) -> p a o", o=P)).then_inc(s_wThi, 1)

            def square(n):
                wait(act, s_cent, 2 * n + 2)
                copy(ln_s(n), ln_x(n), ACT.Square).then_inc(s_sq, 1)

            def input_hi(n):
                wait(act, s_xn, 3 * n + 3)
                inner = xh[:, :].rearrange("p (y x) -> p y x", x=PAD)[:, 1:IMG + 1, 1:IMG + 1]
                copy(inner, ln_x(n).rearrange("p (y x) -> p y x", x=IMG)).then_inc(s_xhi, 1)

            def rot_hi(b, g):
                kind, c, hf = g // 4, g % 4 // 2, g % 2
                wait(act, s_rr, b * 8 + g + 1)
                copy(src[:, 2 * kind, c, hf * NB:(hf + 1) * NB].bitcast(f32r), rot_a[g % 2]).then_inc(s_rhi, 1)

            def out_hi(n, hf):
                for c in range(2):
                    wait(act, s_tr, n * 4 + 2 * hf + c + 1)
                    if hf == 1:
                        wait(act, s_wo, n * 2 + 1)
                    copy(oh[:, c, :], PV[c][:, :]).then_inc(s_ohi, 1)

            def gate_exp(n, hf):
                wait(act, s_wo, n * 2 + hf + 1)
                if hf == 1:
                    wait(act, s_gate, n * 2 + 1)
                copy(eg[:, :], MX[:, NB:2 * NB], ACT.Exp, bias=nbo[:, 0:1], scale=-1.0).then_inc(s_eg, 1)

            def v_copy(b, g):
                wait(act, s_cv, b * 12 + 8 + g + 1)
                if g >= 2:
                    wait(act, s_vT, b * 4 + g - 1)
                copy(vt[g % 2][:, :], conv_bank(g)).then_inc(s_vt, 1)

            def v_hi(b, g):
                c, hf = g // 2, g % 2
                wait(act, s_vT, b * 4 + g + 1)
                copy(vh[:, 4 * hf:4 * hf + 4, c * P:(c + 1) * P],
                     PV[g % 2][:, :].rearrange("p (j o) -> p j o", o=P)).then_inc(s_vhi, 1)

            def row_copy(n, k):
                st, q, _ = par_of(k)
                wait(act, s_mt, n + 1)
                copy(qst[st][MROW:MROW + 1, q * QT:(q + 1) * QT], MX[MROW:MROW + 1, 0:QT]).then_inc(s_mrow, 1)

            def exps(n, k, p):
                wait(act, s_st, 2 * n + p + 1)
                copy(Eh[:, k % 2, 4 * p:4 * p + 4, :].rearrange("p a b -> p (a b)"), ST[p][:, :], ACT.Exp, scale=SCALE)
                wait(act, s_lo, 2 * n + p - 1)
                copy(E32[:, p, :], ST[p][:, :], ACT.Exp, scale=SCALE).then_inc(s_ex, 1)

            def pair(n0, last=False, b=None):
                for k in range(2 * QC):
                    if not (last and k == 7):
                        row_copy(n0 + k + 1, k + 1)
                        for p in range(2):
                            exps(n0 + k + 1, k + 1, p)
                        if last and k == 3:
                            square(b + 1)
                    else:
                        input_hi(b + 1)

            def batch(b):
                prev = None if isinstance(b, int) else b - 1
                rot_hi(b, 0)
                if prev is not None:
                    out_hi(prev, 0)
                for g in range(1, 4):
                    rot_hi(b, g)
                if prev is not None:
                    gate_exp(prev, 0)
                    out_hi(prev, 1)
                rot_hi(b, 4)
                rot_hi(b, 5)
                if prev is not None:
                    gate_exp(prev, 1)
                rot_hi(b, 6)
                rot_hi(b, 7)
                v_copy(b, 0)
                v_copy(b, 1)
                v_hi(b, 0)
                v_copy(b, 2)
                v_hi(b, 1)
                row_copy(b * UNITS, 0)
                exps(b * UNITS, 0, 0)
                v_copy(b, 3)
                v_hi(b, 2)
                v_hi(b, 3)
                exps(b * UNITS, 0, 1)
                with act.Fori(0, HEADS // 2 - 1) as hp:
                    pair(b * UNITS + hp * 8)
                pair(b * UNITS + UNITS - 8, True, b)

            square(0)
            weights(range(0, 6))
            input_hi(0)
            weights(range(6, len(setup)))
            act.wait_ge(s_mix, 2)
            act.wait_ge(t_colv, 1)
            batch(0)
            with act.Fori(1, B) as b:
                batch(b)

            def weights_hi(experts):
                for e in experts:
                    copy(w1h[:, e, :], w1raw[:, e, :], scale=vec_col[:, 0, e:e + 1]).then_inc(t_whi, 1)
                    copy(w2h[:, e, :, :].rearrange("p k d -> p (k d)"),
                         w2raw[:, e, :, :].rearrange("p k d -> p (k d)")).then_inc(t_whi, 1)

            def input_hi2(t, par):
                wait(act, t_xn, t + 1)
                copy(xnh[par][:, :], fc[:, :]).then_inc(t_xnh, 1)

            def route_copy(t, par):
                wait(act, t_wT, t + 1)
                PR = prep_banks(t)[0]
                copy(wst[par][0:EXP, :], PR[0:EXP, :]).then_inc(t_whh, 1)

            def gelus(s, e):
                i = e % 2
                for k in range(HK):
                    wait(act, t_h, 4 * s + k + 1)
                    copy(h32[:, i, k, :], H[k], ACT.Gelu, bias=b1_col[:, e * HK + k:e * HK + k + 1]).then_inc(t_gl, 1)
                    if k == 2:
                        wait(act, t_gl, 4 * s + 2)
                        copy(hh[:, i, 0:2, :].rearrange("p a b -> p (a b)"),
                             h32[:, i, 0:2, :].rearrange("p a b -> p (a b)")).then_inc(t_hh, 1)

            def spread_copy(s, e):
                wait(act, t_bc, s + 1)
                wait(act, t_yd, s)
                copy(wb[e % 2][:, :], WB).then_inc(t_wb, 1)

            def tile(it, par, more):
                t = it * 2 + par
                for e in range(EXP):
                    s = it * 16 + par * EXP + e
                    if e < EXP - 1 or more:
                        gelus(s + 1, (e + 1) % EXP)
                        spread_copy(s + 1, (e + 1) % EXP)
                    if more and e == 5:
                        input_hi2(t + 1, 1 - par)
                    if more and e == 6:
                        route_copy(t + 1, 1 - par)

            out_hi(B - 1, 0)
            act.wait_ge(t_load, 32)
            act.wait_ge(s_pv, 2 * UNITS * B)
            act.wait_ge(s_xin, B + 1)
            weights_hi(range(0, 2))
            gate_exp(B - 1, 0)
            out_hi(B - 1, 1)
            weights_hi(range(2, 5))
            act.wait_ge(t_sel32, 3)
            copy(sel[:, :, :], sel32[:, :, :]).then_inc(t_sel, 1)
            weights_hi(range(5, EXP))
            gate_exp(B - 1, 1)
            input_hi2(0, 0)
            act.wait_ge(t_cst, 2)
            route_copy(0, 0)
            act.wait_ge(s_mid, 32 * B)
            act.wait_ge(t_colv, 2)
            gelus(0, 0)
            spread_copy(0, 0)
            with act.Fori(0, B - 1) as it:
                tile(it, 0, True)
                tile(it, 1, True)
            tile(B - 1, 0, True)
            tile(B - 1, 1, False)

        @block.vector
        def _(dve):
            tt, ts, stt = nc.vector.tensor_tensor, nc.vector.tensor_scalar, nc.vector.scalar_tensor_tensor

            for i in range(2):
                nc.vector.memset(f(kst[i][MROW:MROW + 1, :]), 1.0).then_inc(s_ones, 1)

            def weights(gs):
                for g in gs:
                    hi, lo, srcs = setup[g]
                    dve.wait_ge(s_wThi, g + 1)
                    tt(lo, conv_bank(g)[:, 0:len(srcs) * P].rearrange("p (a o) -> p a o", o=P), f(hi),
                       ALU.subtract).then_inc(s_wTlo, 1)

            def rsqrt(v, y, t, variance, eps, chain, base, done):
                i32 = mybir.dt.int32
                steps = [lambda: ts(v, variance, eps, None, ALU.add),
                         lambda: ts(y.bitcast(i32), v.bitcast(i32), -0.5, float(0x5f3759df), ALU.mult, ALU.add)]
                for _ in range(3):
                    steps += [lambda: stt(t, y, -0.5, y, ALU.mult, ALU.mult),
                              lambda: tt(t, t, v, ALU.mult),
                              lambda: stt(y, t, 1.5, y, ALU.add, ALU.mult)]
                for i, step in enumerate(steps[:-1]):
                    step().then_inc(chain, 1)
                    dve.wait_ge(chain, base + i + 1)
                steps[-1]().then_inc(done, 1)

            def prepare(n, k):
                half = slice((k - 2) % 3 * NB, ((k - 2) % 3 + 1) * NB)
                if k in (2, 3):
                    wait(dve, s_mean, n * 2 + k - 1)
                    tt(ln_x(n)[:, half], xt[:, half], MX[:, 0:NB], ALU.subtract).then_inc(s_cent, 1)
                if k == 4:
                    wait(dve, s_var, n + 1)
                    rsqrt(rs[:, 0, :], rs[:, 1, :], rs[:, 2, :], MX[:, 0:2 * KC:2], 1e-6, s_rsq, n * 10, s_rstd)
                if k in (5, 6):
                    wait(dve, s_rbc, n * 2 + k - 4)
                    tt(ln_x(n)[:, half], ln_x(n)[:, half], MX[:, 0:NB], ALU.mult).then_inc(s_xn, 1)
                if k == 7:
                    wait(dve, s_xn, n * 3 + 2)
                    tt(ln_x(n), ln_x(n), pos_sb[:, :], ALU.add).then_inc(s_xn, 1)

            def input_lo(n):
                wait(dve, s_xhi, n + 1)
                hi, lo = (t[:, :].rearrange("p (y x) -> p y x", x=PAD)[:, 1:IMG + 1, 1:IMG + 1] for t in (xh, xl))
                tt(lo, ln_x(n).rearrange("p (y x) -> p y x", x=IMG), f(hi), ALU.subtract).then_inc(s_xin, 1)

            swap = [i ^ 1 for i in range(32)]

            def rotate(b, g):
                hf, bank = g % 2, conv_bank(g)
                wait(dve, s_cv, b * 12 + g + 1)
                if g >= 2:
                    wait(dve, s_rlo, b * 8 + g - 1)
                tt(rot_a[g % 2], bank, cos_sb[:, hf * NB:(hf + 1) * NB], ALU.mult)
                nc.vector.stream_shuffle(rot_s[g % 2], bank, swap).then_inc(s_rf, 1)

            def rot_lo(b, g):
                kind, c, hf = g // 4, g % 4 // 2, g % 2
                cols = slice(hf * NB, (hf + 1) * NB)
                wait(dve, s_rhi, b * 8 + g + 1)
                tt(src[:, 2 * kind + 1, c, cols].bitcast(f32r), rot_a[g % 2], src[:, 2 * kind, c, cols],
                   ALU.subtract).then_inc(s_rlo, 1)

            def out_lo(n, hf):
                for c in range(2):
                    wait(dve, s_ohi, n * 4 + 2 * hf + c + 1)
                    tt(ol[:, c, :], PV[c][:, :], f(oh[:, c, :]), ALU.subtract).then_inc(s_olo, 1)

            def gate(n, hf):
                cols = slice(hf * NB, (hf + 1) * NB)
                base = n * 6 + hf * 3
                wait(dve, s_eg, n * 2 + hf + 1)
                ts(eg[:, :], eg[:, :], 1.0, None, ALU.add).then_inc(s_gch, 1)
                wait(dve, s_gch, base + 1)
                nc.vector.reciprocal(eg[:, :], eg[:, :]).then_inc(s_gch, 1)
                wait(dve, s_gch, base + 2)
                stt(eg[:, :], MX[:, 0:NB], bo_sb[:, 0:1], eg[:, :], ALU.add, ALU.mult).then_inc(s_gch, 1)
                wait(dve, s_gch, base + 3)
                wait(dve, s_xg, n * 16 + 16)
                tt(xg[:, cols], xg[:, cols], eg[:, :], ALU.add).then_inc(s_gate, 1)

            def v_lo(b, g):
                c, hf = g // 2, g % 2
                at = (slice(None), slice(4 * hf, 4 * hf + 4), slice(c * P, (c + 1) * P))
                wait(dve, s_vhi, b * 4 + g + 1)
                tt(vl[at], PV[g % 2][:, :].rearrange("p (j o) -> p j o", o=P), f(vh[at]), ALU.subtract).then_inc(s_vlo, 1)

            def take_max(n, k, p):
                wait(dve, s_mx, 2 * n + p + 1)
                nc.vector.tensor_reduce(mcol[:, k % 2, p, MROW:MROW + 1], MX[:, :], AX, ALU.max).then_inc(s_red, 1)

            def exp_lo(n, k, p):
                wait(dve, s_ex, 2 * n + p + 1)
                at = (slice(None), k % 2, slice(4 * p, 4 * p + 4), slice(None))
                tt(El[at].rearrange("p a b -> p (a b)"), E32[:, p, :], f(Eh[at]).rearrange("p a b -> p (a b)"),
                   ALU.subtract).then_inc(s_lo, 1)

            def normalise(n, k, p, head):
                wait(dve, s_pv, 2 * n + p + 1)
                nc.vector.reciprocal(rl[:, p:p + 1], PV[p][:, INNER:INNER + 1]).then_inc(s_rl, 1)
                m = mix_sb[:, bass.ds(head * HEADS, HEADS)].rearrange("p (g a) -> p g a", a=1).to_broadcast([P, HEADS, DH])
                wait(dve, s_rl, 2 * n + p + 1)
                wait(dve, s_acc, 2 * n + p + 1)
                stt(tmp[:, p, :].rearrange("p (g d) -> p g d", d=DH), PV[p][:, 0:INNER].rearrange("p (g d) -> p g d", d=DH),
                    rl[:, p:p + 1], m, ALU.mult, ALU.mult).then_inc(s_nrm, 1)

            def pair(n0, h0, last=False, b=None):
                for k in range(2 * QC):
                    n, head = n0 + k, h0 + k // QC
                    for p in range(2):
                        if not (last and k >= 6):
                            take_max(n + 2, k + 2, p)
                        if last and k == 7:
                            if p == 0:
                                prepare(b + 1, 7)
                            else:
                                input_lo(b + 1)
                        normalise(n, k, p, head)
                        if not (last and k == 7):
                            exp_lo(n + 1, k + 1, p)
                        if last and 2 <= k <= 6 and p == 0:
                            prepare(b + 1, k)

            def batch(b):
                prev = None if isinstance(b, int) else b - 1
                n = b * UNITS
                rotate(b, 0)
                for g in range(1, 4):
                    rotate(b, g)
                    rot_lo(b, g - 1)
                    if g == 1 and prev is not None:
                        out_lo(prev, 0)
                rot_lo(b, 3)
                rotate(b, 4)
                if prev is not None:
                    gate(prev, 0)
                    out_lo(prev, 1)
                rot_lo(b, 4)
                rotate(b, 5)
                rot_lo(b, 5)
                rotate(b, 6)
                if prev is not None:
                    gate(prev, 1)
                rot_lo(b, 6)
                rotate(b, 7)
                rot_lo(b, 7)
                take_max(n, 0, 0)
                v_lo(b, 0)
                take_max(n, 0, 1)
                v_lo(b, 1)
                if prev is not None:
                    wait(dve, s_tr, prev * 4 + 4)
                    nc.vector.memset(acc[:, :, :], 0.0)
                take_max(n + 1, 1, 0)
                exp_lo(n, 0, 0)
                v_lo(b, 2)
                v_lo(b, 3)
                take_max(n + 1, 1, 1)
                exp_lo(n, 0, 1)
                with dve.Fori(0, HEADS // 2 - 1) as hp:
                    pair(n + hp * 8, hp * 2)
                pair(n + UNITS - 8, HEADS - 2, True, b)

            prepare(0, 2)
            prepare(0, 3)
            prepare(0, 4)
            weights(range(0, 2))
            prepare(0, 5)
            prepare(0, 6)
            dve.wait_ge(s_tload, 16 * 5)
            prepare(0, 7)
            weights(range(2, 6))
            input_lo(0)
            weights(range(6, len(setup)))
            dve.wait_ge(s_mixp, 1)
            nc.vector.tensor_copy(mix_sb[:, :], PV[0][:, 0:HEADS * HEADS]).then_inc(s_mix, 1)
            ts(nbo[:, :], bo_sb[:, 1:2], -1.0, None, ALU.mult).then_inc(s_mix, 1)
            dve.wait_ge(s_xin, 1)
            nc.vector.memset(acc[:, :, :], 0.0).then_inc(s_nrm, 2)
            dve.wait_ge(t_col, 1)
            nc.vector.tensor_copy(vec_col[:, :, :].rearrange("p a e -> p (a e)"), PV[1][:, 0:3 * EXP])
            nc.vector.tensor_copy(br_sb[:, :], PV[1][:, 64:64 + EXP])
            nc.vector.tensor_copy(rank_sb[:, :], PV[1][:, 80:80 + EXP])
            nc.vector.tensor_copy(b1_col[:, :], PV[1][:, 32:64]).then_inc(t_colv, 1)
            batch(0)
            with dve.Fori(1, B) as b:
                batch(b)

            def weights_lo(experts):
                for e in experts:
                    dve.wait_ge(t_whi, 2 * e + 2)
                    stt(w1l[:, e, :], w1raw[:, e, :], vec_col[:, 0, e:e + 1], f(w1h[:, e, :]),
                        ALU.mult, ALU.subtract).then_inc(t_wlo, 1)
                    tt(w2l[:, e, :, :].rearrange("p k d -> p (k d)"), w2raw[:, e, :, :].rearrange("p k d -> p (k d)"),
                       f(w2h[:, e, :, :]).rearrange("p k d -> p (k d)"), ALU.subtract).then_inc(t_wlo, 1)

            def centre(t, par):
                wait(dve, t_mean, t + 1)
                tt(fc[:, :], xm[par][:, :], prep_banks(t)[0], ALU.subtract).then_inc(t_cent, 1)

            def token_stats(t, part):
                PR, LG = prep_banks(t)
                q = PR[:, 0:2 * R4:2]
                veps, r1, step, m, v, r2, factor, shift = (frs[:, i, :] for i in range(8))
                base = t * NLINK_S

                def link(i, instruction):
                    instruction.then_inc(t_link, 1)
                    dve.wait_ge(t_link, base + i)

                if part == 0:
                    wait(dve, t_stat, t + 1)
                    link(1, nc.vector.tensor_copy(m, LG[:, EXP:R4 * LGW:LGW]))
                    link(2, tt(v, m, m, ALU.mult))
                    link(3, tt(v, q, v, ALU.subtract))
                    rsqrt(veps, r1, step, q, 1e-5, t_link, base + 3, t_link)
                    dve.wait_ge(t_link, base + 14)
                else:
                    link(15, tt(v, v, r1, ALU.mult))
                    link(16, tt(v, v, r1, ALU.mult))
                    rsqrt(veps, r2, step, v, 1e-5, t_link, base + 16, t_link)
                    dve.wait_ge(t_link, base + 27)
                    link(28, tt(factor, r1, r2, ALU.mult))
                    stt(shift, m, -1.0, factor, ALU.mult, ALU.mult).then_inc(t_norm, 1)

            def norm(t):
                PR, shifts = prep_banks(t)
                wait(dve, t_fact, t + 1)
                tt(fc[:, :], fc[:, :], PR, ALU.mult).then_inc(t_mul, 1)
                wait(dve, t_mul, t + 1)
                tt(fc[:, :], fc[:, :], shifts, ALU.add).then_inc(t_xn, 1)

            def split2(t, par):
                wait(dve, t_xnh, t + 1)
                tt(xnl[par][:, :], fc[:, :], f(xnh[par][:, :]), ALU.subtract).then_inc(t_xnl, 1)

            def over(v):
                return v.rearrange("p (a o) -> p a o", o=1).to_broadcast([P, R4, EXP])

            rank_b = rank_sb[:, :].rearrange("p (o e) -> p o e", o=1).to_broadcast([P, R4, EXP])
            br_b = br_sb[:, :].rearrange("p (o e) -> p o e", o=1).to_broadcast([P, R4, EXP])
            all3 = (slice(None),) * 3

            class Links:
                def __init__(self, t):
                    self.t, self.n = t, 0

                def __call__(self, instruction):
                    self.n += 1
                    instruction.then_inc(t_rc, 1)
                    dve.wait_ge(t_rc, self.t * NLINK_R + self.n)

            def top2(t):
                link = Links(t)
                LG = prep_banks(t)[1]
                logits = LG[:, 0:R4 * LGW].rearrange("p (a e) -> p a e", e=LGW)[:, :, 0:EXP]
                link(tt(lg[all3], logits, over(frs[:, 1, :]), ALU.mult))
                link(tt(lg[all3], lg[all3], br_b, ALU.add))
                link(nc.vector.tensor_reduce(r_m[:, 0, :], lg[all3], AX, ALU.max))
                tt(r_d[all3], lg[all3], over(r_m[:, 0, :]), ALU.subtract).then_inc(t_d, 1)
                link(tt(r_c[all3], lg[all3], over(r_m[:, 0, :]), ALU.is_equal))
                link(tt(r_c[all3], r_c[all3], rank_b, ALU.mult))
                link(nc.vector.tensor_reduce(r_m[:, 1, :], r_c[all3], AX, ALU.max))
                link(tt(r_o1[all3], r_c[all3], over(r_m[:, 1, :]), ALU.is_equal))
                link(stt(r_l2[all3], r_o1[all3], -3.0e38, lg[all3], ALU.mult, ALU.add))
                link(nc.vector.tensor_reduce(r_m[:, 2, :], r_l2[all3], AX, ALU.max))
                link(tt(r_c[all3], r_l2[all3], over(r_m[:, 2, :]), ALU.is_equal))
                link(tt(r_c[all3], r_c[all3], rank_b, ALU.mult))
                link(nc.vector.tensor_reduce(r_m[:, 3, :], r_c[all3], AX, ALU.max))
                link(tt(r_o2[all3], r_c[all3], over(r_m[:, 3, :]), ALU.is_equal))
                assert link.n == NLINK_R

            t_wc = sem("t_wc")

            def weigh(t):
                tt(r_o1[all3], r_o1[all3], r_o2[all3], ALU.add).then_inc(t_wc, 1)
                wait(dve, t_ex, t + 1)
                dve.wait_ge(t_wc, t * 4 + 1)
                tt(r_e[all3], r_e[all3], r_o1[all3], ALU.mult).then_inc(t_wc, 1)
                dve.wait_ge(t_wc, t * 4 + 2)
                nc.vector.tensor_reduce(r_m[:, 4, :], r_e[all3], AX, ALU.add).then_inc(t_wc, 1)
                dve.wait_ge(t_wc, t * 4 + 3)
                nc.vector.reciprocal(r_m[:, 5, :], r_m[:, 4, :]).then_inc(t_wc, 1)
                dve.wait_ge(t_wc, t * 4 + 4)
                tt(r_w[all3], r_e[all3], over(r_m[:, 5, :]), ALU.mult).then_inc(t_w, 1)

            def route_lo(t, par):
                wait(dve, t_whh, t + 1)
                PR = prep_banks(t)[0]
                tt(wst[par][LO:LO + EXP, :], PR[0:EXP, :], f(wst[par][0:EXP, :]), ALU.subtract).then_inc(t_whl, 1)

            def gelu_lo(s, e):
                i = e % 2
                pairs = [(t[:, i, 2 * j:2 * j + 2, :].rearrange("p a b -> p (a b)")) for j in range(2) for t in (hl, h32, hh)]
                wait(dve, t_hh, s + 1)
                tt(pairs[0], pairs[1], f(pairs[2]), ALU.subtract).then_inc(t_hl, 1)
                wait(dve, t_gl, 4 * s + 4)
                nc.vector.tensor_copy(pairs[5], pairs[4]).then_inc(t_hh1, 1)
                wait(dve, t_hh1, s + 1)
                tt(pairs[3], pairs[4], f(pairs[5]), ALU.subtract).then_inc(t_hl, 1)

            def weight_out(s, e):
                wait(dve, t_y, s + 1)
                wait(dve, t_wb, s + 1)
                wait(dve, t_ya, s + 1)
                stt(ty[e % 2][:, :], Y, vec_col[:, 2, e:e + 1], wb[e % 2][:, :], ALU.add, ALU.mult).then_inc(t_yd, 1)

            def tile(it, par, more):
                t = it * 2 + par
                for e in range(EXP):
                    s = it * 16 + par * EXP + e
                    if more and e == 6:
                        split2(t + 1, 1 - par)
                    if e < EXP - 1 or more:
                        gelu_lo(s + 1, (e + 1) % EXP)
                    if more:
                        if e == 0:
                            centre(t + 1, 1 - par)
                        if e == 5:
                            norm(t + 1)
                            weigh(t + 1)
                        if e == 6:
                            route_lo(t + 1, 1 - par)
                    weight_out(s, e)
                    if more:
                        if e == 1:
                            token_stats(t + 1, 0)
                        if e == 2:
                            token_stats(t + 1, 1)
                        if e == 3:
                            top2(t + 1)

            out_lo(B - 1, 0)
            centre(0, 0)
            weights_lo(range(0, 2))
            gate(B - 1, 0)
            out_lo(B - 1, 1)
            token_stats(0, 0)
            top2(0)
            token_stats(0, 1)
            gate(B - 1, 1)
            norm(0)
            weigh(0)
            dve.wait_ge(t_lnb, 3)
            tt(b1_col[:, :], ST[1][:, 0:EXP * HK], b1_col[:, :], ALU.add).then_inc(t_colv, 1)
            split2(0, 0)
            dve.wait_ge(t_cst, 2)
            route_lo(0, 0)
            weights_lo(range(2, EXP))
            dve.wait_ge(s_mid, 32 * B)
            nc.vector.memset(ty[1][:, 0:1], 0.0).then_inc(t_yd, 1)
            gelu_lo(0, 0)
            with dve.Fori(0, B - 1) as it:
                tile(it, 0, True)
                tile(it, 1, True)
            tile(B - 1, 0, True)
            tile(B - 1, 1, False)


_INS = ["x", "L0_conv_wq", "L0_conv_wk", "L0_conv_wv", "L0_conv_mix", "L0_conv_wo", "L0_conv_bo",
        "L0_ffn_Wr", "L0_ffn_br", "L0_ffn_ln_g", "L0_ffn_ln_b", "L0_ffn_W1", "L0_ffn_b1", "L0_ffn_W2", "L0_ffn_b2"]


def position_tables():
    one = np.float32
    half = C // 2
    inv = (1.0 / np.power(one(10000.0), np.arange(0, half, 2, dtype=one) / one(half))).astype(one)
    seq = np.linspace(-1.0, 1.0, IMG, dtype=one)
    sinu = seq[None, :] * inv[:, None]
    part_w = np.broadcast_to(sinu[:, None, :], (C // 4, IMG, IMG))
    part_h = np.broadcast_to(sinu[:, :, None], (C // 4, IMG, IMG))
    s = np.concatenate([part_w, part_h], axis=0)
    pos2 = one(2.0) * np.concatenate([np.sin(s), np.cos(s)], axis=0).reshape(C, TOK)
    scales = np.logspace(0.0, np.log(5.0) / np.log(2.0), DH // 4, base=2.0).astype(one)
    fr = (seq[:, None] * scales[None, :] * one(np.pi)).astype(one)
    xs = np.broadcast_to(fr[:, None, :], (IMG, IMG, DH // 4))
    ys = np.broadcast_to(fr[None, :, :], (IMG, IMG, DH // 4))
    ang = np.concatenate([xs, ys], axis=-1).reshape(TOK, DH // 2)
    cos = np.repeat(np.cos(ang), 2, axis=-1).T
    sin = np.repeat(np.sin(ang), 2, axis=-1).T
    sign = np.where(np.arange(DH) % 2 == 0, -1.0, 1.0).astype(one)[:, None]
    rank = (EXP - np.arange(EXP)).astype(one)[None, :]
    return [np.ascontiguousarray(t, dtype=one) for t in (
        pos2, np.tile(cos, (P // DH, 1)), np.tile(sin * sign, (P // DH, 1)), rank)]


def kernel(**inputs):
    import concourse.bacc as _bacc
    from concourse import mybir as _mybir
    from concourse.bass_utils import run_bass_kernel_spmd as _run

    nc = _bacc.Bacc("TRN2", target_bir_lowering=False, num_devices=1)
    arrays, args = {}, []

    def give(name, a):
        arrays[name] = a
        args.append(nc.dram_tensor(name, a.shape, _mybir.dt.from_np(a.dtype), kind="ExternalInput").ap())

    for name in _INS:
        give(f"in_{name}_dram", np.ascontiguousarray(inputs[name]))
    for name, t in zip(("pos2", "rot_cos", "rot_sin", "rank"), position_tables()):
        give(f"table_{name}_dram", t)
    args.append(nc.dram_tensor("out_0_dram", (B, C, IMG, IMG), _mybir.dt.float32, kind="ExternalOutput").ap())
    build(nc, *args)
    r = _run(nc, [arrays], core_ids=[0])
    return r.results[0]["out_0_dram"]
```
